# Optimizing a Trainium2 kernel written in Bass

```python
import numpy as np
import jax
import jax.numpy as jnp

def _softmax(x, axis=-1):
    return jax.nn.softmax(x, axis=axis)

def _gelu(x):
    return jax.nn.gelu(x, approximate=True)

def _silu(x):
    return jax.nn.silu(x)

def _sigmoid(x):
    return jax.nn.sigmoid(x)

def _layernorm(x, axis=-1, eps=1e-05):
    m = jnp.mean(x, axis=axis, keepdims=True)
    v = jnp.var(x, axis=axis, keepdims=True)
    return (x - m) / jnp.sqrt(v + eps)

def _scatter_add(tgt, idx, src, axis=0):
    return tgt.at[idx].add(src)

def _segment_sum(src, seg, n):
    return jax.ops.segment_sum(src, seg, n)
kernel_name = 'mk_xattn_ffn_d2_seqx_r4_afe230'

def setup_inputs(seed: int=0):
    np.random.seed(seed)
    _w = jnp.asarray

    def _rec_inputs():
        import jax
        import jax.numpy as jnp
        _rk = jax.random.key(seed)
        x = 7.22e-05 + 1 * jax.random.normal(jax.random.fold_in(_rk, 1), (4, 1024, 256), jnp.float32)
        _lenS = 1024 - jax.random.randint(jax.random.fold_in(_rk, 7), (4,), 0, max(1, 1024 // 4) + 1, jnp.int32)
        _lenS2 = 77 - jax.random.randint(jax.random.fold_in(_rk, 8), (4,), 0, max(1, 77 // 4) + 1, jnp.int32)
        _ctx_768P = jax.random.normal(jax.random.fold_in(_rk, 11), (4, 16, 192), jnp.float32)
        _ctx_768c = jax.random.dirichlet(jax.random.fold_in(_rk, 511), 0.3 * jnp.ones((16,), jnp.float32), (4, 77))
        _ctx_768t = jnp.einsum('bsk,bkd->bsd', _ctx_768c, _ctx_768P)
        _ctx_768t = _ctx_768t * jax.lax.rsqrt(jnp.mean(jnp.square(_ctx_768t)) + 1e-12) * 0.953939
        ctx_768 = -0.000191848 + 0.999787 * (_ctx_768t + 0.3 * jax.random.normal(jax.random.fold_in(_rk, 611), (4, 77, 192), jnp.float32))
        _validS = jnp.arange(1024)[None, :] < _lenS[:, None]
        _validS2 = jnp.arange(77)[None, :] < _lenS2[:, None]
        _causal = jnp.tril(jnp.ones((1024, 1024), dtype=bool))
        mask_BxS2_bf1 = jnp.ones((4, 77), dtype=bool)
        return (x, ctx_768, mask_BxS2_bf1)
    x, ctx_768, mask_BxS2_bf1 = _rec_inputs()

    def _L0_xattn_setup():
        import jax, jax.numpy as jnp
        import numpy as np
        NUM_HEADS = 16
        CLAMP = 10000.0
        key = jax.random.key(seed)
        ks = jax.random.split(key, 8)
        B, Nq, Nkv, Cq, Ckv = (4, 512, 512, 256, 192)
        s_q = 1.0 / np.sqrt(Cq)
        s_kv = 1.0 / np.sqrt(Ckv)
        return {'query': jax.random.normal(ks[0], (B, Nq, Cq), jnp.float32), 'key_value': jax.random.normal(ks[1], (B, Nkv, Ckv), jnp.float32), 'Wq': jax.random.normal(ks[2], (Cq, Cq), jnp.float32) * s_q, 'bq': jnp.zeros((Cq,), jnp.float32), 'Wk': jax.random.normal(ks[3], (Ckv, Cq), jnp.float32) * s_kv, 'bk': jnp.zeros((Cq,), jnp.float32), 'Wv': jax.random.normal(ks[4], (Ckv, Cq), jnp.float32) * s_kv, 'bv': jnp.zeros((Cq,), jnp.float32), 'Wo': jax.random.normal(ks[5], (Cq, Cq), jnp.float32) * s_q, 'bo': jnp.zeros((Cq,), jnp.float32)}
    _L0_xattn_all = _L0_xattn_setup()
    _L0_xattn_in = {k: v for k, v in _L0_xattn_all.items() if k in ('Wq', 'bq', 'Wk', 'bk', 'Wv', 'bv', 'Wo', 'bo')}
    del _L0_xattn_all

    def _L0_ffn_setup():
        import jax, jax.numpy as jnp
        import numpy as np
        BLOCK = 32
        W_BITS = 4
        ACT_BITS = 16

        def act_qdq(x):
            qmax = 2.0 ** (ACT_BITS - 1) - 1.0
            scale = jnp.maximum(jnp.max(jnp.abs(x)) / qmax, 1e-12)
            return jnp.clip(jnp.round(x / scale), -qmax - 1.0, qmax) * scale

        def fixed_qdq_u16(x):
            scale = 1.0 / 65536.0
            return jnp.clip(jnp.round(x / scale), 0.0, 65535.0) * scale

        def lpbq_dequant(w):
            O, I = w.shape
            qmax = 2.0 ** (W_BITS - 1) - 1.0
            wb = w.reshape(O, I // BLOCK, BLOCK)
            s = jnp.maximum(jnp.max(jnp.abs(wb), axis=-1, keepdims=True) / qmax, 1e-12)
            wq = jnp.clip(jnp.round(wb / s), -qmax - 1.0, qmax) * s
            return wq.reshape(O, I)
        key = jax.random.key(seed)
        k1, k2, k3, k4 = jax.random.split(key, 4)
        B, S, H, I = (2, 1024, 256, 768)
        x = jax.random.normal(k1, (B, S, H), jnp.float32)
        w_gate = jax.random.normal(k2, (I, H), jnp.float32) * 0.02
        w_up = jax.random.normal(k3, (I, H), jnp.float32) * 0.02
        w_down = jax.random.normal(k4, (H, I), jnp.float32) * 0.02
        return {'x': x, 'w_gate': w_gate, 'w_up': w_up, 'w_down': w_down}
    _L0_ffn_all = _L0_ffn_setup()
    _L0_ffn_in = {k: v for k, v in _L0_ffn_all.items() if k in ('w_gate', 'w_up', 'w_down')}
    del _L0_ffn_all

    def _L1_xattn_setup():
        import jax, jax.numpy as jnp
        import numpy as np
        import math
        B, N, M = (4, 256, 256)
        DIM, CTX_DIM = (256, 192)
        HEADS, DIM_HEAD = (16, 64)
        INNER = HEADS * DIM_HEAD

        def layer_norm(t, g, eps=1e-05):
            mean = jnp.mean(t, axis=-1, keepdims=True)
            var = jnp.mean((t - mean) ** 2, axis=-1, keepdims=True)
            return (t - mean) * jax.lax.rsqrt(var + eps) * g
        key = jax.random.key(seed)
        ks = jax.random.split(key, 8)
        return {'x': jax.random.normal(ks[0], (B, N, DIM), jnp.float32), 'context': jax.random.normal(ks[1], (B, M, CTX_DIM), jnp.float32), 'mask': jnp.ones((B, M), dtype=bool), 'g_norm': jnp.ones((DIM,), jnp.float32), 'null_kv': jax.random.normal(ks[2], (2, DIM_HEAD), jnp.float32), 'Wq': jax.random.normal(ks[3], (DIM, INNER), jnp.float32) * DIM ** (-0.5), 'Wkv': jax.random.normal(ks[4], (CTX_DIM, 2 * INNER), jnp.float32) * CTX_DIM ** (-0.5), 'Wout': jax.random.normal(ks[5], (INNER, DIM), jnp.float32) * INNER ** (-0.5), 'g_out': jnp.ones((DIM,), jnp.float32)}
    _L1_xattn_all = _L1_xattn_setup()
    _L1_xattn_in = {k: v for k, v in _L1_xattn_all.items() if k in ('g_norm', 'null_kv', 'Wq', 'Wkv', 'Wout', 'g_out')}
    del _L1_xattn_all

    def _L1_ffn_setup():
        import jax, jax.numpy as jnp
        import numpy as np
        K = 2
        TEMP = 1.0
        key = jax.random.key(seed)
        ks = jax.random.split(key, 5)
        B, S, D, O, E = (4, 512, 256, 256, 8)
        scale = 1.0 / np.sqrt(D)
        x = jax.random.normal(ks[0], (B, S, D), dtype=jnp.float32)
        W = jax.random.normal(ks[1], (E, O, D), dtype=jnp.float32) * scale
        b = jax.random.normal(ks[2], (E, O), dtype=jnp.float32) * 0.01
        Wg = jax.random.normal(ks[3], (E, D), dtype=jnp.float32) * scale
        bg = jnp.zeros((E,), dtype=jnp.float32)
        return {'x': x, 'W': W, 'b': b, 'Wg': Wg, 'bg': bg}
    _L1_ffn_all = _L1_ffn_setup()
    _L1_ffn_in = {k: v for k, v in _L1_ffn_all.items() if k in ('W', 'b', 'Wg', 'bg')}
    del _L1_ffn_all
    return {'x': x, 'ctx_768': ctx_768, 'mask_BxS2_bf1': mask_BxS2_bf1, 'L0_xattn_Wq': _L0_xattn_in['Wq'], 'L0_xattn_bq': _L0_xattn_in['bq'], 'L0_xattn_Wk': _L0_xattn_in['Wk'], 'L0_xattn_bk': _L0_xattn_in['bk'], 'L0_xattn_Wv': _L0_xattn_in['Wv'], 'L0_xattn_bv': _L0_xattn_in['bv'], 'L0_xattn_Wo': _L0_xattn_in['Wo'], 'L0_xattn_bo': _L0_xattn_in['bo'], 'L0_ffn_w_gate': _L0_ffn_in['w_gate'], 'L0_ffn_w_up': _L0_ffn_in['w_up'], 'L0_ffn_w_down': _L0_ffn_in['w_down'], 'L1_xattn_g_norm': _L1_xattn_in['g_norm'], 'L1_xattn_null_kv': _L1_xattn_in['null_kv'], 'L1_xattn_Wq': _L1_xattn_in['Wq'], 'L1_xattn_Wkv': _L1_xattn_in['Wkv'], 'L1_xattn_Wout': _L1_xattn_in['Wout'], 'L1_xattn_g_out': _L1_xattn_in['g_out'], 'L1_ffn_W': _L1_ffn_in['W'], 'L1_ffn_b': _L1_ffn_in['b'], 'L1_ffn_Wg': _L1_ffn_in['Wg'], 'L1_ffn_bg': _L1_ffn_in['bg']}

def reference(x, ctx_768, mask_BxS2_bf1, L0_xattn_Wq, L0_xattn_bq, L0_xattn_Wk, L0_xattn_bk, L0_xattn_Wv, L0_xattn_bv, L0_xattn_Wo, L0_xattn_bo, L0_ffn_w_gate, L0_ffn_w_up, L0_ffn_w_down, L1_xattn_g_norm, L1_xattn_null_kv, L1_xattn_Wq, L1_xattn_Wkv, L1_xattn_Wout, L1_xattn_g_out, L1_ffn_W, L1_ffn_b, L1_ffn_Wg, L1_ffn_bg):
    import jax
    import jax.numpy as jnp

    def _L0_xattn_ref(query, key_value, Wq, bq, Wk, bk, Wv, bv, Wo, bo):
        import jax, jax.numpy as jnp
        import numpy as np
        NUM_HEADS = 16
        CLAMP = 10000.0
        B, Nq, Cq = query.shape
        Nkv = key_value.shape[1]
        H = NUM_HEADS
        D = Cq // H
        scale = D ** (-0.5)
        q = (query @ Wq + bq).reshape(B, Nq, H, D).transpose(0, 2, 1, 3)
        k = (key_value @ Wk + bk).reshape(B, Nkv, H, D).transpose(0, 2, 1, 3)
        v = (key_value @ Wv + bv).reshape(B, Nkv, H, D).transpose(0, 2, 1, 3)
        attn = jnp.einsum('bhqd,bhkd->bhqk', q, k) * scale
        attn = jnp.clip(attn, -CLAMP, CLAMP)
        attn = jax.nn.softmax(attn, axis=-1)
        attn = jnp.where(jnp.any(jnp.isnan(attn)), jnp.asarray(1.0 / Nkv, attn.dtype), attn)
        x = jnp.einsum('bhqk,bhkd->bqhd', attn, v).reshape(B, Nq, Cq)
        return x @ Wo + bo

    def _L0_ffn_ref(x, w_gate, w_up, w_down):
        import jax, jax.numpy as jnp
        import numpy as np
        BLOCK = 32
        W_BITS = 4
        ACT_BITS = 16

        def act_qdq(x):
            qmax = 2.0 ** (ACT_BITS - 1) - 1.0
            scale = jnp.maximum(jnp.max(jnp.abs(x)) / qmax, 1e-12)
            return jnp.clip(jnp.round(x / scale), -qmax - 1.0, qmax) * scale

        def fixed_qdq_u16(x):
            scale = 1.0 / 65536.0
            return jnp.clip(jnp.round(x / scale), 0.0, 65535.0) * scale

        def lpbq_dequant(w):
            O, I = w.shape
            qmax = 2.0 ** (W_BITS - 1) - 1.0
            wb = w.reshape(O, I // BLOCK, BLOCK)
            s = jnp.maximum(jnp.max(jnp.abs(wb), axis=-1, keepdims=True) / qmax, 1e-12)
            wq = jnp.clip(jnp.round(wb / s), -qmax - 1.0, qmax) * s
            return wq.reshape(O, I)
        x = act_qdq(x)
        up = act_qdq(x @ lpbq_dequant(w_up).T)
        gate = act_qdq(x @ lpbq_dequant(w_gate).T)
        sig = fixed_qdq_u16(jax.nn.sigmoid(gate))
        gate = act_qdq(gate * sig)
        o = act_qdq(gate * up)
        return o @ lpbq_dequant(w_down).T

    def _L1_xattn_ref(x, context, mask, g_norm, null_kv, Wq, Wkv, Wout, g_out):
        import jax, jax.numpy as jnp
        import numpy as np
        import math
        B, N, M = (4, 256, 256)
        DIM, CTX_DIM = (256, 192)
        HEADS, DIM_HEAD = (16, 64)
        INNER = HEADS * DIM_HEAD

        def layer_norm(t, g, eps=1e-05):
            mean = jnp.mean(t, axis=-1, keepdims=True)
            var = jnp.mean((t - mean) ** 2, axis=-1, keepdims=True)
            return (t - mean) * jax.lax.rsqrt(var + eps) * g
        b = x.shape[0]
        scale = DIM_HEAD ** (-0.5)
        sqrt_scale = math.sqrt(scale)
        x = layer_norm(x, g_norm)
        q = x @ Wq
        kv = context @ Wkv
        k, v = jnp.split(kv, 2, axis=-1)

        def to_heads(t):
            return t.reshape(b, t.shape[1], HEADS, DIM_HEAD).transpose(0, 2, 1, 3)
        q, k, v = (to_heads(q), to_heads(k), to_heads(v))
        nk = jnp.broadcast_to(null_kv[0], (b, HEADS, 1, DIM_HEAD))
        nv = jnp.broadcast_to(null_kv[1], (b, HEADS, 1, DIM_HEAD))
        k = jnp.concatenate([nk, k], axis=2)
        v = jnp.concatenate([nv, v], axis=2)
        q = q * sqrt_scale
        k = k * sqrt_scale
        sim = jnp.einsum('bhid,bhjd->bhij', q, k)
        max_neg = -jnp.finfo(sim.dtype).max
        full_mask = jnp.pad(mask, ((0, 0), (1, 0)), constant_values=True)
        sim = jnp.where(full_mask[:, None, None, :], sim, max_neg)
        attn = jax.nn.softmax(sim.astype(jnp.float32), axis=-1).astype(sim.dtype)
        out = jnp.einsum('bhij,bhjd->bhid', attn, v)
        out = out.transpose(0, 2, 1, 3).reshape(b, -1, INNER)
        out = out @ Wout
        return layer_norm(out, g_out)

    def _L1_ffn_ref(x, W, b, Wg, bg):
        import jax, jax.numpy as jnp
        import numpy as np
        K = 2
        TEMP = 1.0
        gate_logits = (jnp.einsum('bsd,ed->bse', x, Wg) + bg) / TEMP
        gate_scores = jax.nn.softmax(gate_logits, axis=-1)
        topk_scores, topk_idx = jax.lax.top_k(gate_scores, K)
        expert_outputs = jnp.einsum('bsd,eod->bseo', x, W) + b
        selected = jnp.take_along_axis(expert_outputs, topk_idx[..., None], axis=2)
        output = jnp.sum(selected * topk_scores[..., None], axis=2)
        return output
    x = x + _L0_xattn_ref(_layernorm(x, axis=-1), ctx_768, L0_xattn_Wq, L0_xattn_bq, L0_xattn_Wk, L0_xattn_bk, L0_xattn_Wv, L0_xattn_bv, L0_xattn_Wo, L0_xattn_bo)
    x = x + _L0_ffn_ref(_layernorm(x, axis=-1), L0_ffn_w_gate, L0_ffn_w_up, L0_ffn_w_down)
    x = x + _L1_xattn_ref(_layernorm(x, axis=-1), ctx_768, mask_BxS2_bf1, L1_xattn_g_norm, L1_xattn_null_kv, L1_xattn_Wq, L1_xattn_Wkv, L1_xattn_Wout, L1_xattn_g_out)
    x = x + _L1_ffn_ref(_layernorm(x, axis=-1), L1_ffn_W, L1_ffn_b, L1_ffn_Wg, L1_ffn_bg)
    return x

_drawn_inputs = setup_inputs


def setup_inputs(seed=0):
    import zlib

    import numpy as np

    out = dict(_drawn_inputs(seed))
    spreads = {'L0_xattn_bq': (0.0, 0.1),
     'L0_xattn_bk': (0.0, 2.0),
     'L0_xattn_bv': (0.0, 0.1),
     'L0_xattn_bo': (0.0, 0.1),
     'L1_xattn_g_norm': (1.0, 0.2),
     'L1_xattn_g_out': (1.0, 0.2),
     'L1_ffn_bg': (0.0, 0.1)}
    factors = {'L1_ffn_b': 21.512}
    for name, (base, spread) in spreads.items():
        noise = np.random.default_rng([zlib.crc32(name.encode()), seed]).standard_normal(out[name].shape)
        drawn = base * np.exp(spread * noise) if base else spread * noise
        out[name] = jnp.asarray(drawn.astype(out[name].dtype))
    for name, factor in factors.items():
        out[name] = (out[name] * factor).astype(out[name].dtype)
    return out
```

```python
from contextlib import ExitStack

import concourse.bass as bass
from concourse import mybir
from concourse.alu_op_type import AluOpType as ALU

F32 = mybir.dt.float32
F32R = mybir.dt.float32r
I16 = mybir.dt.int16
U16 = mybir.dt.uint16
U8 = mybir.dt.uint8
ACT = mybir.ActivationFunctionType
AX = mybir.AxisListType
RMAX = bass.bass_isa.ReduceOp.max

P = 128
B, SEQ, D = 4, 1024, 256
NKEY, CD = 77, 192
H = 16
NT = B * SEQ // P
TPB = SEQ // P
KT = D // P
CK = CD // 96
CP = CD // CK
KP = 80
QW = 4 * KP
SW = H * KP
NJ = SW // P
HJ = NJ // 2
D0 = D // H
D1 = 64
CLAMP = 10000.0
EPS = 1e-5
FI = 768
NE = 8


def tile_heads(j):
    a = P * (j % HJ)
    return a // KP, (a + P - 1) // KP - a // KP + 1


def first_slot(j):
    return sum(tile_heads(k)[1] for k in range(j))


NSLOT = first_slot(NJ)


class At:

    def __init__(self, t0, i=None):
        self.t0, self.i = t0, i

    def __add__(self, k):
        return At(self.t0 + k, self.i)

    def of(self, f):
        if self.i is None:
            return f(self.t0)
        return self.i * (f(self.t0 + 2) - f(self.t0)) + f(self.t0)

    @property
    def n(self):
        return self.t0 if self.i is None else self.i * 2 + self.t0

    @property
    def batch(self):
        return self.n // TPB

    @property
    def p(self):
        return self.t0 % 2

    def ok(self):
        return 0 <= self.t0 < NT


def pipeline(eng, body, first, last, lo, hi):
    for t in range(first, lo):
        body(At(t))
    with eng.Fori(0, (hi - lo + 1) // 2) as i:
        body(At(lo, i))
        body(At(lo + 1, i))
    for t in range(hi + 1, last + 1):
        body(At(t))


class Slots:

    def __init__(self, order):
        self.order = order
        self.at = {x: n for n, x in enumerate(order)}

    def bank(self, kind, t, k=0):
        return self.at[kind, t.t0, k] % 2

    def before(self, kind, t, k=0):
        n = self.at[kind, t.t0, k]
        if n < 2:
            return None
        kd, tt, kk = self.order[n - 2]
        return kd, t + (tt - t.t0), kk


def program(nc, x, ctx_kv, mask, w, out):
    stack = ExitStack()
    with stack:
        _program(nc, stack, x, ctx_kv, mask, w, out)


class Sems:

    def __init__(self, nc):
        self.nc, self.stack, self.nums = nc, ExitStack(), []

    def __call__(self, name):
        handle = self.stack.enter_context(self.nc.semaphore(name))
        self.nums.append(handle.num)
        return handle

    def clear(self, eng):
        nums = sorted(self.nums)
        while nums:
            n = 1
            while n < len(nums) and nums[n] == nums[0] + n:
                n += 1
            eng.sem_clear(range(nums[0], nums[0] + n))
            nums = nums[n:]


def _program(nc, stack, x, ctx_kv, mask, w, out):
    sem = Sems(nc)

    def sbuf(st, name, shape, dt=F32):
        return st.enter_context(nc.sbuf_tensor(name, shape, dt))

    xs = sbuf(stack, "xs", [P, NT * D])
    ident = sbuf(stack, "ident", [P, P])
    mhalf = sbuf(stack, "mhalf", [P, 1])
    hstat = sbuf(stack, "hstat", [P, NT * 2])
    hrstd = sbuf(stack, "hrstd", [P, NT])
    hamax = sbuf(stack, "hamax", [P, NT])
    psel = sbuf(stack, "psel", [P, 2, HJ, 3])
    ctxT = sbuf(stack, "ctxT", [CP, CK, B, KP])

    def xt(t):
        return xs[:, bass.ds(t.n * D, D)] if t.i is not None else xs[:, t.t0 * D:(t.t0 + 1) * D]

    def col(a, t, n=1):
        return a[:, bass.ds(t.n * n, n)] if t.i is not None else a[:, t.t0 * n:t.t0 * n + n]

    att0 = ExitStack()
    wq0 = sbuf(att0, "wq0", [P, KT, D])
    wo0 = sbuf(att0, "wo0", [P, KT, D])
    bq0 = sbuf(att0, "bq0", [P, KT])
    bo0 = sbuf(att0, "bo0", [P, D])
    keys0 = sbuf(att0, "keys0", [P, B, KT, 8, KP])
    vals0 = sbuf(att0, "vals0", [P, B, NJ, 3, D0 + 1])

    s_x = [sem(f"s_x{b}") for b in range(B)]
    s_small = sem("s_small")
    s_ctx = sem("s_ctx")
    s_id = sem("s_id")
    s_tbl = sem("s_tbl")
    s_cT = sem("s_cT")
    s_cTe = sem("s_cTe")
    s_k0 = sem("s_k0")
    s_k0e = sem("s_k0e")
    s_v0 = sem("s_v0")
    s_v0e = sem("s_v0e")

    with ExitStack() as st:
        ctx = sbuf(st, "ctx", [NKEY, B, CD])
        ctx3 = sbuf(st, "ctx3", [CP, CK, B, 3, KP])
        wk0 = sbuf(st, "wk0", [CP, CK, D])
        wv0 = sbuf(st, "wv0", [CP, CK, D])
        bk0 = sbuf(st, "bk0", [P, KT])
        bv0 = sbuf(st, "bv0", [P, D])
        hsel = sbuf(st, "hsel", [P, 8])
        kT = sbuf(st, "kT", [P, KT, B, KP])
        pb = [st.enter_context(nc.psum_tensor(f"prep{i}", [P, 512], F32)) for i in range(4)]

        with nc.Block() as block:
            @block.sync
            def _(sp):
                sp.dma_start(ctx[:], ctx_kv.rearrange("b k c -> k b c")).then_inc(s_ctx, 16)
                sp.dma_start(wk0[:], w["Wk"].rearrange("(k p) n -> p k n", p=CP)).then_inc(s_ctx, 16)
                sp.dma_start(wv0[:], w["Wv"].rearrange("(k p) n -> p k n", p=CP)).then_inc(s_ctx, 16)
                sp.dma_start(bk0[:], w["bk"].rearrange("(k p) -> p k", p=P), allow_slow_non_contiguous=True).then_inc(s_ctx, 16)
                sp.dma_start(bv0[:], w["bv"].partition_broadcast(P)).then_inc(s_ctx, 16)
                for b in range(B):
                    sp.dma_start(xs[:, b * TPB * D:(b + 1) * TPB * D].rearrange("p (t d) -> p t d", d=D),
                                 x[b].rearrange("(t p) d -> p t d", p=P)).then_inc(s_x[b], 16)

            @block.scalar
            def _(act):
                act.dma_start(wq0[:], w["Wq"].rearrange("(k p) n -> p k n", p=P)).then_inc(s_small, 16)
                act.dma_start(wo0[:], w["Wo"].rearrange("(k p) n -> p k n", p=P)).then_inc(s_small, 16)
                act.dma_start(bq0[:], w["bq"].rearrange("(k p) -> p k", p=P), allow_slow_non_contiguous=True).then_inc(s_small, 16)
                act.dma_start(bo0[:], w["bo"].partition_broadcast(P)).then_inc(s_small, 16)
                act.wait_ge(s_small, 64)
                act.mul(bq0[:], bq0[:], D0 ** -0.5).then_inc(s_tbl, 1)

            @block.gpsimd
            def _(pool):
                pool.memset(ident[:], 0.0).then_inc(s_id, 1)
                pool.memset(mhalf[:], -0.5).then_inc(s_id, 1)
                pool.memset(hsel[:], 1.0).then_inc(s_id, 1)
                pool.memset(psel[:], 1.0).then_inc(s_id, 1)
                pool.wait_ge(s_id, 4)
                pool.affine_select(out=ident[:], in_=ident[:], compare_op=ALU.not_equal, fill=1.0, base=0,
                                   pattern=[[-1, P]], channel_multiplier=1).then_inc(s_id, 1)
                pool.affine_select(out=hsel[:], in_=hsel[:], compare_op=ALU.is_ge, fill=0.0, base=0,
                                   pattern=[[-D0, 8]], channel_multiplier=1).then_inc(s_id, 1)
                pool.wait_ge(s_id, 6)
                pool.affine_select(out=hsel[:], in_=hsel[:], compare_op=ALU.is_ge, fill=0.0, base=D0 - 1,
                                   pattern=[[D0, 8]], channel_multiplier=-1).then_inc(s_id, 1)
                n = 7
                for v in range(2):
                    for jj in range(HJ):
                        h0, nh = tile_heads(jj)
                        pool.affine_select(out=psel[:, v, jj, :], in_=psel[:, v, jj, :], compare_op=ALU.is_ge,
                                           fill=0.0, base=P * jj - KP * h0, pattern=[[-KP, 3]],
                                           channel_multiplier=1).then_inc(s_id, 1)
                        n += 1
                        pool.wait_ge(s_id, n)
                        pool.affine_select(out=psel[:, v, jj, :], in_=psel[:, v, jj, :], compare_op=ALU.is_ge,
                                           fill=0.0, base=NKEY + v - 1 - P * jj + KP * h0, pattern=[[KP, 3]],
                                           channel_multiplier=-1).then_inc(s_id, 1)
                        n += 1

            @block.tensor
            def _(pe):
                pe.wait_ge(s_ctx, 80)
                pe.wait_ge(s_id, 5)
                for k in range(CK):
                    for b in range(B):
                        last = pe.transpose(pb[k][0:CP, b * KP:b * KP + NKEY], ctx[:, b, k * CP:(k + 1) * CP],
                                            ident[0:NKEY, 0:NKEY])
                    last.then_inc(s_cT, 1)
                pe.wait_ge(s_cTe, 5)
                for m in range(KT):
                    for k in range(CK):
                        last = pe.matmul(pb[2 + m][:, 0:B * KP], wk0[:, k, m * P:(m + 1) * P], ctxT[:, k, :, :],
                                         start=(k == 0), stop=(k == CK - 1))
                    last.then_inc(s_k0, 1)
                for n, (b, j) in enumerate((b, j) for b in range(B) for j in range(NJ)):
                    h0, nh = tile_heads(j)
                    h0 += 8 * (j // HJ)
                    off = P * j % KP
                    if n >= 2:
                        pe.wait_ge(s_v0e, n - 1)
                    for k in range(CK):
                        last = pe.matmul(pb[n % 2][:, 0:nh * D0],
                                         ctx3[:, k, b, :, :].rearrange("p r k -> p (r k)")[:, off:off + P],
                                         wv0[:, k, h0 * D0:(h0 + nh) * D0], start=(k == 0), stop=(k == CK - 1))
                    last.then_inc(s_v0, 1)

            @block.vector
            def _(dve):
                for k in range(CK):
                    dve.wait_ge(s_cT, k + 1)
                    v = pb[k][0:CP, 0:B * KP].rearrange("p (b k) -> p b k", b=B)
                    dve.tensor_copy(ctxT[:, k, :, 0:NKEY], v[:, :, 0:NKEY]).then_inc(s_cTe, 1)
                    dve.tensor_copy(ctxT[:, k, :, NKEY:KP],
                                    v[:, :, 0:1].broadcast_to([CP, B, KP - NKEY])).then_inc(s_cTe, 1)
                dve.wait_ge(s_cTe, 4)
                for r in range(3):
                    last = dve.tensor_copy(ctx3[:, :, :, r, :].rearrange("p c b k -> p (c b) k"),
                                           ctxT[:].rearrange("p c b k -> p (c b) k"))
                last.then_inc(s_cTe, 1)
                dve.wait_ge(s_id, 7)
                for m in range(KT):
                    dve.wait_ge(s_k0, m + 1)
                    dve.tensor_scalar(kT[:, m, :, :], pb[2 + m][:, 0:B * KP].rearrange("p (b k) -> p b k", b=B),
                                      bk0[:, m:m + 1], None, ALU.add).then_inc(s_k0e, 1)
                    dve.wait_ge(s_k0e, m + 1)
                    for h in range(8):
                        dve.tensor_scalar(keys0[:, :, m, h, :], kT[:, m, :, :], hsel[:, h:h + 1], None, ALU.mult)
                dve.wait_ge(s_id, 7 + 2 * HJ)
                for n, (b, j) in enumerate((b, j) for b in range(B) for j in range(NJ)):
                    h0, nh = tile_heads(j)
                    h0 += 8 * (j // HJ)
                    sel = psel[:, 0, j % HJ, 0:nh]
                    dve.wait_ge(s_v0, n + 1)
                    vv = vals0[:, b, j, 0:nh, 0:D0]
                    dve.tensor_tensor(vv, pb[n % 2][:, 0:nh * D0].rearrange("p (h d) -> p h d", d=D0),
                                      bv0[:, h0 * D0:(h0 + nh) * D0].rearrange("p (h d) -> p h d", d=D0),
                                      ALU.add).then_inc(s_v0e, 1)
                    dve.tensor_copy(vals0[:, b, j, 0:nh, D0], sel)
                    dve.wait_ge(s_v0e, n + 1)
                    dve.tensor_tensor(vv, vv, sel.unsqueeze(2).broadcast_to([P, nh, D0]), ALU.mult)

    attention(nc, stack, sem, sbuf, xt, col, 0, dict(
        s_x=s_x, ident=ident, mhalf=mhalf, wq=wq0, bq=bq0, wo=wo0, bo=bo0, keys=keys0, vals=vals0,
        hstat=hstat, hamax=hamax))
    att0.close()
    old, sem = sem, Sems(nc)
    ffn(nc, sem, old, sbuf, xs, dict(w, ident=ident, mhalf=mhalf, hstat=hstat, hrstd=hrstd, hamax=hamax))
    old, sem = sem, Sems(nc)
    with ExitStack() as att1:
        p1 = prepare1(nc, att1, sem, old, sbuf, dict(w, ident=ident, ctxT=ctxT, psel=psel, mask=mask))
        attention(nc, stack, sem, sbuf, xt, col, 1, dict(p1, ident=ident, mhalf=mhalf))
    moe(nc, stack, sem, sbuf, xs, xt, col, dict(w, ident=ident, mhalf=mhalf), out)


def prepare1(nc, st, sem, retired, sbuf, c):
    OD = H * D1
    NM = OD // P

    def s(name):
        return sem("p1_" + name)
    s_in, s_m, s_id3, s_wT, s_wTe = s("in"), s("m"), s("id3"), s("wT"), s("wTe")
    s_mr, s_mre, s_k, s_ke, s_A, s_Ah, s_Al = s("mr"), s("mre"), s("k"), s("ke"), s("A"), s("Ah"), s("Al")
    s_v, s_ve, s_nv, s_c3, s_vf, s_km = s("v"), s("ve"), s("nv"), s("c3"), s("vf"), s("km")
    s_wo = s("wo")

    keysh = sbuf(st, "keysh", [P, B, KT, SW], F32R)
    keysl = sbuf(st, "keysl", [P, B, KT, SW], F32R)
    vals = sbuf(st, "vals1", [P, B, NSLOT, D1 + 1])
    woh = sbuf(st, "woh1", [P, NM, D], F32R)
    wol = sbuf(st, "wol1", [P, NM, D], F32R)
    gout = sbuf(st, "gout", [P, D])
    with ExitStack() as tp:
        wkv = sbuf(tp, "wkv", [CP, CK, 2 * OD])
        wq = sbuf(tp, "wq1", [P, KT, OD])
        wo = wq[:].rearrange("p k n -> p (k n)").rearrange("p (m d) -> p m d", d=D)
        wqT = sbuf(tp, "wqT1", [P, NM, D])
        k1 = sbuf(tp, "k1", [P, 2, B * KP])
        gsc = sbuf(tp, "gsc", [P, KT])
        nk = sbuf(tp, "nk", [P, 1])
        nv = sbuf(tp, "nv", [P, D1])
        m8 = sbuf(tp, "m8", [P, B, NKEY], U8)
        mc8 = sbuf(tp, "mc8", [NKEY, B], U8)
        mb = sbuf(tp, "mb", [P, B, KP])
        nm = sbuf(tp, "nm", [P, B, KP])
        mcol = sbuf(tp, "mcol", [NKEY, B])
        id3 = sbuf(tp, "id3", [NKEY, 3, KP])
        ctx3 = sbuf(tp, "ctx3b", [CP, CK, B, 3, KP])
        mrow = sbuf(tp, "mrow", [P, HJ, B])
        sel = sbuf(tp, "sel1", [P, HJ, B, 3])
        nsel = sbuf(tp, "nsel", [P, HJ, 3])
        NV = sbuf(tp, "NV", [P, HJ, 3, D1])
        pb = [tp.enter_context(nc.psum_tensor(f"p1b{i}", [P, 512], F32)) for i in range(8)]
        WT, KB, AB, VB = pb[0:2], pb[2:4], pb[4:6], pb[6:8]

        with nc.Block() as block:
            @block.sync
            def _(sp):
                sp.dma_start(m8[:], c["mask"].rearrange("b k -> (b k)").partition_broadcast(P)
                             .rearrange("p (b k) -> p b k", b=B)).then_inc(s_m, 16)
                sp.dma_start(mc8[:], c["mask"].rearrange("b k -> k b"),
                             allow_slow_non_contiguous=True).then_inc(s_m, 16)
                sp.dma_start(nk[0:D1, :], c["L1_xattn_null_kv"][0].rearrange("(d a) -> d a", a=1)).then_inc(s_m, 16)
                sp.dma_start(nk[D1:P, :], c["L1_xattn_null_kv"][0].rearrange("(d a) -> d a", a=1)).then_inc(s_m, 16)
                sp.dma_start(nv[:], c["L1_xattn_null_kv"][1].partition_broadcast(P)).then_inc(s_m, 16)
                sp.dma_start(gsc[:], c["L1_xattn_g_norm"].rearrange("(k p) -> p k", p=P),
                             allow_slow_non_contiguous=True).then_inc(s_m, 16)
                sp.dma_start(wq[:], c["L1_xattn_Wq"].rearrange("(k p) n -> p k n", p=P)).then_inc(s_in, 16)
                sp.dma_start(wkv[:], c["L1_xattn_Wkv"].rearrange("(k p) n -> p k n", p=CP)).then_inc(s_in, 16)
                sp.dma_start(gout[:], c["L1_xattn_g_out"].partition_broadcast(P)).then_inc(s_in, 16)
                retired.clear(sp)
                sp.wait_ge(s_wT, NM // 2)
                sp.dma_start(wo[:], c["L1_xattn_Wout"].rearrange("(k p) n -> p k n", p=P)).then_inc(s_wo, 16)

            @block.gpsimd
            def _(pool):
                pool.memset(mb[:], 0.0).then_inc(s_id3, 1)
                for r in range(3):
                    last = pool.tensor_copy(id3[:, r, :], c["ident"][0:NKEY, 0:KP])
                last.then_inc(s_id3, 1)
                for r in range(3):
                    last = pool.tensor_copy(ctx3[:, :, :, r, :].rearrange("p c b k -> p (c b) k"),
                                            c["ctxT"][:].rearrange("p c b k -> p (c b) k"))
                last.then_inc(s_c3, 1)

            @block.tensor
            def _(pe):
                pe.wait_ge(s_in, 48)
                for m in range(NM // 2):
                    if m >= 2:
                        pe.wait_ge(s_wTe, m - 1)
                    for n in range(2):
                        for k in range(KT):
                            last = pe.transpose(WT[m % 2][:, (2 * n + k) * P:(2 * n + k + 1) * P],
                                                wq[:, k, (2 * m + n) * P:(2 * m + n + 1) * P], c["ident"][:])
                    last.then_inc(s_wT, 1)
                pe.wait_ge(s_id3, 2)
                pe.wait_ge(s_mre, 1)
                for jj in range(HJ):
                    off = P * jj % KP
                    last = pe.matmul(VB[0][:, jj * B:(jj + 1) * B],
                                     id3[:].rearrange("p r k -> p (r k)")[:, off:off + P], mcol[:],
                                     start=True, stop=True)
                last.then_inc(s_mr, 1)
                for m in range(NM):
                    if m >= 2:
                        pe.wait_ge(s_ke, m - 1)
                    for k in range(CK):
                        last = pe.matmul(KB[m % 2][:, 0:B * KP], wkv[:, k, m * P:(m + 1) * P],
                                         c["ctxT"][:, k, :, :], start=(k == 0), stop=(k == CK - 1))
                    last.then_inc(s_k, 1)
                    for n in range(5 * m, 5 * m + 5):
                        b, j = n // NJ, n % NJ
                        h0, nh = tile_heads(j)
                        h0 += 8 * (j // HJ)
                        off = P * j % KP
                        if n == 0:
                            pe.wait_ge(s_c3, 1)
                            pe.wait_ge(s_mre, 2)
                        if n >= 2:
                            pe.wait_ge(s_ve, n - 1)
                        for k in range(CK):
                            last = pe.matmul(VB[n % 2][:, 0:nh * D1],
                                             ctx3[:, k, b, :, :].rearrange("p r k -> p (r k)")[:, off:off + P],
                                             wkv[:, k, OD + h0 * D1:OD + (h0 + nh) * D1], start=(k == 0),
                                             stop=(k == CK - 1))
                        last.then_inc(s_v, 1)
                    pe.wait_ge(s_ke, m + 1)
                    pe.wait_ge(s_wTe, m // 2 + 1)
                    for hh in range(2):
                        for k in range(KT):
                            n = 4 * m + 2 * hh + k
                            if n >= 2:
                                pe.wait_ge(s_Al, n - 1)
                            pe.matmul(AB[n % 2][:, 0:B * KP], wqT[hh * D1:(hh + 1) * D1, m, k * P:(k + 1) * P],
                                      k1[hh * D1:(hh + 1) * D1, m % 2, :], start=True, stop=True).then_inc(s_A, 1)

            @block.scalar
            def _(act):
                act.wait_ge(s_m, 96)
                act.mul(gsc[:], gsc[:], D1 ** -0.5).then_inc(s_Ah, 1)
                for m in range(NM // 2):
                    act.wait_ge(s_wT, m + 1)
                    act.copy(wqT[:, 2 * m:2 * m + 2, :].rearrange("p m n -> p (m n)"), WT[m % 2][:]).then_inc(s_wTe, 1)
                for n in range(4 * NM):
                    m, hh, k = n // 4, n // 2 % 2, n % 2
                    h = 2 * m + hh
                    act.wait_ge(s_A, n + 1)
                    act.wait_ge(s_Ah, 1)
                    act.activation(keysh[:, :, k, h * KP:(h + 1) * KP],
                                   AB[n % 2][:, 0:B * KP].rearrange("p (b k) -> p b k", b=B), ACT.Copy,
                                   scale=gsc[:, k:k + 1]).then_inc(s_Ah, 1)
                act.wait_ge(s_wo, 16)
                act.copy(woh[:], wo).then_inc(s_wo, 1)

            @block.vector
            def _(dve):
                dve.wait_ge(s_m, 96)
                dve.wait_ge(s_id3, 1)
                dve.tensor_copy(mb[:, :, 0:NKEY], m8[:]).then_inc(s_nv, 1)
                dve.tensor_copy(mcol[:], mc8[:]).then_inc(s_mre, 1)
                dve.wait_ge(s_nv, 1)
                dve.tensor_scalar(nm[:], mb[:], -1.0, 1.0, ALU.mult, ALU.add).then_inc(s_nv, 1)
                dve.tensor_tensor(nsel[:], c["psel"][:, 1], c["psel"][:, 0], ALU.subtract).then_inc(s_nv, 1)
                dve.wait_ge(s_nv, 3)
                dve.tensor_scalar(nm[:], nm[:], nk[:, 0:1], None, ALU.mult).then_inc(s_nv, 1)
                dve.tensor_tensor(NV[:].rearrange("p j i d -> p (j i) d"),
                                  nsel[:].rearrange("p j i -> p (j i)").unsqueeze(2).broadcast_to([P, 3 * HJ, D1]),
                                  nv[:].unsqueeze(1).broadcast_to([P, 3 * HJ, D1]), ALU.mult).then_inc(s_nv, 1)
                dve.wait_ge(s_mr, 1)
                dve.tensor_copy(mrow[:].rearrange("p j b -> p (j b)"), VB[0][:, 0:HJ * B]).then_inc(s_mre, 1)
                dve.wait_ge(s_mre, 2)
                for jj in range(HJ):
                    last = dve.tensor_tensor(sel[:, jj, :, :], c["psel"][:, 0, jj, :].unsqueeze(1).broadcast_to([P, B, 3]),
                                             mrow[:, jj, :].unsqueeze(2).broadcast_to([P, B, 3]), ALU.mult)
                last.then_inc(s_nv, 1)
                dve.wait_ge(s_nv, 6)

                def remainder(n):
                    m, hh, k = n // 4, n // 2 % 2, n % 2
                    h = 2 * m + hh
                    dve.wait_ge(s_Ah, n + 2)
                    hi = keysh[:, :, k, h * KP:(h + 1) * KP]
                    dve.scalar_tensor_tensor(keysl[:, :, k, h * KP:(h + 1) * KP],
                                             AB[n % 2][:, 0:B * KP].rearrange("p (b k) -> p b k", b=B),
                                             gsc[:, k:k + 1], hi.bitcast(F32), ALU.mult,
                                             ALU.subtract).then_inc(s_Al, 1)
                for m in range(NM):
                    dve.wait_ge(s_k, m + 1)
                    if m >= 2:
                        dve.wait_ge(s_A, 4 * (m - 1))
                    kv = k1[:, m % 2, :]
                    dve.tensor_tensor(kv, KB[m % 2][:, 0:B * KP], mb[:].rearrange("p b k -> p (b k)"),
                                      ALU.mult).then_inc(s_km, 1)
                    dve.wait_ge(s_km, m + 1)
                    dve.tensor_tensor(kv, kv, nm[:].rearrange("p b k -> p (b k)"), ALU.add).then_inc(s_ke, 1)
                    for n in range(5 * m, 5 * m + 5):
                        b, j = n // NJ, n % NJ
                        h0, nh = tile_heads(j)
                        jj = j % HJ
                        n0 = first_slot(j)
                        v = vals[:, b, n0:n0 + nh, 0:D1]
                        dve.wait_ge(s_v, n + 1)
                        dve.tensor_tensor(v, VB[n % 2][:, 0:nh * D1].rearrange("p (h d) -> p h d", d=D1),
                                          sel[:, jj, b, 0:nh].unsqueeze(2).broadcast_to([P, nh, D1]),
                                          ALU.mult).then_inc(s_ve, 1)
                        dve.tensor_tensor(vals[:, b, n0:n0 + nh, D1], sel[:, jj, b, 0:nh], nsel[:, jj, 0:nh], ALU.add)
                        dve.wait_ge(s_ve, n + 1)
                        dve.tensor_tensor(v, v, NV[:, jj, 0:nh, :], ALU.add).then_inc(s_vf, 1)
                    for n in range(4 * m, 4 * m + 4):
                        remainder(n)
                dve.wait_ge(s_wo, 17)
                dve.tensor_tensor(wol[:], wo, woh[:].bitcast(F32), ALU.subtract)
    retired.stack.close()
    return dict(keysh=keysh, keysl=keysl, vals=vals, woh=woh, wol=wol, gout=gout)


def attention(nc, stack, sem, sbuf, xt, col, layer, c):
    L1 = layer == 1
    dh = D1 if L1 else D0
    OD = H * dh
    NO = OD // P
    PH = 1 if L1 else 2
    NC = NO // 4 if L1 else 1
    sb = [0, 1, 2, 0] if L1 else [0, 1, 2, 3]
    PTS = [range(0, 4), range(4, 8), range(8, 10)]
    tag = f"a{layer}_"

    def s(name):
        return sem(tag + name)

    s_stat, s_aggr, s_veps, s_rstd, s_xn = s("stat"), s("aggr"), s("veps"), s("rstd"), s("xn")
    s_xT, s_xTe, s_q, s_qe, s_S = s("xT"), s("xTe"), s("q"), s("qe"), s("S")
    s_mx, s_clip, s_U, s_sh, s_P = s("mx"), s("clip"), s("U"), s("sh"), s("P")
    s_PT, s_PTe, s_PV, s_rec, s_O = s("PT"), s("PTe"), s("PV"), s("rec"), s("O")
    s_oT, s_oTe, s_y, s_xb, s_x1 = s("oT"), s("oTe"), s("y"), s("xb"), s("x1")
    s_st2, s_ag2, s_ve2, s_rs2, s_h = s("st2"), s("ag2"), s("ve2"), s("rs2"), s("h")
    s_y2, s_yg, s_xl, s_oTl = s("y2"), s("yg"), s("xl"), s("oTl")

    order = []
    for t in range(-3, NT + 1):
        order += [("PT", t, k) for k in range(3)] * (0 <= t < NT)
        order += [("xT", t + 3, 0)] * (0 <= t + 3 < NT)
        order += [("oT", t - 1, k) for k in range(NC)] * (0 <= t - 1 < NT)
        order += [("y", t - 1, 0)] * (L1 and 0 <= t - 1 < NT)
    ring = Slots(order)
    freed = {"xT": lambda t, k: (s_xl if L1 else s_xTe, t.of(lambda n: n + 1)),
             "oT": lambda t, k: (s_oTl if L1 else s_oTe, t.of(lambda n: NC * n + k + 1)),
             "PT": lambda t, k: (s_PTe, t.of(lambda n: 3 * n + k + 1)),
             "y": lambda t, k: (s_y2, t.of(lambda n: n + 1))}

    LO, HI, FIRST, LAST = 3, 26, -5, NT + 1
    E1 = D1 + 1
    HB = ((0, 6), (6, 11), (11, 16))

    def tiles_of(bank):
        return [j for j in range(NJ) if bank[0] < (j // HJ) * 8 + sum(tile_heads(j)) and bank[1] > (j // HJ) * 8 + tile_heads(j)[0]]
    first_tile = [tiles_of(q)[0] for q in HB]
    last_tile = [tiles_of(q)[-1] for q in HB]

    with ExitStack() as st:
        ps = [st.enter_context(nc.psum_tensor(f"{tag}ps{i}", [P, 512], F32)) for i in range(8)]
        if L1:
            S, R, PV, M = ps[0:3], ps[3:5], ps[5:8], None
        else:
            S, R, PV, M = ps[0:4], ps[4:6], ps[6:7], ps[7]
        stats = sbuf(st, tag + "stats", [P, 2, 6])
        xag = sbuf(st, tag + "xag", [P, 2, 2])
        xve = sbuf(st, tag + "xve", [P, 2])
        xrs = sbuf(st, tag + "xrs", [P, 2])
        xn = [sbuf(st, f"{tag}xn{i}", [P, D]) for i in range(2)]
        xnT = [sbuf(st, f"{tag}xnT{i}", [P, KT, P], F32R if L1 else F32) for i in range(2)]
        xnl = [sbuf(st, f"{tag}xnl{i}", [P, KT, P], F32R) for i in range(2)] if L1 else None
        qT = None if L1 else [sbuf(st, f"{tag}qT{i}", [P, KT, P]) for i in range(2)]
        mx = [sbuf(st, f"{tag}mx{i}", [P, H]) for i in range(2)]
        U = [sbuf(st, f"{tag}U{i}", [P, SW]) for i in range(2)]
        PTs = [sbuf(st, f"{tag}PT{i}", [P, NJ, P]) for i in range(2)]
        rc = [sbuf(st, f"{tag}rc{i}", [P, H]) for i in range(2)]
        o = [sbuf(st, f"{tag}o{i}", [P, OD]) for i in range(1 if L1 else 2)] * (2 if L1 else 1)
        oT = [sbuf(st, f"{tag}oT{i}", [P, NO, P], F32R if L1 else F32) for i in range(2)]
        st2 = sbuf(st, tag + "st2", [P, 2, 6])
        yag = sbuf(st, tag + "yag", [P, 2, 2])
        hb = None if L1 else sbuf(st, tag + "hb", [P, 2, D])
        oTl = [sbuf(st, f"{tag}oTl{i}", [P, NO, P], F32R) for i in range(2)] if L1 else None
        if L1:
            yb = [sbuf(st, f"{tag}yb{i}", [P, D]) for i in range(2)]
            yve = sbuf(st, tag + "yve", [P, 2])
            yrs = sbuf(st, tag + "yrs", [P, 2])

        def ring_wait(pe, kind, t, k=0):
            prev = ring.before(kind, t, k)
            if prev is not None:
                pe.wait_ge(*freed[prev[0]](prev[1], prev[2]))
            return R[ring.bank(kind, t, k)]

        with nc.Block() as block:
            @block.tensor
            def _(pe):
                def scores(a, g):
                    b = a.batch
                    if L1:
                        if g == 3:
                            pe.wait_ge(s_U, a.of(lambda n: 4 * n + 1))
                        elif a.t0 >= 1:
                            pe.wait_ge(s_U, a.of(lambda n: 4 * n - 4 + (4 if g == 0 else g + 1)))
                        n = 0
                        for x_, k_ in ((xnT, "keysh"), (xnl, "keysh"), (xnT, "keysl")):
                            for k in range(KT):
                                last = pe.matmul(
                                    S[sb[g]][:, 0:QW], x_[a.p][:, k, :],
                                    c[k_][:].rearrange("p b m n -> p (b m n)")[
                                        :, bass.ds(b * (KT * SW) + k * SW + g * QW, QW)],
                                    start=(n == 0), stop=(n == 3 * KT - 1))
                                n += 1
                        last.then_inc(s_S, 1)
                        return
                    if a.t0 >= 1:
                        pe.wait_ge(s_clip, a.of(lambda n: 4 * n - 4 + g + 1))
                    pe.matmul(S[sb[g]][:, 0:QW], qT[a.p][:, g // 2, :],
                              c["keys"][:].rearrange("p b m h k -> p (b m h k)")[
                                  :, bass.ds(b * (KT * 8 * KP) + g * QW, QW)],
                              start=True, stop=True).then_inc(s_S, 1)

                def probs_T(t, k):
                    if k == 0:
                        pe.wait_ge(s_P, t.of(lambda n: PH * (n + 1)))
                    r = ring_wait(pe, "PT", t, k)
                    for n, j in enumerate(PTS[k]):
                        last = pe.transpose(r[:, n * P:(n + 1) * P], U[t.p][:, j * P:(j + 1) * P], c["ident"][:])
                    last.then_inc(s_PT, 1)

                def out_T(a, kk):
                    if kk == 0:
                        pe.wait_ge(s_O, a.of(lambda n: n + 1))
                    r = ring_wait(pe, "oT", a, kk)
                    for k in range(NO // NC):
                        n = kk * (NO // NC) + k
                        last = pe.transpose(r[:, k * P:(k + 1) * P], o[a.p][:, n * P:(n + 1) * P], c["ident"][:])
                    last.then_inc(s_oT, 1)

                def body(t):
                    nxt, new, old = t + 2, t + 3, t + -1
                    if t.ok():
                        probs_T(t, 0)
                        probs_T(t, 1)
                    if nxt.ok():
                        if L1:
                            pe.wait_ge(s_xTe, nxt.of(lambda n: n + 1))
                            pe.wait_ge(s_xl, nxt.of(lambda n: n + 1))
                        else:
                            pe.wait_ge(s_qe, nxt.of(lambda n: n + 1))
                        scores(nxt, 0)
                    if t.ok():
                        probs_T(t, 2)
                    if new.ok():
                        pe.wait_ge(s_xn, new.of(lambda n: n + 1))
                        r = ring_wait(pe, "xT", new)
                        for k in range(KT):
                            last = pe.transpose(r[:, k * P:(k + 1) * P], xn[new.p][:, k * P:(k + 1) * P],
                                                c["ident"][:])
                        last.then_inc(s_xT, 1)
                    if nxt.ok():
                        scores(nxt, 1)
                    if old.ok():
                        out_T(old, 0)
                    a = new
                    if a.ok() and not L1:
                        pe.wait_ge(s_xTe, a.of(lambda n: n + 1))
                        if a.t0 >= 5:
                            pe.wait_ge(s_x1, a.of(lambda n: n - 4))
                        elif a.t0 >= 1:
                            pe.wait_ge(s_qe, a.of(lambda n: n))
                        for m in range(KT):
                            for k in range(KT):
                                last = pe.matmul(M[:, m * P:(m + 1) * P], c["wq"][:, k, m * P:(m + 1) * P],
                                                 xnT[a.p][:, k, :], start=(k == 0), stop=(k == KT - 1))
                        last.then_inc(s_q, 1)
                    if nxt.ok():
                        scores(nxt, 2)
                    for kk in range(1, NC):
                        if old.ok():
                            out_T(old, kk)
                    if nxt.ok():
                        scores(nxt, 3)
                    a = t + -1
                    if a.ok():
                        pe.wait_ge(s_oTe, a.of(lambda n: NC * (n + 1)))
                        if L1:
                            y = ring_wait(pe, "y", a)
                        elif a.t0 + 4 < NT:
                            pe.wait_ge(s_qe, a.of(lambda n: n + 5))
                        else:
                            pe.wait_ge(s_x1, a.of(lambda n: n))
                        if not L1:
                            y = M
                        if L1:
                            parts = ((oT, c["woh"]), (oT, c["wol"]), (oTl, c["woh"]))
                        else:
                            parts = ((oT, c["wo"]),)
                        pairs = [(o_[a.p][:, k, :], w_[:, k, :]) for o_, w_ in parts for k in range(NO)]
                        for n, (lhs, rhs) in enumerate(pairs):
                            if n == 2 * NO:
                                pe.wait_ge(s_oTl, a.of(lambda n: NC * (n + 1)))
                            last = pe.matmul(y[:, 0:D], lhs, rhs, start=(n == 0), stop=(n == len(pairs) - 1))
                        last.then_inc(s_y, 1)
                    if t.ok():
                        if t.t0 >= 1:
                            pe.wait_ge(s_O, t.of(lambda n: n))
                        for k, js in enumerate(PTS):
                            pe.wait_ge(s_PTe, t.of(lambda n: 3 * n + k + 1))
                            for j in js:
                                h0, nh = tile_heads(j)
                                h0 += 8 * (j // HJ)
                                if L1:
                                    row = t.batch * (NSLOT * E1) + first_slot(j) * E1
                                    for q, (lo_, hi_) in enumerate(HB):
                                        a_, b_ = max(h0, lo_), min(h0 + nh, hi_)
                                        if a_ >= b_:
                                            continue
                                        last = pe.matmul(
                                            PV[q][:, (a_ - lo_) * E1:(b_ - lo_) * E1], PTs[t.p][:, j, :],
                                            c["vals"][:].rearrange("p b s e -> p (b s e)")[
                                                :, bass.ds(row + (a_ - h0) * E1, (b_ - a_) * E1)],
                                            start=(j == first_tile[q]),
                                            stop=(j == last_tile[q]), skip_group_check=True)
                                    continue
                                E = D0 + 1
                                last = pe.matmul(
                                    PV[0][:, h0 * E:(h0 + nh) * E], PTs[t.p][:, j, :],
                                    c["vals"][:].rearrange("p b j h e -> p (b j h e)")[
                                        :, bass.ds(t.batch * (NJ * 3 * E) + j * 3 * E, nh * E)],
                                    start=(j == 0), stop=(j == NJ - 1), skip_group_check=True)
                        last.then_inc(s_PV, 1)

                pipeline(pe, body, FIRST, LAST, LO, HI)

            @block.scalar
            def _(act):
                def body(t):
                    if t.ok():
                        if t.t0 >= 2:
                            act.wait_ge(s_PV, t.of(lambda n: n - 1))
                        for k, js in enumerate(PTS):
                            act.wait_ge(s_PT, t.of(lambda n: 3 * n + k + 1))
                            act.copy(PTs[t.p][:, js[0]:js[-1] + 1, :].rearrange("p j n -> p (j n)"),
                                     R[ring.bank("PT", t, k)][:, 0:len(js) * P]).then_inc(s_PTe, 1)
                    a = t + 3
                    if a.ok():
                        act.wait_ge(s_xT, a.of(lambda n: n + 1))
                        if a.t0 >= 2 and L1:
                            act.wait_ge(s_S, a.of(lambda n: 4 * (n - 1)))
                        elif a.t0 >= 2:
                            act.wait_ge(s_q, a.of(lambda n: n - 1))
                        act.copy(xnT[a.p][:].rearrange("p k n -> p (k n)"),
                                 R[ring.bank("xT", a)][:, 0:D]).then_inc(s_xTe, 1)
                    a = t + -1
                    if a.ok():
                        if a.t0 >= 2:
                            act.wait_ge(s_y, a.of(lambda n: n - 1))
                        for kk in range(NC):
                            act.wait_ge(s_oT, a.of(lambda n: NC * n + kk + 1))
                            w_ = OD // NC
                            act.copy(oT[a.p][:].rearrange("p k n -> p (k n)")[:, kk * w_:(kk + 1) * w_],
                                     R[ring.bank("oT", a, kk)][:, 0:w_]).then_inc(s_oTe, 1)
                    a = t + -1
                    if a.ok() and L1:
                        act.wait_ge(s_y, a.of(lambda n: n + 1))
                        if a.t0 >= 2:
                            act.wait_ge(s_x1, a.of(lambda n: n - 1))
                        act.copy(yb[a.p][:], R[ring.bank("y", a)][:, 0:D]).then_inc(s_y2, 1)
                    a = t + 3
                    if a.ok() and not L1:
                        act.wait_ge(s_q, a.of(lambda n: n + 1))
                        if a.t0 >= 2:
                            act.wait_ge(s_S, a.of(lambda n: 4 * (n - 1)))
                        for m in range(KT):
                            last = act.activation(qT[a.p][:, m, :], M[:, m * P:(m + 1) * P], ACT.Identity,
                                                  bias=c["bq"][:, m:m + 1], scale=D0 ** -0.5)
                        last.then_inc(s_qe, 1)
                    a = t + 2
                    if a.ok():
                        if L1:
                            act.wait_ge(s_U, a.of(lambda n: 4 * n + 4))
                            act.activation(U[a.p][:], U[a.p][:], ACT.Exp).then_inc(s_P, 1)
                        else:
                            act.wait_ge(s_sh, a.of(lambda n: 2 * n + 2))
                            act.activation(U[a.p][:, 0:2 * QW], U[a.p][:, 0:2 * QW], ACT.Exp).then_inc(s_P, 1)
                            act.wait_ge(s_mx, a.of(lambda n: 4 * n + 4))
                            for h in range(8, H):
                                v = U[a.p][:, h * KP:(h + 1) * KP]
                                last = act.activation(v, v, ACT.Exp, bias=mx[a.p][:, h:h + 1])
                            last.then_inc(s_P, 1)

                pipeline(act, body, FIRST, LAST, LO, HI)

            @block.gpsimd
            def _(pool):
                def rsqrt(t, ve, rs, s_ve, s_rs):
                    pool.wait_ge(s_ve, t.of(lambda n: n + 1))
                    pool.tensor_tensor(rs[:, t.p:t.p + 1], ve[:, t.p:t.p + 1], c["mhalf"][:],
                                       ALU.pow).then_inc(s_rs, 1)

                def body(t):
                    a = t + 2
                    if a.ok() and not L1:
                        for g in range(2):
                            pool.wait_ge(s_mx, a.of(lambda n: 4 * n + g + 1))
                            v = U[a.p][:, g * QW:(g + 1) * QW].rearrange("p (h k) -> p h k", k=KP)
                            pool.tensor_tensor(v, v, mx[a.p][:, 4 * g:4 * g + 4].unsqueeze(2).broadcast_to([P, 4, KP]),
                                               ALU.add).then_inc(s_sh, 1)
                    a = t + 5
                    if a.ok():
                        rsqrt(a, xve, xrs, s_veps, s_rstd)
                    if t.ok() and not L1:
                        pool.wait_ge(s_xn, t.of(lambda n: n + 1))
                        pool.tensor_tensor(xt(t), xt(t), c["bo"][:], ALU.add).then_inc(s_xb, 1)
                    a = t + -1
                    if a.ok() and L1:
                        rsqrt(a, yve, yrs, s_ve2, s_rs2)
                    a = t + -2
                    if a.ok() and L1:
                        pool.wait_ge(s_h, a.of(lambda n: n + 1))
                        pool.tensor_tensor(yb[a.p][:], yb[a.p][:], c["gout"][:], ALU.mult).then_inc(s_yg, 1)
                        pool.wait_ge(s_yg, a.of(lambda n: n + 1))
                        pool.tensor_tensor(xt(a), xt(a), yb[a.p][:], ALU.add).then_inc(s_x1, 1)

                pipeline(pool, body, FIRST, LAST, LO, HI)

            @block.vector
            def _(dve):
                def o_remainder(a, kk):
                    if a.t0 >= 2 and kk == 0:
                        dve.wait_ge(s_y, a.of(lambda n: n - 1))
                    dve.wait_ge(s_oTe, a.of(lambda n: NC * n + kk + 1))
                    w_ = OD // NC
                    dve.tensor_tensor(oTl[a.p][:].rearrange("p k n -> p (k n)")[:, kk * w_:(kk + 1) * w_],
                                      R[ring.bank("oT", a, kk)][:, 0:w_],
                                      oT[a.p][:].rearrange("p k n -> p (k n)")[:, kk * w_:(kk + 1) * w_].bitcast(F32),
                                      ALU.subtract).then_inc(s_oTl, 1)

                def remainder(a):
                    dve.wait_ge(s_xTe, a.of(lambda n: n + 1))
                    if a.t0 >= 2:
                        dve.wait_ge(s_S, a.of(lambda n: 4 * (n - 1)))
                    dve.tensor_tensor(xnl[a.p][:].rearrange("p k n -> p (k n)"), R[ring.bank("xT", a)][:, 0:D],
                                      xnT[a.p][:].rearrange("p k n -> p (k n)").bitcast(F32),
                                      ALU.subtract).then_inc(s_xl, 1)

                def body(t):
                    a = t + 2
                    if L1:
                        def quad(g):
                            return S[sb[g]][:, 0:QW].rearrange("p (h k) -> p h k", k=KP)

                        def top(g):
                            if a.ok():
                                dve.wait_ge(s_S, a.of(lambda n: 4 * n + g + 1))
                                dve.tensor_reduce(mx[a.p][:, 4 * g:4 * g + 4], quad(g), AX.X,
                                                  ALU.max).then_inc(s_mx, 1)

                        def shift(g):
                            if not a.ok():
                                return
                            if g == 0 and a.t0 >= 2:
                                dve.wait_ge(s_PT, a.of(lambda n: 3 * (n - 1)))
                            dve.wait_ge(s_mx, a.of(lambda n: 4 * n + g + 1))
                            dve.tensor_tensor(U[a.p][:, g * QW:(g + 1) * QW].rearrange("p (h k) -> p h k", k=KP),
                                              quad(g), mx[a.p][:, 4 * g:4 * g + 4].unsqueeze(2).broadcast_to([P, 4, KP]),
                                              ALU.subtract).then_inc(s_U, 1)
                        top(0)
                        if (t + 3).ok():
                            remainder(t + 3)
                        top(1)
                        shift(0)
                        if (t + -1).ok():
                            o_remainder(t + -1, 0)
                        shift(1)
                        top(2)
                        if (t + -1).ok():
                            o_remainder(t + -1, 1)
                        shift(2)
                        top(3)
                        shift(3)
                    if a.ok() and not L1:
                        if a.t0 >= 2:
                            dve.wait_ge(s_PT, a.of(lambda n: 3 * (n - 1)))

                        def clip(g):
                            dve.wait_ge(s_S, a.of(lambda n: 4 * n + g + 1))
                            dve.tensor_scalar(U[a.p][:, g * QW:(g + 1) * QW], S[g][:, 0:QW], CLAMP, -CLAMP, ALU.min,
                                              ALU.max).then_inc(s_clip, 1)

                        def neg_top(g):
                            dve.wait_ge(s_clip, a.of(lambda n: 4 * n + g + 1))
                            dve.tensor_reduce(mx[a.p][:, 4 * g:4 * g + 4],
                                              U[a.p][:, g * QW:(g + 1) * QW].rearrange("p (h k) -> p h k", k=KP),
                                              AX.X, ALU.max, negate=True).then_inc(s_mx, 1)
                        clip(0)
                        clip(1)
                        neg_top(0)
                        clip(2)
                        neg_top(1)
                        clip(3)
                        neg_top(2)
                        neg_top(3)
                    a = t + -1
                    if a.ok() and not L1:
                        dve.wait_ge(s_y, a.of(lambda n: n + 1))
                        dve.wait_ge(s_xb, a.of(lambda n: n + 1))
                        dve.tensor_tensor(xt(a), M[:, 0:D], xt(a), ALU.add).then_inc(s_x1, 1)
                    b = t + 4
                    if b.ok():
                        dve.wait_ge(s_rstd, b.of(lambda n: n + 1))
                        if b.t0 >= 2:
                            dve.wait_ge(s_xT, b.of(lambda n: n - 1))
                        if a.ok() and not L1:
                            dve.wait_ge(s_x1, a.of(lambda n: n + 1))
                        dve.tensor_scalar(xn[b.p][:], xt(b), xag[:, b.p, 0:1], xrs[:, b.p:b.p + 1],
                                          ALU.subtract, ALU.mult).then_inc(s_xn, 1)
                    a = t + -1
                    if a.ok():
                        if not L1:
                            if not b.ok():
                                dve.wait_ge(s_x1, a.of(lambda n: n + 1))
                            dve.bn_stats(st2[:, a.p, :], xt(a)).then_inc(s_st2, 1)
                        else:
                            dve.wait_ge(s_y2, a.of(lambda n: n + 1))
                            dve.bn_stats(st2[:, a.p, :], yb[a.p][:]).then_inc(s_st2, 1)
                    a = t + 5
                    if a.ok():
                        dve.bn_stats(stats[:, a.p, :], xt(a)).then_inc(s_stat, 1)
                    a = t + -2
                    if a.ok() and L1:
                        dve.wait_ge(s_rs2, a.of(lambda n: n + 1))
                        dve.tensor_scalar(yb[a.p][:], yb[a.p][:], yag[:, a.p, 0:1], yrs[:, a.p:a.p + 1],
                                          ALU.subtract, ALU.mult).then_inc(s_h, 1)
                    def statistics_done():
                        if (t + -1).ok():
                            dve.wait_ge(s_st2, (t + -1).of(lambda n: n + 1))
                        if (t + 5).ok():
                            dve.wait_ge(s_stat, (t + 5).of(lambda n: n + 1))
                    if t.ok() and L1:
                        dve.wait_ge(s_PV, t.of(lambda n: n + 1))
                        def pv(q):
                            n_ = HB[q][1] - HB[q][0]
                            return PV[q][:, 0:n_ * E1].rearrange("p (h e) -> p h e", e=E1)
                        for q, (lo_, hi_) in enumerate(HB):
                            last = dve.reciprocal(rc[t.p][:, lo_:hi_], pv(q)[:, :, D1])
                        last.then_inc(s_rec, 1)
                        dve.wait_ge(s_rec, t.of(lambda n: n + 1))
                        if t.t0 >= 1:
                            dve.wait_ge(s_oT, t.of(lambda n: NC * n))
                        statistics_done()
                        for q, (lo_, hi_) in enumerate(HB):
                            last = dve.tensor_tensor(
                                o[t.p][:, lo_ * D1:hi_ * D1].rearrange("p (h d) -> p h d", d=D1), pv(q)[:, :, 0:D1],
                                rc[t.p][:, lo_:hi_].unsqueeze(2).broadcast_to([P, hi_ - lo_, D1]), ALU.mult)
                        last.then_inc(s_O, 1)
                    if t.ok() and not L1:
                        dve.wait_ge(s_PV, t.of(lambda n: n + 1))
                        pv = PV[0][:, 0:H * (D0 + 1)].rearrange("p (h e) -> p h e", e=D0 + 1)
                        dve.reciprocal(rc[t.p][:], pv[:, :, D0]).then_inc(s_rec, 1)
                        dve.wait_ge(s_rec, t.of(lambda n: n + 1))
                        if t.t0 >= 2:
                            dve.wait_ge(s_oT, t.of(lambda n: n - 1))
                        statistics_done()
                        dve.tensor_tensor(o[t.p][:].rearrange("p (h d) -> p h d", d=D0), pv[:, :, 0:D0],
                                          rc[t.p][:].unsqueeze(2).broadcast_to([P, H, D0]),
                                          ALU.mult).then_inc(s_O, 1)

                    if (t + -1).ok():
                        if not t.ok():
                            statistics_done()
                        dve.bn_aggr(yag[:, 1 - t.p, :], st2[:, 1 - t.p, :]).then_inc(s_ag2, 1)
                    if (t + 5).ok():
                        if not t.ok():
                            statistics_done()
                        dve.bn_aggr(xag[:, 1 - t.p, :], stats[:, 1 - t.p, :]).then_inc(s_aggr, 1)
                    a = t + -1
                    if a.ok() and L1:
                        dve.wait_ge(s_ag2, a.of(lambda n: n + 1))
                        dve.tensor_scalar(yve[:, a.p:a.p + 1], yag[:, a.p, 1:2], EPS, None, ALU.add).then_inc(s_ve2, 1)
                    elif a.ok():
                        dve.wait_ge(s_ag2, a.of(lambda n: n + 1))
                        dve.tensor_scalar(hb[:, a.p, :], xt(a), yag[:, a.p, 0:1], None, ALU.subtract).then_inc(s_h, 1)
                        dve.tensor_copy(col(c["hstat"], a, 2), yag[:, a.p, :])
                        dve.wait_ge(s_h, a.of(lambda n: n + 1))
                        dve.tensor_reduce(col(c["hamax"], a), hb[:, a.p, :], AX.X, ALU.max,
                                          apply_absolute_value=True)
                    a = t + 5
                    if a.ok():
                        dve.wait_ge(s_aggr, a.of(lambda n: n + 1))
                        if L1:
                            dve.tensor_scalar(xve[:, a.p:a.p + 1], xag[:, a.p, 1:2], 1.0 + EPS, EPS * EPS, ALU.mult,
                                              ALU.add).then_inc(s_veps, 1)
                        else:
                            dve.tensor_scalar(xve[:, a.p:a.p + 1], xag[:, a.p, 1:2], EPS, None,
                                              ALU.add).then_inc(s_veps, 1)
                if not L1:
                    for b in range(B):
                        dve.wait_ge(c["s_x"][b], 16)
                pipeline(dve, body, FIRST, LAST, LO, HI)


def ffn(nc, sem, retired, sbuf, xs, c):
    NCH, CW = 8, 512
    TC = CW // P
    MF = FI // P
    NM = 2 * MF
    NU, UW = 24, 1024
    UC = NU // NCH
    QM = 32767.0
    U16S = 65536.0

    def s(n):
        return sem("f_" + n)
    s_w = [s(f"w{i}") for i in range(3)]
    s_wb, s_wT, s_wh, s_wl = s("wb"), s("wT"), s("wh"), s("wl")
    s_sc, s_loc, s_all = s("sc"), s("loc"), s("all")
    s_hb, s_hq, s_hf, s_hT, s_hh, s_hl = s("hb"), s("hq"), s("hf"), s("hT"), s("hh"), s("hl")
    s_mm, s_ev, s_am, s_uw = s("mm"), s("ev"), s("am"), s("uw")
    s_gq, s_sg, s_su, s_g2, s_am2 = s("gq"), s("sg"), s("su"), s("g2"), s("am2")
    s_ul, s_uq, s_g3, s_pr, s_am3 = [s("ul0"), s("ul1")], s("uq"), s("g3"), s("pr"), s("am3")
    s_oq, s_oh, s_ol, s_dn, s_x2 = s("oq"), s("oh"), s("ol"), s("dn"), s("x2")
    s_ln = s("ln")

    uscr = nc.dram_tensor("up_scratch", (NU, P, UW), F32, kind="Internal").ap()
    with ExitStack() as st:
        G = sbuf(st, "G", [P, NU * UW])
        dTh = sbuf(st, "dTh", [P, MF, D], F32R)
        dTl = sbuf(st, "dTl", [P, MF, D], F32R)
        sc = sbuf(st, "sc", [P, 24])
        loc = sbuf(st, "loc", [P, 4])
        allm = sbuf(st, "allm", [P, 4])
        amt = sbuf(st, "amt", [P, NCH * NM])
        am2 = sbuf(st, "am2", [P, NU])
        am3 = sbuf(st, "am3", [P, NU])
        u1 = ExitStack()
        wTh = sbuf(u1, "wTh", [P, 2, KT, FI], F32R)
        wTl = sbuf(u1, "wTl", [P, 2, KT, FI], F32R)
        ps = [st.enter_context(nc.psum_tensor(f"f_ps{i}", [P, 512], F32)) for i in range(8)]
        T, R, Y = ps[0:2], ps[2:6], ps[6:8]
        (sh, ih, sup, kup, sga, kga, ssl, ksl, spr, kpr, tmp, sps) = [sc[:, i:i + 1] for i in range(12)]

        with ExitStack() as sw:
            raw = [sbuf(sw, f"f_raw{i}", [P, 2 * FI]) for i in range(3)]
            wq = sbuf(sw, "f_wq", [P, 3, 2 * FI], I16)
            NB = 2 * FI // 32
            wa = sbuf(sw, "f_wa", [P, 3, NB])
            wr = sbuf(sw, "f_wr", [P, 3, NB])

            def blocks(n):
                i, m = n // 3, 2 * (n % 3)
                if i < 2:
                    return [raw[i][:, (m + a) * D + k * P:(m + a) * D + (k + 1) * P]
                            for k in range(KT) for a in range(2)]
                return [raw[2][:, o * FI + (m + a) * P:o * FI + (m + a + 1) * P] for a in range(2) for o in range(2)]

            def split(n, high):
                i, m = n // 3, 2 * (n % 3)
                if i < 2:
                    return (wTh if high else wTl)[:, i, :, m * P:(m + 2) * P]
                return (dTh if high else dTl)[:, m:m + 2, :]

            def bank(n):
                return R[n % 4][:].rearrange("p (k n) -> p k n", k=2)

            hstat = c["hstat"][:].rearrange("p (t c) -> p t c", c=2)
            with nc.Block() as block:
                @block.gpsimd
                def _(pool):
                    pool.wait_ge(s_ln, 1)
                    pool.tensor_tensor(c["hrstd"][:], c["hrstd"][:], c["mhalf"][:].broadcast_to([P, NT]),
                                       ALU.pow).then_inc(s_ln, 1)

                @block.sync
                def _(sp):
                    for i, n in enumerate(("L0_ffn_w_up", "L0_ffn_w_gate", "L0_ffn_w_down")):
                        v = c[n]
                        sp.dma_start(raw[i][:].rearrange("p (m n) -> p m n", n=v.shape[1]),
                                     v.rearrange("(m p) n -> p m n", p=P)).then_inc(s_w[i], 16)
                    retired.clear(sp)

                @block.vector
                def _(dve):
                    dve.tensor_scalar(c["hrstd"][:], hstat[:, :, 1], EPS, None, ALU.add).then_inc(s_ln, 1)
                    for i in range(3):
                        dve.wait_ge(s_w[i], 16)
                        blk = raw[i][:].rearrange("p (b k) -> p b k", k=32)
                        qb = wq[:, i, :].rearrange("p (b k) -> p b k", k=32)
                        dve.tensor_reduce(wa[:, i, :], blk, AX.X, ALU.max,
                                          apply_absolute_value=True).then_inc(s_wb, 1)
                        dve.wait_ge(s_wb, 5 * i + 1)
                        dve.tensor_scalar(wa[:, i, :], wa[:, i, :], 1.0 / 7.0, 1e-12, ALU.mult,
                                          ALU.max).then_inc(s_wb, 1)
                        dve.wait_ge(s_wb, 5 * i + 2)
                        dve.reciprocal(wr[:, i, :], wa[:, i, :]).then_inc(s_wb, 1)
                        dve.wait_ge(s_wb, 5 * i + 3)
                        dve.tensor_tensor(qb, blk, wr[:, i, :].unsqueeze(2).broadcast_to([P, NB, 32]),
                                          ALU.mult).then_inc(s_wb, 1)
                        dve.wait_ge(s_wb, 5 * i + 4)
                        dve.tensor_tensor(blk, qb, wa[:, i, :].unsqueeze(2).broadcast_to([P, NB, 32]),
                                          ALU.mult).then_inc(s_wb, 1)
                    for n in range(9):
                        dve.wait_ge(s_wh, n + 1)
                        dve.tensor_tensor(split(n, False), bank(n), split(n, True).bitcast(F32),
                                          ALU.subtract).then_inc(s_wl, 1)
                    dve.wait_ge(s_ln, 2)
                    dve.tensor_tensor(c["hamax"][:], c["hamax"][:], c["hrstd"][:], ALU.mult).then_inc(s_ln, 1)

                @block.tensor
                def _(pe):
                    for n in range(9):
                        pe.wait_ge(s_wb, 5 * (n // 3 + 1))
                        if n >= 4:
                            pe.wait_ge(s_wl, n - 3)
                        for j, src in enumerate(blocks(n)):
                            last = pe.transpose(R[n % 4][:, j * P:(j + 1) * P], src, c["ident"][:])
                        last.then_inc(s_wT, 1)

                @block.scalar
                def _(act):
                    for n in range(9):
                        act.wait_ge(s_wT, n + 1)
                        act.copy(split(n, True), bank(n)).then_inc(s_wh, 1)
        retired.stack.close()

        hb = sbuf(u1, "f_hb", [P, TC, D])
        hq = sbuf(u1, "f_hq", [P, TC, D], I16)
        hh = [sbuf(u1, f"f_hh{i}", [P, KT, CW], F32R) for i in range(2)]
        hl = [sbuf(u1, f"f_hl{i}", [P, KT, CW], F32R) for i in range(2)]
        ub = sbuf(u1, "f_ub", [P, MF, CW])
        u1.close()
        u2 = ExitStack()
        iq = [sbuf(u2, f"f_iq{i}", [P, UW], I16) for i in range(2)]
        sg = [sbuf(u2, f"f_sg{i}", [P, UW]) for i in range(2)]
        su = [sbuf(u2, f"f_su{i}", [P, UW], U16) for i in range(2)]
        ul = [sbuf(u2, f"f_ul{i}", [P, UW]) for i in range(2)]
        uq = [sbuf(u2, f"f_uq{i}", [P, UW], I16) for i in range(2)]
        u2.close()
        u3 = ExitStack()
        oh = [sbuf(u3, f"f_oh{i}", [P, UC, UW], F32R) for i in range(2)]
        ol = [sbuf(u3, f"f_ol{i}", [P, UC, UW], F32R) for i in range(2)]
        oq = [sbuf(u3, f"f_oq{i}", [P, UW], I16) for i in range(2)]
        u3.close()

        def unit(n):
            return G[:, bass.ds(n * UW, UW)]

        with nc.Block() as block:
            @block.vector
            def _(dve):
                k = 0
                dve.tensor_reduce(loc[:, 0:1], c["hamax"][:], AX.X, ALU.max).then_inc(s_loc, 1)
                dve.wait_ge(s_all, 1)
                dve.tensor_scalar(sh, allm[:, 0:1], 1.0 / QM, 1e-12, ALU.mult, ALU.max).then_inc(s_sc, 1)
                dve.wait_ge(s_sc, 1)
                dve.reciprocal(ih, sh).then_inc(s_sc, 1)
                dve.wait_ge(s_sc, 2)

                def body(t):
                    a = t + 2
                    if 0 <= a.t0 < NCH:
                        if a.t0 >= 1:
                            dve.wait_ge(s_hT, a.of(lambda n: n))
                        for j in range(TC):
                            n = a.n * TC + j
                            last = dve.tensor_scalar(hb[:, j, :], xs[:, bass.ds(n * D, D)],
                                                     c["hstat"][:, bass.ds(n * 2, 1)],
                                                     c["hrstd"][:, bass.ds(n, 1)], ALU.subtract, ALU.mult)
                        last.then_inc(s_hb, 1)
                        dve.wait_ge(s_hb, a.of(lambda n: n + 1))
                        dve.tensor_scalar(hq[:], hb[:], ih, None, ALU.mult).then_inc(s_hq, 1)
                    a = t + 1
                    if 0 <= a.t0 < NCH:
                        dve.wait_ge(s_hh, a.of(lambda n: 2 * n + 2))
                        if a.t0 >= 2:
                            dve.wait_ge(s_mm, a.of(lambda n: NM * (n - 1)))
                        for k in range(KT):
                            dve.tensor_tensor(hl[a.p][:, k, :], T[k][:], hh[a.p][:, k, :].bitcast(F32),
                                              ALU.subtract).then_inc(s_hl, 1)
                    if 0 <= t.t0 < NCH:
                        for m in range(NM):
                            dve.wait_ge(s_ev, t.of(lambda n: NM * n + m + 1))
                            src = ub[:, m, :] if m < MF else G[:, bass.ds((t.n * MF + m - MF) * CW, CW)]
                            dve.tensor_reduce(amt[:, bass.ds((t.n * NM + m), 1)], src, AX.X, ALU.max,
                                              apply_absolute_value=True).then_inc(s_am, 1)
                pipeline(dve, body, -2, NCH, 2, 5)
                dve.wait_ge(s_am, NCH * NM)
                v = amt[:].rearrange("p (c g m) -> p g c m", c=NCH, g=2)
                for g in range(2):
                    dve.tensor_reduce(loc[:, 1 + g:2 + g], v[:, g], AX.XY, ALU.max).then_inc(s_loc, 1)
                for g, (scale, factor) in enumerate(((sup, kup), (sga, kga))):
                    dve.wait_ge(s_all, 3)
                    n = 2 + 4 * g
                    dve.tensor_scalar(tmp, allm[:, 1 + g:2 + g], sh, 1.0 / QM, ALU.mult, ALU.mult).then_inc(s_sc, 1)
                    dve.wait_ge(s_sc, n + 1)
                    dve.tensor_scalar(scale, tmp, 1e-12, None, ALU.max).then_inc(s_sc, 1)
                    dve.wait_ge(s_sc, n + 2)
                    dve.reciprocal(tmp, scale).then_inc(s_sc, 1)
                    dve.wait_ge(s_sc, n + 3)
                    dve.tensor_tensor(factor, tmp, sh, ALU.mult).then_inc(s_sc, 1)
                    dve.wait_ge(s_sc, n + 4)

            @block.gpsimd
            def _(pool):
                pool.wait_ge(s_loc, 1)
                pool.partition_all_reduce(allm[:, 0:1], loc[:, 0:1], P, RMAX).then_inc(s_all, 1)
                pool.wait_ge(s_loc, 3)
                for g in (1, 2):
                    pool.partition_all_reduce(allm[:, g:g + 1], loc[:, g:g + 1], P, RMAX).then_inc(s_all, 1)

            @block.tensor
            def _(pe):
                def body(t):
                    a = t + 1
                    if 0 <= a.t0 < NCH:
                        pe.wait_ge(s_hf, a.of(lambda n: n + 1))
                        if a.t0 >= 1:
                            pe.wait_ge(s_hl, a.of(lambda n: 2 * n))
                        for k in range(KT):
                            for j in range(TC):
                                last = pe.transpose(T[k][:, j * P:(j + 1) * P], hb[:, j, k * P:(k + 1) * P],
                                                    c["ident"][:])
                        last.then_inc(s_hT, 1)
                    if 0 <= t.t0 < NCH:
                        pe.wait_ge(s_hh, t.of(lambda n: 2 * n + 2))
                        pe.wait_ge(s_hl, t.of(lambda n: 2 * n + 2))
                        for m in range(NM):
                            if m >= 4 or t.t0 >= 1:
                                pe.wait_ge(s_ev, t.of(lambda n: NM * n + m - 3))
                            g, mm = m // MF, m % MF
                            pairs = [(w, h) for w, h in ((wTh, hh), (wTh, hl), (wTl, hh))]
                            n = 0
                            for w_, h_ in pairs:
                                for k in range(KT):
                                    last = pe.matmul(R[m % 4][:], w_[:, g, k, mm * P:(mm + 1) * P], h_[t.p][:, k, :],
                                                     start=(n == 0), stop=(n == 3 * KT - 1))
                                    n += 1
                            last.then_inc(s_mm, 1)
                pipeline(pe, body, -1, NCH - 1, 2, 5)

            @block.scalar
            def _(act):
                def body(t):
                    a = t + 2
                    if 0 <= a.t0 < NCH:
                        act.wait_ge(s_hq, a.of(lambda n: n + 1))
                        act.copy(hb[:], hq[:]).then_inc(s_hf, 1)
                    a = t + 1
                    if 0 <= a.t0 < NCH:
                        act.wait_ge(s_hT, a.of(lambda n: n + 1))
                        if a.t0 >= 2:
                            act.wait_ge(s_mm, a.of(lambda n: NM * (n - 1)))
                        for k in range(KT):
                            act.copy(hh[a.p][:, k, :], T[k][:]).then_inc(s_hh, 1)
                    if 0 <= t.t0 < NCH:
                        for m in range(NM):
                            act.wait_ge(s_mm, t.of(lambda n: NM * n + m + 1))
                            if m == 0 and t.t0 >= 1:
                                act.wait_ge(s_uw, t.of(lambda n: 16 * n))
                                act.wait_ge(s_am, t.of(lambda n: NM * (n - 1) + MF))
                            dst = ub[:, m, :] if m < MF else G[:, bass.ds((t.n * MF + m - MF) * CW, CW)]
                            act.copy(dst, R[m % 4][:]).then_inc(s_ev, 1)
                pipeline(act, body, -2, NCH - 1, 2, 5)

            @block.sync
            def _(sp):
                with sp.Fori(0, NCH) as i:
                    sp.wait_ge(s_ev, i * NM + MF)
                    sp.dma_start(uscr[bass.ds(i * UC, UC)].rearrange("u p n -> p u n"),
                                 ub[:].rearrange("p m n -> p (m n)").rearrange("p (u n) -> p u n", n=UW)
                                 ).then_inc(s_uw, 16)
                sp.wait_ge(s_uw, 16 * NCH)

        with nc.Block() as block:
            @block.scalar
            def _(act):
                def gate(t):
                    if t.t0 >= 2:
                        act.wait_ge(s_g2, t.of(lambda n: n - 1))
                    act.activation(iq[t.p][:], unit(t.n), ACT.Copy, scale=kga).then_inc(s_gq, 1)
                    act.wait_ge(s_gq, t.of(lambda n: n + 1))
                    act.activation(sg[t.p][:], iq[t.p][:], ACT.Sigmoid, scale=sga).then_inc(s_sg, 1)
                pipeline(act, gate, 0, NU - 1, 2, NU - 1)
                act.wait_ge(s_sc, 13)

                def ints(t):
                    if t.t0 >= 2:
                        act.wait_ge(s_pr, t.of(lambda n: n - 1))
                    act.activation(iq[t.p][:], unit(t.n), ACT.Copy, scale=ksl).then_inc(s_g3, 1)
                    act.wait_ge(s_ul[t.p], t.of(lambda n: 16 * (n // 2 + 1)))
                    act.activation(uq[t.p][:], ul[t.p][:], ACT.Copy, scale=kup).then_inc(s_uq, 1)
                pipeline(act, ints, 0, NU - 1, 2, NU - 1)

            @block.sync
            def _(sp):
                def load(t):
                    if t.t0 >= 2:
                        sp.wait_ge(s_uq, t.of(lambda n: n - 1))
                    sp.dma_start(ul[t.p][:], uscr[bass.ds(t.n, 1)].rearrange("u p n -> p (u n)")
                                 ).then_inc(s_ul[t.p], 16)
                pipeline(sp, load, 0, NU - 1, 2, NU - 1)

            @block.gpsimd
            def _(pool):
                for k, n in ((3, 4), (0, 5)):
                    pool.wait_ge(s_loc, n)
                    pool.partition_all_reduce(allm[:, k:k + 1], loc[:, k:k + 1], P, RMAX).then_inc(s_all, 1)

            @block.vector
            def _(dve):
                def silu(t):
                    dve.wait_ge(s_sg, t.of(lambda n: n + 1))
                    dve.tensor_scalar(su[t.p][:], sg[t.p][:], U16S, U16S - 1, ALU.mult, ALU.min).then_inc(s_su, 1)
                    dve.wait_ge(s_su, t.of(lambda n: n + 1))
                    dve.scalar_tensor_tensor(unit(t.n), iq[t.p][:], sga, su[t.p][:], ALU.mult,
                                             ALU.mult).then_inc(s_g2, 1)
                    dve.wait_ge(s_g2, t.of(lambda n: n + 1))
                    dve.tensor_reduce(am2[:, bass.ds(t.n, 1)], unit(t.n), AX.X, ALU.max,
                                      apply_absolute_value=True).then_inc(s_am2, 1)
                pipeline(dve, silu, 0, NU - 1, 2, NU - 1)
                dve.wait_ge(s_am2, NU)
                dve.tensor_reduce(loc[:, 3:4], am2[:], AX.X, ALU.max).then_inc(s_loc, 1)
                dve.wait_ge(s_all, 4)
                dve.tensor_scalar(tmp, allm[:, 3:4], 1.0 / U16S, 1.0 / QM, ALU.mult, ALU.mult).then_inc(s_sc, 1)
                dve.wait_ge(s_sc, 11)
                dve.tensor_scalar(ssl, tmp, 1e-12, None, ALU.max).then_inc(s_sc, 1)
                dve.wait_ge(s_sc, 12)
                dve.reciprocal(sps, ssl).then_inc(s_su, 1)
                dve.wait_ge(s_su, NU + 1)
                dve.tensor_scalar(ksl, sps, 1.0 / U16S, None, ALU.mult).then_inc(s_sc, 1)

                def product(t):
                    dve.wait_ge(s_g3, t.of(lambda n: n + 1))
                    dve.wait_ge(s_uq, t.of(lambda n: n + 1))
                    dve.tensor_tensor(unit(t.n), iq[t.p][:], uq[t.p][:], ALU.mult).then_inc(s_pr, 1)
                    dve.wait_ge(s_pr, t.of(lambda n: n + 1))
                    dve.tensor_reduce(am3[:, bass.ds(t.n, 1)], unit(t.n), AX.X, ALU.max,
                                      apply_absolute_value=True).then_inc(s_am3, 1)
                pipeline(dve, product, 0, NU - 1, 2, NU - 1)
                dve.wait_ge(s_am3, NU)
                dve.tensor_reduce(loc[:, 0:1], am3[:], AX.X, ALU.max).then_inc(s_loc, 1)
                dve.tensor_tensor(sps, ssl, sup, ALU.mult).then_inc(s_sc, 1)
                dve.wait_ge(s_sc, 14)
                dve.wait_ge(s_all, 5)
                dve.tensor_scalar(tmp, allm[:, 0:1], sps, 1.0 / QM, ALU.mult, ALU.mult).then_inc(s_sc, 1)
                dve.wait_ge(s_sc, 15)
                dve.tensor_scalar(spr, tmp, 1e-12, None, ALU.max).then_inc(s_sc, 1)
                dve.wait_ge(s_sc, 16)
                dve.reciprocal(tmp, spr).then_inc(s_sc, 1)
                dve.wait_ge(s_sc, 17)
                dve.tensor_tensor(kpr, tmp, sps, ALU.mult).then_inc(s_sc, 1)

        with nc.Block() as block:
            @block.vector
            def _(dve):
                def body(t):
                    a = t + 1
                    if 0 <= a.t0 < NCH:
                        for k in range(UC):
                            dve.wait_ge(s_oq, a.of(lambda n: UC * n + k + 1))
                            dve.wait_ge(s_oh, a.of(lambda n: UC * n + k + 1))
                            if a.t0 >= 2 and k == 0:
                                dve.wait_ge(s_dn, a.of(lambda n: TC * (n - 1)))
                            dve.tensor_tensor(ol[a.p][:, k, :], oq[(k + a.t0) % 2][:], oh[a.p][:, k, :].bitcast(F32),
                                              ALU.subtract).then_inc(s_ol, 1)
                    if 0 <= t.t0 < NCH:
                        for j in range(TC):
                            dve.wait_ge(s_dn, t.of(lambda n: TC * n + j + 1))
                            xv = xs[:, bass.ds((t.n * TC + j) * D, D)]
                            dve.scalar_tensor_tensor(xv, Y[j % 2][:, 0:D], spr, xv, ALU.mult,
                                                     ALU.add).then_inc(s_x2, 1)
                pipeline(dve, body, -1, NCH - 1, 2, 5)

            @block.scalar
            def _(act):
                def body(t):
                    for k in range(UC):
                        if t.t0 * UC + k >= 2:
                            act.wait_ge(s_ol, t.of(lambda n: UC * n + k - 1))
                        q = oq[(k + t.t0) % 2]
                        act.activation(q[:], unit(t.n * UC + k), ACT.Copy, scale=kpr).then_inc(s_oq, 1)
                        act.wait_ge(s_oq, t.of(lambda n: UC * n + k + 1))
                        if t.t0 >= 2 and k == 0:
                            act.wait_ge(s_dn, t.of(lambda n: TC * (n - 1)))
                        act.copy(oh[t.p][:, k, :], q[:]).then_inc(s_oh, 1)
                pipeline(act, body, 0, NCH - 1, 2, 5)

            @block.tensor
            def _(pe):
                def body(t):
                    for j in range(TC):
                        if t.t0 * TC + j >= 2:
                            pe.wait_ge(s_x2, t.of(lambda n: TC * n + j - 1))
                        if j == 0:
                            pe.wait_ge(s_oh, t.of(lambda n: UC * (n + 1)))
                            pe.wait_ge(s_ol, t.of(lambda n: UC * (n + 1)))
                        n = 0
                        for o_, w_ in ((oh, dTh), (ol, dTh), (oh, dTl)):
                            for k in range(MF):
                                lhs = o_[t.p][:, k // 2, (k % 2) * CW + j * P:(k % 2) * CW + (j + 1) * P]
                                last = pe.matmul(Y[j % 2][:, 0:D], lhs, w_[:, k, :], start=(n == 0),
                                                 stop=(n == 3 * MF - 1))
                                n += 1
                        last.then_inc(s_dn, 1)
                pipeline(pe, body, 0, NCH - 1, 2, 5)


def moe(nc, stack, sem, sbuf, xs, xt, col, c, out):
    def s(name):
        return sem("m_" + name)
    NB = NE // 2
    EW = NE * D
    NA = 5
    s_w, s_wT, s_wh, s_wl, s_c = s("w"), s("wT"), s("wh"), s("wl"), s("c")
    s_stat, s_aggr, s_veps, s_rstd, s_xn = s("stat"), s("aggr"), s("veps"), s("rstd"), s("xn")
    s_xT, s_xh, s_xl, s_lg, s_E = s("xT"), s("xh"), s("xl"), s("lg"), s("E")
    s_l, s_top, s_idx, s_fi, s_sel, s_sh, s_ex = s("l"), s("top"), s("idx"), s("fi"), s("sel"), s("sh"), s("ex")
    s_r, s_g, s_gT, s_gTe, s_bias, s_acc = s("r"), s("g"), s("gT"), s("gTe"), s("bias"), s("acc")
    s_out, s_m1, s_sc, s_h1, s_half, s_done = s("out"), s("m1"), s("sc"), s("h1"), s("half"), s("done")

    with ExitStack() as st:
        wh = sbuf(st, "m_wh", [P, KT, EW + NE], F32R)
        wl = sbuf(st, "m_wl", [P, KT, EW + NE], F32R)
        be = sbuf(st, "m_be", [NE, D])
        bg = sbuf(st, "m_bg", [P, NE])
        iota = sbuf(st, "m_iota", [P, NE])
        ps = [st.enter_context(nc.psum_tensor(f"m_ps{i}", [P, 512], F32)) for i in range(8)]
        X, T, GL, GT, BO = ps[0:4], ps[4], ps[5], ps[6], ps[7]
        with ExitStack() as sw:
            raw = sbuf(sw, "m_raw", [P, NE, 2, D])
            rg = sbuf(sw, "m_rg", [NE, D])

            def bank(n):
                return ps[n % 4][:].rearrange("p (k o) -> p k o", k=KT)[:, :, 0:D if n < NE else NE]

            def part(w_, n):
                return w_[:, :, n * D:(n + 1) * D] if n < NE else w_[:, :, EW:EW + NE]

            with nc.Block() as block:
                @block.sync
                def _(sp):
                    for h in range(2):
                        sp.dma_start(raw[:, 4 * h:4 * h + 4].rearrange("p e m d -> p (e m) d"),
                                     c["L1_ffn_W"][4 * h:4 * h + 4].rearrange("e (m p) d -> p (e m) d", p=P)
                                     ).then_inc(s_w, 16)
                    sp.dma_start(rg[:], c["L1_ffn_Wg"]).then_inc(s_w, 16)
                    sp.dma_start(be[:], c["L1_ffn_b"]).then_inc(s_c, 16)
                    sp.dma_start(bg[:], c["L1_ffn_bg"].partition_broadcast(P)).then_inc(s_c, 16)

                @block.gpsimd
                def _(pool):
                    for e in range(NE):
                        pool.memset(iota[:, e:e + 1], float(e)).then_inc(s_c, 1)

                @block.tensor
                def _(pe):
                    pe.wait_ge(s_w, 48)
                    for n in range(NE + 1):
                        if n >= 4:
                            pe.wait_ge(s_wl, n - 3)
                        for k in range(KT):
                            if n < NE:
                                for m in range(2):
                                    last = pe.transpose(ps[n % 4][:, k * D + m * P:k * D + (m + 1) * P],
                                                        raw[:, n, m, k * P:(k + 1) * P], c["ident"][:])
                            else:
                                last = pe.transpose(ps[n % 4][:, k * D:k * D + NE], rg[:, k * P:(k + 1) * P],
                                                    c["ident"][0:NE, 0:NE])
                        last.then_inc(s_wT, 1)

                @block.scalar
                def _(act):
                    for n in range(NE + 1):
                        act.wait_ge(s_wT, n + 1)
                        act.copy(part(wh, n), bank(n)).then_inc(s_wh, 1)

                @block.vector
                def _(dve):
                    for n in range(NE + 1):
                        dve.wait_ge(s_wh, n + 1)
                        dve.tensor_tensor(part(wl, n), bank(n), part(wh, n).bitcast(F32),
                                          ALU.subtract).then_inc(s_wl, 1)

        stats = sbuf(st, "m_stats", [P, 2, 6])
        ag = sbuf(st, "m_ag", [P, 2, 2])
        ve = sbuf(st, "m_ve", [P, 2])
        rstd = sbuf(st, "m_rstd", [P, 2])
        xn = [sbuf(st, f"m_xn{i}", [P, D]) for i in range(2)]
        xh = [sbuf(st, f"m_xh{i}", [P, KT, P], F32R) for i in range(2)]
        xl = [sbuf(st, f"m_xl{i}", [P, KT, P], F32R) for i in range(2)]
        lg = [sbuf(st, f"m_lg{i}", [P, NE]) for i in range(2)]
        ls = [sbuf(st, f"m_ls{i}", [P, NE]) for i in range(2)]
        ex = [sbuf(st, f"m_ex{i}", [P, NE]) for i in range(2)]
        m1 = [sbuf(st, f"m_max{i}", [P, 1]) for i in range(2)]
        top = [sbuf(st, f"m_top{i}", [P, NE]) for i in range(2)]
        idx = [sbuf(st, f"m_idx{i}", [P, NE], U16) for i in range(2)]
        fi = [sbuf(st, f"m_fi{i}", [P, 2]) for i in range(2)]
        sel = [sbuf(st, f"m_sel{i}", [P, 2, NE]) for i in range(2)]
        es = [sbuf(st, f"m_es{i}", [P, 1]) for i in range(2)]
        rs = [sbuf(st, f"m_rs{i}", [P, 1]) for i in range(2)]
        g = [sbuf(st, f"m_g{i}", [P, NE]) for i in range(2)]
        gT = [sbuf(st, f"m_gT{i}", [NE, P]) for i in range(2)]
        half = [sbuf(st, f"m_half{i}", [P, 4, D]) for i in range(2)]
        FIRST, LAST, LO, HI = -4, NT, 4, 27

        def product(pe, a, o_, cols):
            n = 0
            for x_, w_ in ((xh, wh), (xl, wh), (xh, wl)):
                for k in range(KT):
                    last = pe.matmul(o_, x_[a.p][:, k, :], w_[:, k, cols], start=(n == 0), stop=(n == 3 * KT - 1))
                    n += 1
            return last

        with nc.Block() as block:
            @block.tensor
            def _(pe):
                def body(t):
                    if t.ok():
                        pe.wait_ge(s_gTe, t.of(lambda n: n + 1))
                        if t.t0 >= 1:
                            pe.wait_ge(s_acc, t.of(lambda n: NA * (n - 1) + 1))
                        pe.matmul(BO[:, 0:D], gT[t.p][:], be[:], start=True, stop=True).then_inc(s_bias, 1)
                    a = t + 1
                    if a.ok():
                        pe.wait_ge(s_xl, a.of(lambda n: n + 1))
                        if a.t0 >= 1:
                            pe.wait_ge(s_l, a.of(lambda n: n))
                        product(pe, a, GL[:, 0:NE], slice(EW, EW + NE)).then_inc(s_lg, 1)

                    def experts(q):
                        if t.t0 >= 1 and q < 2:
                            pe.wait_ge(s_acc, t.of(lambda n: NA * (n - 1) + 2 * q + 3))
                        elif t.t0 >= 1:
                            pe.wait_ge(s_sc, t.of(lambda n: 4 * (n - 1) + 2 * q - 2))
                        product(pe, t, X[q][:], slice(q * 2 * D, (q + 1) * 2 * D)).then_inc(s_E, 1)
                    if t.ok():
                        experts(0)
                        experts(1)
                    a = t + 2
                    if a.ok():
                        pe.wait_ge(s_xn, a.of(lambda n: n + 1))
                        if a.t0 >= 1:
                            pe.wait_ge(s_xl, a.of(lambda n: n))
                        for k in range(KT):
                            last = pe.transpose(T[:, k * P:(k + 1) * P], xn[a.p][:, k * P:(k + 1) * P], c["ident"][:])
                        last.then_inc(s_xT, 1)
                    if t.ok():
                        experts(2)
                        experts(3)
                    a = t + 1
                    if a.ok():
                        pe.wait_ge(s_g, a.of(lambda n: n + 1))
                        if a.t0 >= 1:
                            pe.wait_ge(s_gTe, a.of(lambda n: n))
                        pe.transpose(GT[0:NE, 0:P], g[a.p][:], c["ident"][:]).then_inc(s_gT, 1)
                pipeline(pe, body, FIRST, LAST, LO, HI)

            @block.scalar
            def _(act):
                def body(t):
                    a = t + 1
                    if a.ok():
                        act.wait_ge(s_sh, a.of(lambda n: n + 1))
                        act.activation(ex[a.p][:], ls[a.p][:], ACT.Exp, accum_out=es[a.p][:]).then_inc(s_ex, 1)
                    a = t + 2
                    if a.ok():
                        act.wait_ge(s_xT, a.of(lambda n: n + 1))
                        if a.t0 >= 2:
                            act.wait_ge(s_E, a.of(lambda n: NB * (n - 1)))
                        act.copy(xh[a.p][:].rearrange("p k n -> p (k n)"), T[:, 0:D]).then_inc(s_xh, 1)
                    a = t + 1
                    if a.ok():
                        act.wait_ge(s_gT, a.of(lambda n: n + 1))
                        if a.t0 >= 2:
                            act.wait_ge(s_bias, a.of(lambda n: n - 1))
                        act.copy(gT[a.p][:], GT[0:NE, 0:P]).then_inc(s_gTe, 1)
                    if t.ok():
                        if t.t0 >= 2:
                            act.wait_ge(s_done, t.of(lambda n: n - 1))
                        for e in range(4):
                            act.wait_ge(s_E, t.of(lambda n: NB * n + 3 + e // 2))
                            act.activation(half[t.p][:, e, :], X[2 + e // 2][:, (e % 2) * D:(e % 2 + 1) * D], ACT.Copy,
                                           scale=g[t.p][:, 4 + e:5 + e]).then_inc(s_sc, 1)
                pipeline(act, body, FIRST, LAST, LO, HI)

            @block.gpsimd
            def _(pool):
                def body(t):
                    if t.ok():
                        pool.wait_ge(s_sc, t.of(lambda n: 4 * n + 4))
                        pool.tensor_tensor(half[t.p][:, 0:2, :], half[t.p][:, 0:2, :], half[t.p][:, 2:4, :],
                                           ALU.add).then_inc(s_h1, 1)
                        pool.wait_ge(s_h1, t.of(lambda n: n + 1))
                        pool.tensor_tensor(half[t.p][:, 0, :], half[t.p][:, 0, :], half[t.p][:, 1, :],
                                           ALU.add).then_inc(s_half, 1)
                    a = t + 4
                    if a.ok():
                        pool.wait_ge(s_veps, a.of(lambda n: n + 1))
                        pool.tensor_tensor(rstd[:, a.p:a.p + 1], ve[:, a.p:a.p + 1], c["mhalf"][:],
                                           ALU.pow).then_inc(s_rstd, 1)
                pipeline(pool, body, FIRST, LAST, LO, HI)

            @block.sync
            def _(sp):
                with sp.Fori(0, NT // TPB) as b:
                    sp.wait_ge(s_done, b * TPB + TPB)
                    sp.dma_start(out.rearrange("b (t p) d -> b p t d", p=P)[bass.ds(b, 1)]
                                 .rearrange("b p t d -> p (b t) d"),
                                 xs[:, bass.ds(b * (TPB * D), TPB * D)].rearrange("p (t d) -> p t d", d=D)
                                 ).then_inc(s_out, 16)
                sp.wait_ge(s_out, 16 * B)

            @block.vector
            def _(dve):
                dve.wait_ge(s_c, 32 + NE)

                def body(t):
                    a = t + 1
                    if a.ok():
                        p = a.p
                        one = a.of(lambda n: n + 1)
                        dve.wait_ge(s_lg, one)
                        if a.t0 >= 2:
                            dve.wait_ge(s_gT, a.of(lambda n: n - 1))
                        dve.tensor_tensor(lg[p][:], GL[:, 0:NE], bg[:], ALU.add).then_inc(s_l, 1)
                        dve.wait_ge(s_l, one)
                        dve.tensor_reduce(m1[p][:], lg[p][:], AX.X, ALU.max).then_inc(s_m1, 1)
                        dve.max(top[p][:], lg[p][:]).then_inc(s_top, 1)
                        dve.wait_ge(s_m1, one)
                        dve.wait_ge(s_top, one)
                        dve.tensor_scalar(ls[p][:], lg[p][:], m1[p][:, 0:1], None, ALU.subtract).then_inc(s_sh, 1)
                        dve.max_index(idx[p][:], top[p][:], lg[p][:]).then_inc(s_idx, 1)
                        dve.wait_ge(s_idx, one)
                        dve.tensor_copy(fi[p][:], idx[p][:, 0:2]).then_inc(s_fi, 1)
                        dve.wait_ge(s_fi, one)
                        dve.tensor_scalar(sel[p][:, 0, :], iota[:], fi[p][:, 0:1], None, ALU.is_equal).then_inc(s_sel, 1)
                        dve.wait_ge(s_sel, a.of(lambda n: 2 * n + 1))
                        dve.scalar_tensor_tensor(sel[p][:, 1, :], iota[:], fi[p][:, 1:2], sel[p][:, 0, :],
                                                 ALU.is_equal, ALU.add).then_inc(s_sel, 1)
                        dve.wait_ge(s_ex, one)
                        dve.reciprocal(rs[p][:], es[p][:]).then_inc(s_r, 1)
                        dve.wait_ge(s_r, one)
                        dve.wait_ge(s_sel, a.of(lambda n: 2 * n + 2))
                        dve.scalar_tensor_tensor(g[p][:], ex[p][:], rs[p][:, 0:1], sel[p][:, 1, :], ALU.mult,
                                                 ALU.mult).then_inc(s_g, 1)

                    def add(e):
                        dve.wait_ge(s_E, t.of(lambda n: NB * n + e // 2 + 1))
                        dve.wait_ge(s_acc, t.of(lambda n: NA * n + e + 1))
                        dve.scalar_tensor_tensor(xt(t), X[e // 2][:, (e % 2) * D:(e % 2 + 1) * D],
                                                 g[t.p][:, e:e + 1], xt(t), ALU.mult, ALU.add).then_inc(s_acc, 1)
                    if t.ok():
                        dve.wait_ge(s_bias, t.of(lambda n: n + 1))
                        dve.tensor_tensor(xt(t), BO[:, 0:D], xt(t), ALU.add).then_inc(s_acc, 1)
                        for e in range(4):
                            add(e)
                    a = t + 2
                    if a.ok():
                        dve.wait_ge(s_xh, a.of(lambda n: n + 1))
                        if a.t0 >= 2:
                            dve.wait_ge(s_E, a.of(lambda n: NB * (n - 1)))
                        dve.tensor_tensor(xl[a.p][:].rearrange("p k n -> p (k n)"), T[:, 0:D],
                                          xh[a.p][:].rearrange("p k n -> p (k n)").bitcast(F32),
                                          ALU.subtract).then_inc(s_xl, 1)
                    a = t + -1
                    if a.ok():
                        dve.wait_ge(s_acc, a.of(lambda n: NA * (n + 1)))
                        dve.wait_ge(s_half, a.of(lambda n: n + 1))
                        dve.tensor_tensor(xt(a), half[a.p][:, 0, :], xt(a), ALU.add).then_inc(s_done, 1)
                    a, b = t + 4, t + 3
                    if a.ok():
                        dve.bn_stats(stats[:, a.p, :], xt(a)).then_inc(s_stat, 1)
                        dve.wait_ge(s_stat, a.of(lambda n: n + 1))
                    if b.ok():
                        dve.wait_ge(s_rstd, b.of(lambda n: n + 1))
                        if b.t0 >= 2:
                            dve.wait_ge(s_xT, b.of(lambda n: n - 1))
                        dve.tensor_scalar(xn[b.p][:], xt(b), ag[:, b.p, 0:1], rstd[:, b.p:b.p + 1],
                                          ALU.subtract, ALU.mult).then_inc(s_xn, 1)
                    if a.ok():
                        dve.bn_aggr(ag[:, a.p, :], stats[:, a.p, :]).then_inc(s_aggr, 1)
                        dve.wait_ge(s_aggr, a.of(lambda n: n + 1))
                        dve.tensor_scalar(ve[:, a.p:a.p + 1], ag[:, a.p, 1:2], EPS, None, ALU.add).then_inc(s_veps, 1)
                pipeline(dve, body, FIRST, LAST, LO, HI)



_INS = ["x", "ctx_768", "mask_BxS2_bf1", "L0_xattn_Wq", "L0_xattn_bq", "L0_xattn_Wk", "L0_xattn_bk",
        "L0_xattn_Wv", "L0_xattn_bv", "L0_xattn_Wo", "L0_xattn_bo", "L0_ffn_w_gate", "L0_ffn_w_up",
        "L0_ffn_w_down", "L1_xattn_g_norm", "L1_xattn_null_kv", "L1_xattn_Wq", "L1_xattn_Wkv",
        "L1_xattn_Wout", "L1_xattn_g_out", "L1_ffn_W", "L1_ffn_b", "L1_ffn_Wg", "L1_ffn_bg"]


def kernel(**inputs):
    import numpy as np
    import concourse.bacc as bacc
    from concourse.bass_utils import run_bass_kernel_spmd

    nc = bacc.Bacc("TRN2", target_bir_lowering=False, num_devices=1)
    arrays, aps = {}, {}
    for name in _INS:
        a = np.ascontiguousarray(inputs[name])
        if a.dtype == np.bool_:
            a = a.view(np.uint8)
        arrays[f"in_{name}"] = a
        aps[name] = nc.dram_tensor(f"in_{name}", a.shape, mybir.dt.from_np(a.dtype), kind="ExternalInput").ap()
    out = nc.dram_tensor("out", (B, SEQ, D), F32, kind="ExternalOutput").ap()
    w = {n.replace("L0_xattn_", ""): aps[n] for n in _INS if n.startswith("L0_xattn_")}
    w.update({n: aps[n] for n in _INS})
    program(nc, aps["x"], aps["ctx_768"], aps["mask_BxS2_bf1"], w, out)
    r = run_bass_kernel_spmd(nc, [arrays], core_ids=[0])
    return r.results[0]["out"]
```

```python
from contextlib import ExitStack

import concourse.bass as bass
from concourse import mybir
from concourse.alu_op_type import AluOpType as ALU

F32 = mybir.dt.float32
F32R = mybir.dt.float32r
I16 = mybir.dt.int16
U16 = mybir.dt.uint16
U8 = mybir.dt.uint8
ACT = mybir.ActivationFunctionType
AX = mybir.AxisListType
RMAX = bass.bass_isa.ReduceOp.max

P = 128
B, SEQ, D = 4, 1024, 256
NKEY, CD = 77, 192
H = 16
NT = B * SEQ // P
TPB = SEQ // P
KT = D // P
CK = CD // 96
CP = CD // CK
KP = 80
QW = 4 * KP
SW = H * KP
NJ = SW // P
HJ = NJ // 2
D0 = D // H
D1 = 64
CLAMP = 10000.0
EPS = 1e-5
FI = 768
NE = 8


def tile_heads(j):
    a = P * (j % HJ)
    return a // KP, (a + P - 1) // KP - a // KP + 1


def first_slot(j):
    return sum(tile_heads(k)[1] for k in range(j))


NSLOT = first_slot(NJ)


class At:

    def __init__(self, t0, i=None):
        self.t0, self.i = t0, i

    def __add__(self, k):
        return At(self.t0 + k, self.i)

    def of(self, f):
        if self.i is None:
            return f(self.t0)
        return self.i * (f(self.t0 + 2) - f(self.t0)) + f(self.t0)

    @property
    def n(self):
        return self.t0 if self.i is None else self.i * 2 + self.t0

    @property
    def batch(self):
        return self.n // TPB

    @property
    def p(self):
        return self.t0 % 2

    def ok(self):
        return 0 <= self.t0 < NT


def pipeline(eng, body, first, last, lo, hi):
    for t in range(first, lo):
        body(At(t))
    with eng.Fori(0, (hi - lo + 1) // 2) as i:
        body(At(lo, i))
        body(At(lo + 1, i))
    for t in range(hi + 1, last + 1):
        body(At(t))


class Slots:

    def __init__(self, order, place):
        self.banks, self.last, held = {}, {}, {}
        for n, x in enumerate(order):
            b = place(n, x[0], x[2])
            self.banks[x], self.last[x] = b, held.get(b)
            held[b] = x

    def bank(self, kind, t, k=0):
        return self.banks[kind, t.t0, k]

    def before(self, kind, t, k=0):
        last = self.last[kind, t.t0, k]
        return last and (last[0], t + (last[1] - t.t0), last[2])


def program(nc, x, ctx_kv, mask, w, out):
    stack = ExitStack()
    with stack:
        _program(nc, stack, x, ctx_kv, mask, w, out)


class Sems:

    def __init__(self, nc):
        self.nc, self.stack, self.nums = nc, ExitStack(), []

    def __call__(self, name):
        handle = self.stack.enter_context(self.nc.semaphore(name))
        self.nums.append(handle.num)
        return handle

    def clear(self, eng):
        nums = sorted(self.nums)
        while nums:
            n = 1
            while n < len(nums) and nums[n] == nums[0] + n:
                n += 1
            eng.sem_clear(range(nums[0], nums[0] + n))
            nums = nums[n:]


def _program(nc, stack, x, ctx_kv, mask, w, out):
    sem = Sems(nc)

    def sbuf(st, name, shape, dt=F32):
        return st.enter_context(nc.sbuf_tensor(name, shape, dt))

    xs = sbuf(stack, "xs", [P, NT * D])
    ident = sbuf(stack, "ident", [P, P])
    mhalf = sbuf(stack, "mhalf", [P, 1])
    hmean = sbuf(stack, "hmean", [P, NT])
    hrstd = sbuf(stack, "hrstd", [P, NT])
    hamax = sbuf(stack, "hamax", [P, NT])
    psel = sbuf(stack, "psel", [P, 2, HJ, 3])
    cscr = nc.dram_tensor("context_scratch", (CP, CK * B * KP), F32, kind="Internal").ap()

    def xt(t):
        return xs[:, bass.ds(t.n * D, D)] if t.i is not None else xs[:, t.t0 * D:(t.t0 + 1) * D]

    def col(a, t, n=1):
        return a[:, bass.ds(t.n * n, n)] if t.i is not None else a[:, t.t0 * n:t.t0 * n + n]

    prep, until_ffn = ExitStack(), ExitStack()
    s_id = sem("s_id")
    ffnw = FfnWeights(nc, until_ffn, prep, sem, sbuf, ident)
    fw = dict(wTh=ffnw.wTh, wTl=ffnw.wTl, dTh=ffnw.dTh, dTl=ffnw.dTl)
    att0 = ExitStack()
    wq0 = sbuf(att0, "wq0", [P, KT, D])
    wo0 = sbuf(att0, "wo0", [P, KT, D])
    bq0 = sbuf(att0, "bq0", [P, KT])
    bo0 = sbuf(att0, "bo0", [P, D])
    keys0 = sbuf(att0, "keys0", [P, B, KT, 8, KP])
    vals0 = sbuf(att0, "vals0", [P, B, NSLOT, D0 + 1])

    s_x = [sem(f"s_x{b}") for b in range(B)]
    s_small = sem("s_small")
    s_ctx = sem("s_ctx")
    s_tbl = sem("s_tbl")
    s_cT = sem("s_cT")
    s_cTe = sem("s_cTe")
    s_k0 = sem("s_k0")
    s_k0e = sem("s_k0e")
    s_v0 = sem("s_v0")
    s_v0e = sem("s_v0e")

    with prep as st:
        ffnw.scratch()
        ctx = sbuf(st, "ctx", [NKEY, B, CD])
        ctxT = sbuf(st, "ctxT", [CP, CK, B, KP])
        ctx3 = sbuf(st, "ctx3", [CP, CK, B, 3, KP])
        wk0 = sbuf(st, "wk0", [CP, CK, D])
        wv0 = sbuf(st, "wv0", [CP, CK, D])
        bk0 = sbuf(st, "bk0", [P, KT])
        bv0 = sbuf(st, "bv0", [P, D])
        bvs = sbuf(st, "bvs", [P, NSLOT, D0])
        sels = sbuf(st, "sels", [P, NSLOT])
        hsel = sbuf(st, "hsel", [P, 8])
        kT = sbuf(st, "kT", [P, KT, B, KP])
        pb = [st.enter_context(nc.psum_tensor(f"prep{i}", [P, 512], F32)) for i in range(4)]

        with nc.Block() as block:
            @block.sync
            def _(sp):
                sp.dma_start(ctx[:], ctx_kv.rearrange("b k c -> k b c")).then_inc(s_ctx, 16)
                sp.dma_start(wk0[:], w["Wk"].rearrange("(k p) n -> p k n", p=CP)).then_inc(s_ctx, 16)
                sp.dma_start(wv0[:], w["Wv"].rearrange("(k p) n -> p k n", p=CP)).then_inc(s_ctx, 16)
                sp.dma_start(bk0[:], w["bk"].rearrange("(k p) -> p k", p=P), allow_slow_non_contiguous=True).then_inc(s_ctx, 16)
                sp.dma_start(bv0[:], w["bv"].partition_broadcast(P)).then_inc(s_ctx, 16)
                ffnw.load(sp, w)
                for b in range(B):
                    sp.dma_start(xs[:, b * TPB * D:(b + 1) * TPB * D].rearrange("p (t d) -> p t d", d=D),
                                 x[b].rearrange("(t p) d -> p t d", p=P)).then_inc(s_x[b], 16)
                sp.wait_ge(s_cTe, 4)
                sp.dma_start(cscr, ctxT[:].rearrange("p c b k -> p (c b k)")).then_inc(s_ctx, 16)
                sp.wait_ge(s_ctx, 96)

            @block.scalar
            def _(act):
                act.dma_start(wq0[:], w["Wq"].rearrange("(k p) n -> p k n", p=P)).then_inc(s_small, 16)
                act.dma_start(wo0[:], w["Wo"].rearrange("(k p) n -> p k n", p=P)).then_inc(s_small, 16)
                act.dma_start(bq0[:], w["bq"].rearrange("(k p) -> p k", p=P), allow_slow_non_contiguous=True).then_inc(s_small, 16)
                act.dma_start(bo0[:], w["bo"].partition_broadcast(P)).then_inc(s_small, 16)
                act.wait_ge(s_small, 64)
                act.mul(bq0[:], bq0[:], D0 ** -0.5).then_inc(s_tbl, 1)
                ffnw.to_float(act)
                ffnw.high(act)

            @block.gpsimd
            def _(pool):
                pool.memset(ident[:], 0.0).then_inc(s_id, 1)
                pool.memset(mhalf[:], -0.5).then_inc(s_id, 1)
                pool.memset(hsel[:], 1.0).then_inc(s_id, 1)
                pool.memset(psel[:], 1.0).then_inc(s_id, 1)
                pool.wait_ge(s_id, 4)
                pool.affine_select(out=ident[:], in_=ident[:], compare_op=ALU.not_equal, fill=1.0, base=0,
                                   pattern=[[-1, P]], channel_multiplier=1).then_inc(s_id, 1)
                pool.affine_select(out=hsel[:], in_=hsel[:], compare_op=ALU.is_ge, fill=0.0, base=0,
                                   pattern=[[-D0, 8]], channel_multiplier=1).then_inc(s_id, 1)
                pool.wait_ge(s_id, 6)
                pool.affine_select(out=hsel[:], in_=hsel[:], compare_op=ALU.is_ge, fill=0.0, base=D0 - 1,
                                   pattern=[[D0, 8]], channel_multiplier=-1).then_inc(s_id, 1)
                n = 7
                for v in range(2):
                    for jj in range(HJ):
                        h0, nh = tile_heads(jj)
                        pool.affine_select(out=psel[:, v, jj, :], in_=psel[:, v, jj, :], compare_op=ALU.is_ge,
                                           fill=0.0, base=P * jj - KP * h0, pattern=[[-KP, 3]],
                                           channel_multiplier=1).then_inc(s_id, 1)
                        n += 1
                        pool.wait_ge(s_id, n)
                        pool.affine_select(out=psel[:, v, jj, :], in_=psel[:, v, jj, :], compare_op=ALU.is_ge,
                                           fill=0.0, base=NKEY + v - 1 - P * jj + KP * h0, pattern=[[KP, 3]],
                                           channel_multiplier=-1).then_inc(s_id, 1)
                        n += 1
                ffnw.dequantise(pool)

            @block.tensor
            def _(pe):
                pe.wait_ge(s_ctx, 80)
                pe.wait_ge(s_id, 5)
                for k in range(CK):
                    for b in range(B):
                        last = pe.transpose(pb[k][0:CP, b * KP:b * KP + NKEY], ctx[:, b, k * CP:(k + 1) * CP],
                                            ident[0:NKEY, 0:NKEY])
                    last.then_inc(s_cT, 1)
                pe.wait_ge(s_cTe, 5)
                for m in range(KT):
                    for k in range(CK):
                        last = pe.matmul(pb[2 + m][:, 0:B * KP], wk0[:, k, m * P:(m + 1) * P], ctxT[:, k, :, :],
                                         start=(k == 0), stop=(k == CK - 1))
                    last.then_inc(s_k0, 1)
                for b in range(B):
                    if b == 2:
                        pe.wait_ge(s_k0e, KT)
                    for j in range(HJ):
                        h0, nh = tile_heads(j)
                        off, n0 = P * j % KP, first_slot(j)
                        for k in range(CK):
                            last = pe.matmul(
                                pb[b][:, 0:NSLOT * D0].rearrange("p (a n) -> p a n", a=2)[:, :, n0 * D0:(n0 + nh) * D0],
                                ctx3[:, k, b, :, :].rearrange("p r k -> p (r k)")[:, off:off + P],
                                wv0[:, k, :].rearrange("p (a n) -> p a n", a=2)[:, :, h0 * D0:(h0 + nh) * D0],
                                start=(k == 0), stop=(k == CK - 1))
                    last.then_inc(s_v0, 1)
                ffnw.transpose(pe)

            @block.vector
            def _(dve):
                for k in range(CK):
                    dve.wait_ge(s_cT, k + 1)
                    v = pb[k][0:CP, 0:B * KP].rearrange("p (b k) -> p b k", b=B)
                    dve.tensor_copy(ctxT[:, k, :, 0:NKEY], v[:, :, 0:NKEY]).then_inc(s_cTe, 1)
                    dve.tensor_copy(ctxT[:, k, :, NKEY:KP],
                                    v[:, :, 0:1].broadcast_to([CP, B, KP - NKEY])).then_inc(s_cTe, 1)
                dve.wait_ge(s_cTe, 4)
                for r in range(3):
                    last = dve.tensor_copy(ctx3[:, :, :, r, :].rearrange("p c b k -> p (c b) k"),
                                           ctxT[:].rearrange("p c b k -> p (c b) k"))
                last.then_inc(s_cTe, 1)
                dve.wait_ge(s_id, 7)
                for m in range(KT):
                    dve.wait_ge(s_k0, m + 1)
                    dve.tensor_scalar(kT[:, m, :, :], pb[2 + m][:, 0:B * KP].rearrange("p (b k) -> p b k", b=B),
                                      bk0[:, m:m + 1], None, ALU.add).then_inc(s_k0e, 1)
                    dve.wait_ge(s_k0e, m + 1)
                    for h in range(8):
                        dve.tensor_scalar(keys0[:, :, m, h, :], kT[:, m, :, :], hsel[:, h:h + 1], None, ALU.mult)
                ffnw.quantise(dve)
                dve.wait_ge(s_id, 7 + 2 * HJ)
                for j in range(NJ):
                    h0, nh = tile_heads(j)
                    h0 += 8 * (j // HJ)
                    n0 = first_slot(j)
                    dve.tensor_copy(sels[:, n0:n0 + nh], psel[:, 0, j % HJ, 0:nh])
                    last = dve.tensor_copy(bvs[:, n0:n0 + nh, :].rearrange("p h d -> p (h d)"),
                                           bv0[:, h0 * D0:(h0 + nh) * D0])
                last.then_inc(s_v0e, 1)
                dve.wait_ge(s_v0e, 1)
                for b in range(B):
                    dve.wait_ge(s_v0, b + 1)
                    vv = vals0[:, b, :, 0:D0]
                    dve.tensor_tensor(vv, pb[b][:, 0:NSLOT * D0].rearrange("p (h d) -> p h d", d=D0), bvs[:],
                                      ALU.add).then_inc(s_v0e, 1)
                    dve.tensor_copy(vals0[:, b, :, D0], sels[:])
                    dve.wait_ge(s_v0e, b + 2)
                    dve.tensor_tensor(vv, vv, sels[:].unsqueeze(2).broadcast_to([P, NSLOT, D0]), ALU.mult)
                ffnw.remainder(dve)

    attention(nc, stack, sem, sbuf, xt, col, 0, dict(
        s_x=s_x, ident=ident, mhalf=mhalf, wq=wq0, bq=bq0, wo=wo0, bo=bo0, keys=keys0, vals=vals0,
        hmean=hmean, hrstd=hrstd, hamax=hamax))
    att0.close()
    old, sem = sem, Sems(nc)
    ffn(nc, sem, old, sbuf, xs, dict(fw, ident=ident, hmean=hmean, hrstd=hrstd, hamax=hamax))
    until_ffn.close()
    old, sem = sem, Sems(nc)
    with ExitStack() as att1:
        p1 = prepare1(nc, att1, sem, old, sbuf, dict(w, ident=ident, cscr=cscr, psel=psel, mask=mask))
        attention(nc, stack, sem, sbuf, xt, col, 1, dict(p1, ident=ident, mhalf=mhalf))
    moe(nc, stack, sem, sbuf, xs, xt, col, dict(w, ident=ident, mhalf=mhalf), out)


def prepare1(nc, st, sem, retired, sbuf, c):
    OD = H * D1
    NM = OD // P

    def s(name):
        return sem("p1_" + name)
    s_in, s_m, s_id3, s_wT, s_wTe = s("in"), s("m"), s("id3"), s("wT"), s("wTe")
    s_mr, s_mre, s_k, s_ke, s_A, s_Ah, s_Al = s("mr"), s("mre"), s("k"), s("ke"), s("A"), s("Ah"), s("Al")
    s_v, s_ve, s_nv, s_c3, s_km = s("v"), s("ve"), s("nv"), s("c3"), s("km")
    s_wo, s_ct, s_wq = s("wo"), s("ct"), s("wq")

    keysh = sbuf(st, "keysh", [P, B, KT, SW], F32R)
    keysl = sbuf(st, "keysl", [P, B, KT, SW], F32R)
    vals = sbuf(st, "vals1", [P, B, NSLOT, D1 + 1])
    woh = sbuf(st, "woh1", [P, NM, D], F32R)
    wol = sbuf(st, "wol1", [P, NM, D], F32R)
    gout = sbuf(st, "gout", [P, D])
    with ExitStack() as tp:
        wkv = sbuf(tp, "wkv", [CP, CK, 2 * OD])
        wq = sbuf(tp, "wq1", [P, KT, OD])
        wo = wq[:].rearrange("p k n -> p (k n)").rearrange("p (m d) -> p m d", d=D)
        wqT = sbuf(tp, "wqT1", [P, NM, D])
        k1 = sbuf(tp, "k1", [P, 2, B * KP])
        gsc = sbuf(tp, "gsc", [P, KT])
        nk = sbuf(tp, "nk", [P, 1])
        nv = sbuf(tp, "nv", [P, D1])
        m8 = sbuf(tp, "m8", [P, B, NKEY], U8)
        mc8 = sbuf(tp, "mc8", [NKEY, B], U8)
        mb = sbuf(tp, "mb", [P, B, KP])
        nm = sbuf(tp, "nm", [P, B, KP])
        mcol = sbuf(tp, "mcol", [NKEY, B])
        id3 = sbuf(tp, "id3", [NKEY, 3, KP])
        ctxT = sbuf(tp, "ctxTb", [CP, CK, B, KP])
        ctx3 = sbuf(tp, "ctx3b", [CP, CK, B, 3, KP])
        mrow = sbuf(tp, "mrow", [P, HJ, B])
        sel = sbuf(tp, "sel1", [P, HJ, B, 3])
        nsel = sbuf(tp, "nsel", [P, HJ, 3])
        NV = sbuf(tp, "NV", [P, HJ, 3, D1])
        pb = [tp.enter_context(nc.psum_tensor(f"p1b{i}", [P, 512], F32)) for i in range(8)]
        WT, KB, AB, VB = pb[0:2], pb[2:4], pb[4:6] + pb[0:2], pb[6:8]

        order = [("k", 0)]
        for m in range(NM):
            order += [("k", m + 1)] * (m + 1 < NM)
            order += [("a", 4 * m + i) for i in range(4)]
            order += [("v", n) for n in range(B * HJ * m // NM, B * HJ * (m + 1) // NM)]

        def pair(b, j):
            n0, nh = first_slot(j), tile_heads(j)[1]
            return vals[:, b, :, :].rearrange("p (a s) e -> p a s e", a=2)[:, :, n0:n0 + nh, :]

        with nc.Block() as block:
            @block.sync
            def _(sp):
                sp.dma_start(wq[:], c["L1_xattn_Wq"].rearrange("(k p) n -> p k n", p=P)).then_inc(s_wq, 16)
                sp.dma_start(m8[:], c["mask"].rearrange("b k -> (b k)").partition_broadcast(P)
                             .rearrange("p (b k) -> p b k", b=B)).then_inc(s_m, 16)
                sp.dma_start(mc8[:], c["mask"].rearrange("b k -> k b"),
                             allow_slow_non_contiguous=True).then_inc(s_m, 16)
                sp.dma_start(nk[0:D1, :], c["L1_xattn_null_kv"][0].rearrange("(d a) -> d a", a=1)).then_inc(s_m, 16)
                sp.dma_start(nk[D1:P, :], c["L1_xattn_null_kv"][0].rearrange("(d a) -> d a", a=1)).then_inc(s_m, 16)
                sp.dma_start(nv[:], c["L1_xattn_null_kv"][1].partition_broadcast(P)).then_inc(s_m, 16)
                sp.dma_start(gsc[:], c["L1_xattn_g_norm"].rearrange("(k p) -> p k", p=P),
                             allow_slow_non_contiguous=True).then_inc(s_m, 16)
                sp.dma_start(wkv[:], c["L1_xattn_Wkv"].rearrange("(k p) n -> p k n", p=CP)).then_inc(s_in, 16)
                sp.dma_start(gout[:], c["L1_xattn_g_out"].partition_broadcast(P)).then_inc(s_in, 16)
                sp.dma_start(ctxT[:].rearrange("p c b k -> p (c b k)"), c["cscr"]).then_inc(s_ct, 16)
                retired.clear(sp)
                sp.wait_ge(s_wT, NM // 2)
                sp.dma_start(wo[:], c["L1_xattn_Wout"].rearrange("(k p) n -> p k n", p=P)).then_inc(s_wo, 16)

            @block.gpsimd
            def _(pool):
                pool.memset(mb[:], 0.0).then_inc(s_id3, 1)
                for r in range(3):
                    last = pool.tensor_copy(id3[:, r, :], c["ident"][0:NKEY, 0:KP])
                last.then_inc(s_id3, 1)
                pool.wait_ge(s_ct, 16)
                for r in range(3):
                    last = pool.tensor_copy(ctx3[:, :, :, r, :].rearrange("p c b k -> p (c b) k"),
                                            ctxT[:].rearrange("p c b k -> p (c b) k"))
                last.then_inc(s_c3, 1)
                pool.wait_ge(s_nv, 6)
                for n in range(B * HJ):
                    b, j = n // HJ, n % HJ
                    nh = tile_heads(j)[1]
                    pool.wait_ge(s_ve, n + 1)
                    v = pair(b, j)[:, :, :, 0:D1]
                    pool.tensor_tensor(v, v, NV[:, j, 0:nh, :].unsqueeze(1).broadcast_to([P, 2, nh, D1]), ALU.add)

            @block.tensor
            def _(pe):
                pe.wait_ge(s_wq, 16)
                for m in range(NM // 2):
                    if m >= 2:
                        pe.wait_ge(s_wTe, m - 1)
                    for n in range(2):
                        for k in range(KT):
                            last = pe.transpose(WT[m % 2][:, (2 * n + k) * P:(2 * n + k + 1) * P],
                                                wq[:, k, (2 * m + n) * P:(2 * m + n + 1) * P], c["ident"][:])
                    last.then_inc(s_wT, 1)
                pe.wait_ge(s_id3, 2)
                pe.wait_ge(s_mre, 1)
                for jj in range(HJ):
                    off = P * jj % KP
                    last = pe.matmul(VB[0][:, jj * B:(jj + 1) * B],
                                     id3[:].rearrange("p r k -> p (r k)")[:, off:off + P], mcol[:],
                                     start=True, stop=True)
                last.then_inc(s_mr, 1)
                for kind, n in order:
                    if kind == "k":
                        if n == 0:
                            pe.wait_ge(s_in, 32)
                            pe.wait_ge(s_ct, 16)
                        if n >= 2:
                            pe.wait_ge(s_ke, n - 1)
                        for k in range(CK):
                            last = pe.matmul(KB[n % 2][:, 0:B * KP], wkv[:, k, n * P:(n + 1) * P],
                                             ctxT[:, k, :, :], start=(k == 0), stop=(k == CK - 1))
                        last.then_inc(s_k, 1)
                    elif kind == "v":
                        b, j = n // HJ, n % HJ
                        h0, nh = tile_heads(j)
                        off = P * j % KP
                        if n == 0:
                            pe.wait_ge(s_c3, 1)
                            pe.wait_ge(s_mre, 2)
                        if n >= 2:
                            pe.wait_ge(s_ve, n - 1)
                        for k in range(CK):
                            last = pe.matmul(VB[n % 2][:, 0:2 * nh * D1].rearrange("p (a n) -> p a n", a=2),
                                             ctx3[:, k, b, :, :].rearrange("p r k -> p (r k)")[:, off:off + P],
                                             wkv[:, k, OD:2 * OD].rearrange("p (a n) -> p a n", a=2)[
                                                 :, :, h0 * D1:(h0 + nh) * D1], start=(k == 0), stop=(k == CK - 1))
                        last.then_inc(s_v, 1)
                    else:
                        m, hh, k = n // 4, n // 2 % 2, n % 2
                        if n % 4 == 0:
                            pe.wait_ge(s_ke, m + 1)
                            pe.wait_ge(s_wTe, m // 2 + 1)
                        if n == 2:
                            pe.wait_ge(s_wTe, NM // 2)
                        if n >= 4:
                            pe.wait_ge(s_Al, n - 3)
                        pe.matmul(AB[n % 4][:, 0:B * KP], wqT[hh * D1:(hh + 1) * D1, m, k * P:(k + 1) * P],
                                  k1[hh * D1:(hh + 1) * D1, m % 2, :], start=True, stop=True).then_inc(s_A, 1)

            @block.scalar
            def _(act):
                act.wait_ge(s_m, 96)
                act.mul(gsc[:], gsc[:], D1 ** -0.5).then_inc(s_Ah, 1)
                for m in range(NM // 2):
                    act.wait_ge(s_wT, m + 1)
                    act.copy(wqT[:, 2 * m:2 * m + 2, :].rearrange("p m n -> p (m n)"), WT[m % 2][:]).then_inc(s_wTe, 1)
                for n in range(4 * NM):
                    m, hh, k = n // 4, n // 2 % 2, n % 2
                    h = 2 * m + hh
                    act.wait_ge(s_A, n + 1)
                    act.wait_ge(s_Ah, 1)
                    act.activation(keysh[:, :, k, h * KP:(h + 1) * KP],
                                   AB[n % 4][:, 0:B * KP].rearrange("p (b k) -> p b k", b=B), ACT.Copy,
                                   scale=gsc[:, k:k + 1]).then_inc(s_Ah, 1)
                act.wait_ge(s_wo, 16)
                act.copy(woh[:], wo).then_inc(s_wo, 1)

            @block.vector
            def _(dve):
                dve.wait_ge(s_m, 96)
                dve.wait_ge(s_id3, 1)
                dve.tensor_copy(mb[:, :, 0:NKEY], m8[:]).then_inc(s_nv, 1)
                dve.tensor_copy(mcol[:], mc8[:]).then_inc(s_mre, 1)
                dve.wait_ge(s_nv, 1)
                dve.tensor_scalar(nm[:], mb[:], -1.0, 1.0, ALU.mult, ALU.add).then_inc(s_nv, 1)
                dve.tensor_tensor(nsel[:], c["psel"][:, 1], c["psel"][:, 0], ALU.subtract).then_inc(s_nv, 1)
                dve.wait_ge(s_nv, 3)
                dve.tensor_scalar(nm[:], nm[:], nk[:, 0:1], None, ALU.mult).then_inc(s_nv, 1)
                dve.tensor_tensor(NV[:].rearrange("p j i d -> p (j i) d"),
                                  nsel[:].rearrange("p j i -> p (j i)").unsqueeze(2).broadcast_to([P, 3 * HJ, D1]),
                                  nv[:].unsqueeze(1).broadcast_to([P, 3 * HJ, D1]), ALU.mult).then_inc(s_nv, 1)
                dve.wait_ge(s_mr, 1)
                dve.tensor_copy(mrow[:].rearrange("p j b -> p (j b)"), VB[0][:, 0:HJ * B]).then_inc(s_mre, 1)
                dve.wait_ge(s_mre, 2)
                for jj in range(HJ):
                    last = dve.tensor_tensor(sel[:, jj, :, :], c["psel"][:, 0, jj, :].unsqueeze(1).broadcast_to([P, B, 3]),
                                             mrow[:, jj, :].unsqueeze(2).broadcast_to([P, B, 3]), ALU.mult)
                last.then_inc(s_nv, 1)
                dve.wait_ge(s_nv, 6)

                def remainder(n):
                    m, hh, k = n // 4, n // 2 % 2, n % 2
                    h = 2 * m + hh
                    dve.wait_ge(s_Ah, n + 2)
                    hi = keysh[:, :, k, h * KP:(h + 1) * KP]
                    dve.scalar_tensor_tensor(keysl[:, :, k, h * KP:(h + 1) * KP],
                                             AB[n % 4][:, 0:B * KP].rearrange("p (b k) -> p b k", b=B),
                                             gsc[:, k:k + 1], hi.bitcast(F32), ALU.mult,
                                             ALU.subtract).then_inc(s_Al, 1)
                for kind, n in order:
                    if kind == "k":
                        dve.wait_ge(s_k, n + 1)
                        if n >= 2:
                            dve.wait_ge(s_A, 4 * (n - 1))
                        kv = k1[:, n % 2, :]
                        dve.tensor_tensor(kv, KB[n % 2][:, 0:B * KP], mb[:].rearrange("p b k -> p (b k)"),
                                          ALU.mult).then_inc(s_km, 1)
                        dve.wait_ge(s_km, n + 1)
                        dve.tensor_tensor(kv, kv, nm[:].rearrange("p b k -> p (b k)"), ALU.add).then_inc(s_ke, 1)
                    elif kind == "v":
                        b, j = n // HJ, n % HJ
                        h0, nh = tile_heads(j)
                        dve.wait_ge(s_v, n + 1)
                        keep = sel[:, j, b, 0:nh]
                        dve.tensor_tensor(
                            pair(b, j)[:, :, :, 0:D1],
                            VB[n % 2][:, 0:2 * nh * D1].rearrange("p (a h d) -> p a h d", a=2, d=D1),
                            keep.unsqueeze(1).unsqueeze(3).broadcast_to([P, 2, nh, D1]), ALU.mult).then_inc(s_ve, 1)
                        for a in range(2):
                            dve.tensor_tensor(pair(b, j)[:, a, :, D1], keep, nsel[:, j, 0:nh], ALU.add)
                    else:
                        remainder(n)
                dve.wait_ge(s_wo, 17)
                dve.tensor_tensor(wol[:], wo, woh[:].bitcast(F32), ALU.subtract)
    retired.stack.close()
    return dict(keysh=keysh, keysl=keysl, vals=vals, woh=woh, wol=wol, gout=gout)


def attention(nc, stack, sem, sbuf, xt, col, layer, c):
    L1 = layer == 1
    dh = D1 if L1 else D0
    OD = H * dh
    NO = OD // P
    PH = 1 if L1 else 2
    NC = NO // 4 if L1 else 1
    sb = [0, 1, 2, 0] if L1 else [0, 1, 0, 1]
    PTS = [range(0, 4), range(4, 8), range(8, 10)]
    tag = f"a{layer}_"

    def s(name):
        return sem(tag + name)

    s_stat, s_aggr, s_veps, s_rstd, s_xn = s("stat"), s("aggr"), s("veps"), s("rstd"), s("xn")
    s_xT, s_xTe, s_q, s_qe, s_S = s("xT"), s("xTe"), s("q"), s("qe"), s("S")
    s_mx, s_clip, s_U, s_sh, s_P = s("mx"), s("clip"), s("U"), s("sh"), s("P")
    s_PT, s_PTe, s_PV, s_rec, s_O = s("PT"), s("PTe"), s("PV"), s("rec"), s("O")
    s_oT, s_oTe, s_y, s_xb, s_x1 = s("oT"), s("oTe"), s("y"), s("xb"), s("x1")
    s_st2, s_ag2, s_ve2, s_rs2, s_h, s_am = s("st2"), s("ag2"), s("ve2"), s("rs2"), s("h"), s("am")
    s_y2, s_yg, s_xl, s_oTl = s("y2"), s("yg"), s("xl"), s("oTl")

    order = []
    for t in range(-3, NT + 1):
        order += [("PT", t, k) for k in range(3)] * (0 <= t < NT)
        order += [("xT", t + 3, 0)] * (0 <= t + 3 < NT)
        order += [("oT", t - 1, k) for k in range(NC)] * (0 <= t - 1 < NT)
        order += [("y", t - 1, 0)] * (L1 and 0 <= t - 1 < NT)
    ring = Slots(order, lambda n, kind, k: n % 2 if L1 else k if kind == "PT" else 3)
    freed = {"xT": lambda t, k: (s_xl if L1 else s_xTe, t.of(lambda n: n + 1)),
             "oT": lambda t, k: (s_oTl if L1 else s_oTe, t.of(lambda n: NC * n + k + 1)),
             "PT": lambda t, k: (s_PTe, t.of(lambda n: 3 * n + k + 1)),
             "y": lambda t, k: (s_y2, t.of(lambda n: n + 1))}

    LO, HI, FIRST, LAST = 3, 26, -5, NT + 1
    E1 = D1 + 1
    HB = ((0, 6), (6, 11), (11, 16))

    def tiles_of(bank):
        return [j for j in range(NJ) if bank[0] < (j // HJ) * 8 + sum(tile_heads(j)) and bank[1] > (j // HJ) * 8 + tile_heads(j)[0]]
    first_tile = [tiles_of(q)[0] for q in HB]
    last_tile = [tiles_of(q)[-1] for q in HB]

    with ExitStack() as st:
        ps = [st.enter_context(nc.psum_tensor(f"{tag}ps{i}", [P, 512], F32)) for i in range(8)]
        if L1:
            S, R, PV, M = ps[0:3], ps[3:5], ps[5:8], None
        else:
            S, R, PV, M = ps[0:2], ps[2:6], ps[6:7], ps[7]
        stats = sbuf(st, tag + "stats", [P, 2, 6])
        xag = sbuf(st, tag + "xag", [P, 2, 2])
        xve = sbuf(st, tag + "xve", [P, 2])
        xrs = sbuf(st, tag + "xrs", [P, 2])
        xn = [sbuf(st, f"{tag}xn{i}", [P, D]) for i in range(2)]
        xnT = [sbuf(st, f"{tag}xnT{i}", [P, KT, P], F32R if L1 else F32) for i in range(2)]
        xnl = [sbuf(st, f"{tag}xnl{i}", [P, KT, P], F32R) for i in range(2)] if L1 else None
        qT = None if L1 else [sbuf(st, f"{tag}qT{i}", [P, KT, P]) for i in range(2)]
        mx = [sbuf(st, f"{tag}mx{i}", [P, H]) for i in range(2)]
        U = [sbuf(st, f"{tag}U{i}", [P, SW]) for i in range(2)]
        PTs = [sbuf(st, f"{tag}PT{i}", [P, NJ, P]) for i in range(2)]
        rc = [sbuf(st, f"{tag}rc{i}", [P, H]) for i in range(2)]
        o = [sbuf(st, f"{tag}o{i}", [P, OD]) for i in range(1 if L1 else 2)] * (2 if L1 else 1)
        oT = [sbuf(st, f"{tag}oT{i}", [P, NO, P], F32R if L1 else F32) for i in range(2)]
        st2 = sbuf(st, tag + "st2", [P, 2, 6])
        yag = sbuf(st, tag + "yag", [P, 2, 2])
        hb = None if L1 else sbuf(st, tag + "hb", [P, 2, D])
        oTl = [sbuf(st, f"{tag}oTl{i}", [P, NO, P], F32R) for i in range(2)] if L1 else None
        yve = sbuf(st, tag + "yve", [P, 2])
        yrs = sbuf(st, tag + "yrs", [P, 2])
        if L1:
            yb = [sbuf(st, f"{tag}yb{i}", [P, D]) for i in range(2)]
        else:
            amx = sbuf(st, tag + "amx", [P, 2])

        def ring_wait(pe, kind, t, k=0):
            prev = ring.before(kind, t, k)
            if prev is not None:
                pe.wait_ge(*freed[prev[0]](prev[1], prev[2]))
            return R[ring.bank(kind, t, k)]

        with nc.Block() as block:
            @block.tensor
            def _(pe):
                def scores(a, g):
                    b = a.batch
                    if L1:
                        if g == 3:
                            pe.wait_ge(s_U, a.of(lambda n: 4 * n + 1))
                        elif a.t0 >= 1:
                            pe.wait_ge(s_U, a.of(lambda n: 4 * n - 4 + (4 if g == 0 else g + 1)))
                        n = 0
                        for x_, k_ in ((xnT, "keysh"), (xnl, "keysh"), (xnT, "keysl")):
                            for k in range(KT):
                                last = pe.matmul(
                                    S[sb[g]][:, 0:QW], x_[a.p][:, k, :],
                                    c[k_][:].rearrange("p b m n -> p (b m n)")[
                                        :, bass.ds(b * (KT * SW) + k * SW + g * QW, QW)],
                                    start=(n == 0), stop=(n == 3 * KT - 1))
                                n += 1
                        last.then_inc(s_S, 1)
                        return
                    if a.t0 >= 1 or g >= 2:
                        pe.wait_ge(s_clip, a.of(lambda n: 4 * n + g - 1))
                    pe.matmul(S[sb[g]][:, 0:QW], qT[a.p][:, g // 2, :],
                              c["keys"][:].rearrange("p b m h k -> p (b m h k)")[
                                  :, bass.ds(b * (KT * 8 * KP) + g * QW, QW)],
                              start=True, stop=True).then_inc(s_S, 1)

                def probs_T(t, k):
                    if k == 0:
                        pe.wait_ge(s_P, t.of(lambda n: PH * (n + 1)))
                    r = ring_wait(pe, "PT", t, k)
                    for n, j in enumerate(PTS[k]):
                        last = pe.transpose(r[:, n * P:(n + 1) * P], U[t.p][:, j * P:(j + 1) * P], c["ident"][:])
                    last.then_inc(s_PT, 1)

                def out_T(a, kk):
                    if kk == 0:
                        pe.wait_ge(s_O, a.of(lambda n: n + 1))
                    r = ring_wait(pe, "oT", a, kk)
                    for k in range(NO // NC):
                        n = kk * (NO // NC) + k
                        last = pe.transpose(r[:, k * P:(k + 1) * P], o[a.p][:, n * P:(n + 1) * P], c["ident"][:])
                    last.then_inc(s_oT, 1)

                def body(t):
                    nxt, new, old = t + 2, t + 3, t + -1
                    if t.ok():
                        probs_T(t, 0)
                        probs_T(t, 1)
                    if nxt.ok():
                        if L1:
                            pe.wait_ge(s_xTe, nxt.of(lambda n: n + 1))
                            pe.wait_ge(s_xl, nxt.of(lambda n: n + 1))
                        else:
                            pe.wait_ge(s_qe, nxt.of(lambda n: n + 1))
                        scores(nxt, 0)
                    if t.ok():
                        probs_T(t, 2)
                    if new.ok():
                        pe.wait_ge(s_xn, new.of(lambda n: n + 1))
                        r = ring_wait(pe, "xT", new)
                        for k in range(KT):
                            last = pe.transpose(r[:, k * P:(k + 1) * P], xn[new.p][:, k * P:(k + 1) * P],
                                                c["ident"][:])
                        last.then_inc(s_xT, 1)
                    if nxt.ok():
                        scores(nxt, 1)
                    if old.ok():
                        out_T(old, 0)
                    a = new
                    if a.ok() and not L1:
                        pe.wait_ge(s_xTe, a.of(lambda n: n + 1))
                        if a.t0 >= 5:
                            pe.wait_ge(s_x1, a.of(lambda n: n - 4))
                        elif a.t0 >= 1:
                            pe.wait_ge(s_qe, a.of(lambda n: n))
                        for m in range(KT):
                            for k in range(KT):
                                last = pe.matmul(M[:, m * P:(m + 1) * P], c["wq"][:, k, m * P:(m + 1) * P],
                                                 xnT[a.p][:, k, :], start=(k == 0), stop=(k == KT - 1))
                        last.then_inc(s_q, 1)
                    if nxt.ok():
                        scores(nxt, 2)
                    for kk in range(1, NC):
                        if old.ok():
                            out_T(old, kk)
                    if nxt.ok():
                        scores(nxt, 3)
                    a = t + -1
                    if a.ok():
                        pe.wait_ge(s_oTe, a.of(lambda n: NC * (n + 1)))
                        if L1:
                            y = ring_wait(pe, "y", a)
                        elif a.t0 + 4 < NT:
                            pe.wait_ge(s_qe, a.of(lambda n: n + 5))
                        else:
                            pe.wait_ge(s_x1, a.of(lambda n: n))
                        if not L1:
                            y = M
                        if L1:
                            parts = ((oT, c["woh"]), (oT, c["wol"]), (oTl, c["woh"]))
                        else:
                            parts = ((oT, c["wo"]),)
                        pairs = [(o_[a.p][:, k, :], w_[:, k, :]) for o_, w_ in parts for k in range(NO)]
                        for n, (lhs, rhs) in enumerate(pairs):
                            if n == 2 * NO:
                                pe.wait_ge(s_oTl, a.of(lambda n: NC * (n + 1)))
                            last = pe.matmul(y[:, 0:D], lhs, rhs, start=(n == 0), stop=(n == len(pairs) - 1))
                        last.then_inc(s_y, 1)
                    if t.ok():
                        if t.t0 >= 1:
                            pe.wait_ge(s_O, t.of(lambda n: n))
                        for k, js in enumerate(PTS):
                            pe.wait_ge(s_PTe, t.of(lambda n: 3 * n + k + 1))
                            for j in js:
                                h0, nh = tile_heads(j)
                                h0 += 8 * (j // HJ)
                                if L1:
                                    row = t.batch * (NSLOT * E1) + first_slot(j) * E1
                                    for q, (lo_, hi_) in enumerate(HB):
                                        a_, b_ = max(h0, lo_), min(h0 + nh, hi_)
                                        if a_ >= b_:
                                            continue
                                        last = pe.matmul(
                                            PV[q][:, (a_ - lo_) * E1:(b_ - lo_) * E1], PTs[t.p][:, j, :],
                                            c["vals"][:].rearrange("p b s e -> p (b s e)")[
                                                :, bass.ds(row + (a_ - h0) * E1, (b_ - a_) * E1)],
                                            start=(j == first_tile[q]),
                                            stop=(j == last_tile[q]), skip_group_check=True)
                                    continue
                                E = D0 + 1
                                last = pe.matmul(
                                    PV[0][:, h0 * E:(h0 + nh) * E], PTs[t.p][:, j, :],
                                    c["vals"][:].rearrange("p b s e -> p (b s e)")[
                                        :, bass.ds(t.batch * (NSLOT * E) + first_slot(j) * E, nh * E)],
                                    start=(j == 0), stop=(j == NJ - 1), skip_group_check=True)
                        last.then_inc(s_PV, 1)

                pipeline(pe, body, FIRST, LAST, LO, HI)

            @block.scalar
            def _(act):
                def body(t):
                    if t.ok():
                        if t.t0 >= 2:
                            act.wait_ge(s_PV, t.of(lambda n: n - 1))
                        for k, js in enumerate(PTS):
                            act.wait_ge(s_PT, t.of(lambda n: 3 * n + k + 1))
                            act.copy(PTs[t.p][:, js[0]:js[-1] + 1, :].rearrange("p j n -> p (j n)"),
                                     R[ring.bank("PT", t, k)][:, 0:len(js) * P]).then_inc(s_PTe, 1)
                    a = t + 3
                    if a.ok():
                        act.wait_ge(s_xT, a.of(lambda n: n + 1))
                        if a.t0 >= 2 and L1:
                            act.wait_ge(s_S, a.of(lambda n: 4 * (n - 1)))
                        elif a.t0 >= 2:
                            act.wait_ge(s_q, a.of(lambda n: n - 1))
                        act.copy(xnT[a.p][:].rearrange("p k n -> p (k n)"),
                                 R[ring.bank("xT", a)][:, 0:D]).then_inc(s_xTe, 1)
                    a = t + -1
                    if a.ok():
                        if a.t0 >= 2:
                            act.wait_ge(s_y, a.of(lambda n: n - 1))
                        for kk in range(NC):
                            act.wait_ge(s_oT, a.of(lambda n: NC * n + kk + 1))
                            w_ = OD // NC
                            act.copy(oT[a.p][:].rearrange("p k n -> p (k n)")[:, kk * w_:(kk + 1) * w_],
                                     R[ring.bank("oT", a, kk)][:, 0:w_]).then_inc(s_oTe, 1)
                    a = t + -1
                    if a.ok() and L1:
                        act.wait_ge(s_y, a.of(lambda n: n + 1))
                        if a.t0 >= 2:
                            act.wait_ge(s_x1, a.of(lambda n: n - 1))
                        act.copy(yb[a.p][:], R[ring.bank("y", a)][:, 0:D]).then_inc(s_y2, 1)
                    a = t + 3
                    if a.ok() and not L1:
                        act.wait_ge(s_q, a.of(lambda n: n + 1))
                        if a.t0 >= 2:
                            act.wait_ge(s_S, a.of(lambda n: 4 * (n - 1)))
                        for m in range(KT):
                            last = act.activation(qT[a.p][:, m, :], M[:, m * P:(m + 1) * P], ACT.Identity,
                                                  bias=c["bq"][:, m:m + 1], scale=D0 ** -0.5)
                        last.then_inc(s_qe, 1)
                    a = t + 2
                    if a.ok():
                        if L1:
                            act.wait_ge(s_U, a.of(lambda n: 4 * n + 4))
                            act.activation(U[a.p][:], U[a.p][:], ACT.Exp).then_inc(s_P, 1)
                        else:
                            act.wait_ge(s_sh, a.of(lambda n: 2 * n + 2))
                            act.activation(U[a.p][:, 0:2 * QW], U[a.p][:, 0:2 * QW], ACT.Exp).then_inc(s_P, 1)
                            act.wait_ge(s_mx, a.of(lambda n: 4 * n + 4))
                            for h in range(8, H):
                                v = U[a.p][:, h * KP:(h + 1) * KP]
                                last = act.activation(v, v, ACT.Exp, bias=mx[a.p][:, h:h + 1])
                            last.then_inc(s_P, 1)

                pipeline(act, body, FIRST, LAST, LO, HI)

            @block.gpsimd
            def _(pool):
                def rsqrt(t, ve, rs, s_ve, s_rs):
                    pool.wait_ge(s_ve, t.of(lambda n: n + 1))
                    pool.tensor_tensor(rs[:, t.p:t.p + 1], ve[:, t.p:t.p + 1], c["mhalf"][:],
                                       ALU.pow).then_inc(s_rs, 1)

                def body(t):
                    a = t + 2
                    if a.ok() and not L1:
                        for g in range(2):
                            pool.wait_ge(s_mx, a.of(lambda n: 4 * n + g + 1))
                            v = U[a.p][:, g * QW:(g + 1) * QW].rearrange("p (h k) -> p h k", k=KP)
                            pool.tensor_tensor(v, v, mx[a.p][:, 4 * g:4 * g + 4].unsqueeze(2).broadcast_to([P, 4, KP]),
                                               ALU.add).then_inc(s_sh, 1)
                    a = t + 5
                    if a.ok():
                        rsqrt(a, xve, xrs, s_veps, s_rstd)
                    if t.ok() and not L1:
                        pool.wait_ge(s_xn, t.of(lambda n: n + 1))
                        pool.tensor_tensor(xt(t), xt(t), c["bo"][:], ALU.add).then_inc(s_xb, 1)
                    a = t + -1
                    if a.ok():
                        rsqrt(a, yve, yrs, s_ve2, s_rs2)
                    a = t + -2
                    if a.ok() and L1:
                        pool.wait_ge(s_h, a.of(lambda n: n + 1))
                        pool.tensor_tensor(yb[a.p][:], yb[a.p][:], c["gout"][:], ALU.mult).then_inc(s_yg, 1)
                        pool.wait_ge(s_yg, a.of(lambda n: n + 1))
                        pool.tensor_tensor(xt(a), xt(a), yb[a.p][:], ALU.add).then_inc(s_x1, 1)

                pipeline(pool, body, FIRST, LAST, LO, HI)

            @block.vector
            def _(dve):
                def o_remainder(a, kk):
                    if a.t0 >= 2 and kk == 0:
                        dve.wait_ge(s_y, a.of(lambda n: n - 1))
                    dve.wait_ge(s_oTe, a.of(lambda n: NC * n + kk + 1))
                    w_ = OD // NC
                    dve.tensor_tensor(oTl[a.p][:].rearrange("p k n -> p (k n)")[:, kk * w_:(kk + 1) * w_],
                                      R[ring.bank("oT", a, kk)][:, 0:w_],
                                      oT[a.p][:].rearrange("p k n -> p (k n)")[:, kk * w_:(kk + 1) * w_].bitcast(F32),
                                      ALU.subtract).then_inc(s_oTl, 1)

                def remainder(a):
                    dve.wait_ge(s_xTe, a.of(lambda n: n + 1))
                    if a.t0 >= 2:
                        dve.wait_ge(s_S, a.of(lambda n: 4 * (n - 1)))
                    dve.tensor_tensor(xnl[a.p][:].rearrange("p k n -> p (k n)"), R[ring.bank("xT", a)][:, 0:D],
                                      xnT[a.p][:].rearrange("p k n -> p (k n)").bitcast(F32),
                                      ALU.subtract).then_inc(s_xl, 1)

                def body(t):
                    a = t + 2
                    if L1:
                        def quad(g):
                            return S[sb[g]][:, 0:QW].rearrange("p (h k) -> p h k", k=KP)

                        def top(g):
                            if a.ok():
                                dve.wait_ge(s_S, a.of(lambda n: 4 * n + g + 1))
                                dve.tensor_reduce(mx[a.p][:, 4 * g:4 * g + 4], quad(g), AX.X,
                                                  ALU.max).then_inc(s_mx, 1)

                        def shift(g):
                            if not a.ok():
                                return
                            if g == 0 and a.t0 >= 2:
                                dve.wait_ge(s_PT, a.of(lambda n: 3 * (n - 1)))
                            dve.wait_ge(s_mx, a.of(lambda n: 4 * n + g + 1))
                            dve.tensor_tensor(U[a.p][:, g * QW:(g + 1) * QW].rearrange("p (h k) -> p h k", k=KP),
                                              quad(g), mx[a.p][:, 4 * g:4 * g + 4].unsqueeze(2).broadcast_to([P, 4, KP]),
                                              ALU.subtract).then_inc(s_U, 1)
                        top(0)
                        if (t + 3).ok():
                            remainder(t + 3)
                        top(1)
                        shift(0)
                        if (t + -1).ok():
                            o_remainder(t + -1, 0)
                        shift(1)
                        top(2)
                        if (t + -1).ok():
                            o_remainder(t + -1, 1)
                        shift(2)
                        top(3)
                        shift(3)
                    if a.ok() and not L1:
                        if a.t0 >= 2:
                            dve.wait_ge(s_PT, a.of(lambda n: 3 * (n - 1)))

                        def clip(g):
                            dve.wait_ge(s_S, a.of(lambda n: 4 * n + g + 1))
                            dve.tensor_scalar(U[a.p][:, g * QW:(g + 1) * QW], S[sb[g]][:, 0:QW], CLAMP, -CLAMP, ALU.min,
                                              ALU.max).then_inc(s_clip, 1)

                        def neg_top(g):
                            dve.wait_ge(s_clip, a.of(lambda n: 4 * n + g + 1))
                            dve.tensor_reduce(mx[a.p][:, 4 * g:4 * g + 4],
                                              U[a.p][:, g * QW:(g + 1) * QW].rearrange("p (h k) -> p h k", k=KP),
                                              AX.X, ALU.max, negate=True).then_inc(s_mx, 1)
                        clip(0)
                        clip(1)
                        neg_top(0)
                        clip(2)
                        neg_top(1)
                        clip(3)
                        neg_top(2)
                        neg_top(3)
                    a = t + -1
                    if a.ok() and not L1:
                        dve.wait_ge(s_y, a.of(lambda n: n + 1))
                        dve.wait_ge(s_xb, a.of(lambda n: n + 1))
                        dve.tensor_tensor(xt(a), M[:, 0:D], xt(a), ALU.add).then_inc(s_x1, 1)
                    b = t + 4
                    if b.ok():
                        dve.wait_ge(s_rstd, b.of(lambda n: n + 1))
                        if b.t0 >= 2:
                            dve.wait_ge(s_xT, b.of(lambda n: n - 1))
                        if a.ok() and not L1:
                            dve.wait_ge(s_x1, a.of(lambda n: n + 1))
                        dve.tensor_scalar(xn[b.p][:], xt(b), xag[:, b.p, 0:1], xrs[:, b.p:b.p + 1],
                                          ALU.subtract, ALU.mult).then_inc(s_xn, 1)
                    a = t + -1
                    if a.ok():
                        if not L1:
                            if not b.ok():
                                dve.wait_ge(s_x1, a.of(lambda n: n + 1))
                            dve.bn_stats(st2[:, a.p, :], xt(a)).then_inc(s_st2, 1)
                        else:
                            dve.wait_ge(s_y2, a.of(lambda n: n + 1))
                            dve.bn_stats(st2[:, a.p, :], yb[a.p][:]).then_inc(s_st2, 1)
                    a = t + 5
                    if a.ok():
                        dve.bn_stats(stats[:, a.p, :], xt(a)).then_inc(s_stat, 1)
                    a = t + -2
                    if a.ok() and not L1:
                        dve.wait_ge(s_am, a.of(lambda n: n + 1))
                        dve.wait_ge(s_rs2, a.of(lambda n: n + 1))
                        dve.tensor_scalar(col(c["hamax"], a), amx[:, a.p:a.p + 1], yrs[:, a.p:a.p + 1], None, ALU.mult)
                        dve.tensor_copy(col(c["hrstd"], a), yrs[:, a.p:a.p + 1])
                    if a.ok() and L1:
                        dve.wait_ge(s_rs2, a.of(lambda n: n + 1))
                        dve.tensor_scalar(yb[a.p][:], yb[a.p][:], yag[:, a.p, 0:1], yrs[:, a.p:a.p + 1],
                                          ALU.subtract, ALU.mult).then_inc(s_h, 1)
                    def statistics_done():
                        if (t + -1).ok():
                            dve.wait_ge(s_st2, (t + -1).of(lambda n: n + 1))
                        if (t + 5).ok():
                            dve.wait_ge(s_stat, (t + 5).of(lambda n: n + 1))
                    if t.ok() and L1:
                        dve.wait_ge(s_PV, t.of(lambda n: n + 1))
                        def pv(q):
                            n_ = HB[q][1] - HB[q][0]
                            return PV[q][:, 0:n_ * E1].rearrange("p (h e) -> p h e", e=E1)
                        for q, (lo_, hi_) in enumerate(HB):
                            last = dve.reciprocal(rc[t.p][:, lo_:hi_], pv(q)[:, :, D1])
                        last.then_inc(s_rec, 1)
                        dve.wait_ge(s_rec, t.of(lambda n: n + 1))
                        if t.t0 >= 1:
                            dve.wait_ge(s_oT, t.of(lambda n: NC * n))
                        statistics_done()
                        for q, (lo_, hi_) in enumerate(HB):
                            last = dve.tensor_tensor(
                                o[t.p][:, lo_ * D1:hi_ * D1].rearrange("p (h d) -> p h d", d=D1), pv(q)[:, :, 0:D1],
                                rc[t.p][:, lo_:hi_].unsqueeze(2).broadcast_to([P, hi_ - lo_, D1]), ALU.mult)
                        last.then_inc(s_O, 1)
                    if t.ok() and not L1:
                        dve.wait_ge(s_PV, t.of(lambda n: n + 1))
                        pv = PV[0][:, 0:H * (D0 + 1)].rearrange("p (h e) -> p h e", e=D0 + 1)
                        dve.reciprocal(rc[t.p][:], pv[:, :, D0]).then_inc(s_rec, 1)
                        dve.wait_ge(s_rec, t.of(lambda n: n + 1))
                        if t.t0 >= 2:
                            dve.wait_ge(s_oT, t.of(lambda n: n - 1))
                        statistics_done()
                        dve.tensor_tensor(o[t.p][:].rearrange("p (h d) -> p h d", d=D0), pv[:, :, 0:D0],
                                          rc[t.p][:].unsqueeze(2).broadcast_to([P, H, D0]),
                                          ALU.mult).then_inc(s_O, 1)

                    if (t + -1).ok():
                        if not t.ok():
                            statistics_done()
                        dve.bn_aggr(yag[:, 1 - t.p, :], st2[:, 1 - t.p, :]).then_inc(s_ag2, 1)
                    if (t + 5).ok():
                        if not t.ok():
                            statistics_done()
                        dve.bn_aggr(xag[:, 1 - t.p, :], stats[:, 1 - t.p, :]).then_inc(s_aggr, 1)
                    a = t + -1
                    if a.ok():
                        dve.wait_ge(s_ag2, a.of(lambda n: n + 1))
                        dve.tensor_scalar(yve[:, a.p:a.p + 1], yag[:, a.p, 1:2], EPS, None, ALU.add).then_inc(s_ve2, 1)
                    if a.ok() and not L1:
                        dve.tensor_scalar(hb[:, a.p, :], xt(a), yag[:, a.p, 0:1], None, ALU.subtract).then_inc(s_h, 1)
                        dve.tensor_copy(col(c["hmean"], a), yag[:, a.p, 0:1])
                        dve.wait_ge(s_h, a.of(lambda n: n + 1))
                        dve.tensor_reduce(amx[:, a.p:a.p + 1], hb[:, a.p, :], AX.X, ALU.max,
                                          apply_absolute_value=True).then_inc(s_am, 1)
                    a = t + 5
                    if a.ok():
                        dve.wait_ge(s_aggr, a.of(lambda n: n + 1))
                        if L1:
                            dve.tensor_scalar(xve[:, a.p:a.p + 1], xag[:, a.p, 1:2], 1.0 + EPS, EPS * EPS, ALU.mult,
                                              ALU.add).then_inc(s_veps, 1)
                        else:
                            dve.tensor_scalar(xve[:, a.p:a.p + 1], xag[:, a.p, 1:2], EPS, None,
                                              ALU.add).then_inc(s_veps, 1)
                if not L1:
                    for b in range(B):
                        dve.wait_ge(c["s_x"][b], 16)
                pipeline(dve, body, FIRST, LAST, LO, HI)


class FfnWeights:

    def __init__(self, nc, keep, temp, sem, sbuf, ident):
        self.wTh = sbuf(keep, "wTh", [P, 2, KT, FI], F32R)
        self.wTl = sbuf(keep, "wTl", [P, 2, KT, FI], F32R)
        self.dTh = sbuf(keep, "dTh", [P, FI // P, D], F32R)
        self.dTl = sbuf(keep, "dTl", [P, FI // P, D], F32R)
        self.ident, self.temp, self.nc, self.sbuf = ident, temp, nc, sbuf
        self.s_w = [sem(f"fw_in{i}") for i in range(3)]
        self.s_wb, self.s_q, self.s_f, self.s_wd = sem("fw_b"), sem("fw_q"), sem("fw_f"), sem("fw_d")
        self.s_wT, self.s_wh, self.s_wl = sem("fw_T"), sem("fw_h"), sem("fw_l")

    def scratch(self):
        nc, temp, sbuf = self.nc, self.temp, self.sbuf
        self.raw = [sbuf(temp, f"f_raw{i}", [P, 2 * FI]) for i in range(3)]
        self.wq = sbuf(temp, "f_wq", [P, 3, 2 * FI], I16)
        self.NB = 2 * FI // 32
        self.wa = sbuf(temp, "f_wa", [P, 3, self.NB])
        self.wr = sbuf(temp, "f_wr", [P, 3, self.NB])
        self.R = [temp.enter_context(nc.psum_tensor(f"fw_ps{i}", [P, 512], F32)) for i in range(4)]

    def blocks(self, n):
        i, m = n // 3, 2 * (n % 3)
        if i < 2:
            return [self.raw[i][:, (m + a) * D + k * P:(m + a) * D + (k + 1) * P]
                    for k in range(KT) for a in range(2)]
        return [self.raw[2][:, o * FI + (m + a) * P:o * FI + (m + a + 1) * P] for a in range(2) for o in range(2)]

    def part(self, n, high):
        i, m = n // 3, 2 * (n % 3)
        if i < 2:
            return (self.wTh if high else self.wTl)[:, i, :, m * P:(m + 2) * P]
        return (self.dTh if high else self.dTl)[:, m:m + 2, :]

    def bank(self, n):
        return self.R[n % 4][:].rearrange("p (k n) -> p k n", k=2)

    def load(self, sp, w):
        for i, n in enumerate(("L0_ffn_w_up", "L0_ffn_w_gate", "L0_ffn_w_down")):
            sp.dma_start(self.raw[i][:].rearrange("p (m n) -> p m n", n=w[n].shape[1]),
                         w[n].rearrange("(m p) n -> p m n", p=P)).then_inc(self.s_w[i], 16)

    def quantise(self, dve):
        for i in range(3):
            wa, wr = self.wa[:, i, :], self.wr[:, i, :]
            dve.wait_ge(self.s_w[i], 16)
            blk = self.raw[i][:].rearrange("p (b k) -> p b k", k=32)
            qb = self.wq[:, i, :].rearrange("p (b k) -> p b k", k=32)
            dve.tensor_reduce(wa, blk, AX.X, ALU.max, apply_absolute_value=True).then_inc(self.s_wb, 1)
            dve.wait_ge(self.s_wb, 3 * i + 1)
            dve.tensor_scalar(wa, wa, 1.0 / 7.0, 1e-12, ALU.mult, ALU.max).then_inc(self.s_wb, 1)
            dve.wait_ge(self.s_wb, 3 * i + 2)
            dve.reciprocal(wr, wa).then_inc(self.s_wb, 1)
            dve.wait_ge(self.s_wb, 3 * i + 3)
            dve.tensor_tensor(qb, blk, wr.unsqueeze(2).broadcast_to([P, self.NB, 32]), ALU.mult).then_inc(self.s_q, 1)

    def to_float(self, act):
        for i in range(3):
            act.wait_ge(self.s_q, i + 1)
            act.copy(self.raw[i][:], self.wq[:, i, :]).then_inc(self.s_f, 1)

    def dequantise(self, pool):
        for i in range(3):
            pool.wait_ge(self.s_f, i + 1)
            blk = self.raw[i][:].rearrange("p (b k) -> p b k", k=32)
            pool.tensor_tensor(blk, blk, self.wa[:, i, :].unsqueeze(2).broadcast_to([P, self.NB, 32]),
                               ALU.mult).then_inc(self.s_wd, 1)

    def transpose(self, pe):
        for n in range(9):
            pe.wait_ge(self.s_wd, n // 3 + 1)
            if n >= 4:
                pe.wait_ge(self.s_wl, n - 3)
            for j, src in enumerate(self.blocks(n)):
                last = pe.transpose(self.R[n % 4][:, j * P:(j + 1) * P], src, self.ident[:])
            last.then_inc(self.s_wT, 1)

    def high(self, act):
        for n in range(9):
            act.wait_ge(self.s_wT, n + 1)
            act.copy(self.part(n, True), self.bank(n)).then_inc(self.s_wh, 1)

    def remainder(self, dve):
        for n in range(9):
            dve.wait_ge(self.s_wh, n + 1)
            dve.tensor_tensor(self.part(n, False), self.bank(n), self.part(n, True).bitcast(F32),
                              ALU.subtract).then_inc(self.s_wl, 1)


def ffn(nc, sem, retired, sbuf, xs, c):
    NCH, CW = 8, 512
    TC = CW // P
    MF = FI // P
    NU, UW = 24, 1024
    UC = NU // NCH
    QM = 32767.0
    U16S = 65536.0

    def s(n):
        return sem("f_" + n)
    s_sc, s_loc, s_all = s("sc"), s("loc"), s("all")
    s_hb, s_hq, s_hf, s_hT, s_hh, s_hl, s_hi = s("hb"), s("hq"), s("hf"), s("hT"), s("hh"), s("hl"), s("hi")
    s_mm, s_ev, s_am = s("mm"), s("ev"), s("am")
    s_bh, s_bl, s_um, s_ue, s_ua, s_uw = s("bh"), s("bl"), s("um"), s("ue"), s("ua"), [s("uw0"), s("uw1")]
    s_gq, s_sg, s_su, s_g2, s_am2 = s("gq"), s("sg"), s("su"), s("g2"), s("am2")
    s_ul, s_uq, s_g3, s_pr, s_am3 = [s("ul0"), s("ul1")], s("uq"), s("g3"), s("pr"), s("am3")
    s_oq, s_oh, s_ol, s_dn, s_x2 = s("oq"), s("oh"), s("ol"), s("dn"), s("x2")

    uscr = nc.dram_tensor("up_scratch", (NU, P, UW), F32, kind="Internal").ap()
    with ExitStack() as st:
        G = sbuf(st, "G", [P, NU * UW])
        wTh, wTl, dTh, dTl = c["wTh"], c["wTl"], c["dTh"], c["dTl"]
        sc = sbuf(st, "sc", [P, 24])
        loc = sbuf(st, "loc", [P, 5])
        allm = sbuf(st, "allm", [P, 5])
        amt = sbuf(st, "amt", [P, NCH * MF])
        amu = sbuf(st, "amu", [P, NU])
        am2 = sbuf(st, "am2", [P, NU])
        am3 = sbuf(st, "am3", [P, NU])
        ps = [st.enter_context(nc.psum_tensor(f"f_ps{i}", [P, 512], F32)) for i in range(8)]
        T, R, Y = ps[0:2], ps[2:6], ps[4:8]
        (sh, ih, sup, kup, sga, kga, ssl, ksl, spr, kpr, tmp, sps) = [sc[:, i:i + 1] for i in range(12)]

        u0 = ExitStack()
        hiT = sbuf(u0, "f_hiT", [P, KT, NCH * CW], I16)
        u1 = ExitStack()
        hb = sbuf(u1, "f_hb", [P, TC, D])
        hq = sbuf(u1, "f_hq", [P, TC, D], I16)
        hh = [sbuf(u1, f"f_hh{i}", [P, KT, CW], F32R) for i in range(2)]
        hl = [sbuf(u1, f"f_hl{i}", [P, KT, CW], F32R) for i in range(2)]
        u1.close()
        ub_ = ExitStack()
        bh = sbuf(ub_, "f_bh", [P, KT, CW], F32R)
        bl = sbuf(ub_, "f_bl", [P, KT, CW], F32R)
        ub = [sbuf(ub_, f"f_ub{i}", [P, UW]) for i in range(2)]
        iq = [sbuf(ub_, f"f_iq{i}", [P, UW], I16) for i in range(2)]
        sg = sbuf(ub_, "f_sg", [P, UW])
        su = sbuf(ub_, "f_su", [P, UW], U16)
        ub_.close()
        u0.close()
        u2 = ExitStack()
        gq = [sbuf(u2, f"f_gq{i}", [P, UW], I16) for i in range(2)]
        ul = [sbuf(u2, f"f_ul{i}", [P, UW]) for i in range(2)]
        uq = [sbuf(u2, f"f_uq{i}", [P, UW], I16) for i in range(2)]
        u2.close()
        u3 = ExitStack()
        oh, ol = ([v[:].rearrange("p g k n -> p (g k n)").rearrange("p (u n) -> p u n", n=UW),
                   sbuf(u3, f"f_o{i}", [P, UC, UW], F32R)[:]] for i, v in enumerate((wTh, wTl)))
        oq = [sbuf(u3, f"f_oq{i}", [P, UW], I16) for i in range(2)]
        u3.close()

        def unit(n):
            return G[:, bass.ds(n * UW, UW)]

        def gate_tile(t, m):
            return G[:, bass.ds((t.n * MF + m) * CW, CW)]

        def products(pe, out_, g, m, xh, xl):
            n = 0
            for w_, h_ in ((wTh, xh), (wTl, xh), (wTh, xl)):
                for k in range(KT):
                    last = pe.matmul(out_, w_[:, g, k, m * P:(m + 1) * P], h_[:, k, :],
                                     start=(n == 0), stop=(n == 3 * KT - 1))
                    n += 1
            return last

        links = [0]

        def link(dve, instruction):
            instruction.then_inc(s_sc, 1)
            links[0] += 1
            dve.wait_ge(s_sc, links[0])

        def integer_scale(dve, k, unit_scale, extra, scale, factor):
            dve.wait_ge(s_all, k + 1)
            link(dve, dve.tensor_scalar(tmp, allm[:, k:k + 1], unit_scale, extra / QM, ALU.mult, ALU.mult))
            link(dve, dve.tensor_scalar(scale, tmp, 1e-12, None, ALU.max))
            link(dve, dve.reciprocal(tmp, scale))
            link(dve, dve.tensor_scalar(factor, tmp, unit_scale, extra, ALU.mult, ALU.mult))

        def reduce_all(pool, k):
            pool.wait_ge(s_loc, k + 1)
            pool.partition_all_reduce(allm[:, k:k + 1], loc[:, k:k + 1], P, RMAX).then_inc(s_all, 1)

        with nc.Block() as block:
            @block.sync
            def _(sp):
                retired.clear(sp)

            @block.vector
            def _(dve):
                dve.tensor_reduce(loc[:, 0:1], c["hamax"][:], AX.X, ALU.max).then_inc(s_loc, 1)
                integer_scale(dve, 0, 1.0, 1.0, sh, ih)

                def gate_max(t, ms):
                    for m in ms if 0 <= t.t0 < NCH else ():
                        dve.wait_ge(s_ev, t.of(lambda n: MF * n + m + 1))
                        dve.tensor_reduce(amt[:, bass.ds((t.n * MF + m), 1)], gate_tile(t, m), AX.X, ALU.max,
                                          apply_absolute_value=True).then_inc(s_am, 1)

                def body(t):
                    a = t + 1
                    if 0 <= a.t0 < NCH:
                        if a.t0 >= 2:
                            dve.wait_ge(s_mm, a.of(lambda n: MF * (n - 1)))
                        for k in range(KT):
                            dve.wait_ge(s_hi, a.of(lambda n: 2 * n + k + 1))
                            dve.tensor_tensor(hl[a.p][:, k, :], T[k][:], hh[a.p][:, k, :].bitcast(F32),
                                              ALU.subtract).then_inc(s_hl, 1)
                    gate_max(t, range(0, 2))
                    a = t + 2
                    if 0 <= a.t0 < NCH:
                        if a.t0 >= 1:
                            dve.wait_ge(s_hT, a.of(lambda n: n))
                        for j in range(TC):
                            n = a.n * TC + j
                            last = dve.tensor_scalar(hb[:, j, :], xs[:, bass.ds(n * D, D)],
                                                     c["hmean"][:, bass.ds(n, 1)],
                                                     c["hrstd"][:, bass.ds(n, 1)], ALU.subtract, ALU.mult)
                        last.then_inc(s_hb, 1)
                        dve.wait_ge(s_hb, a.of(lambda n: n + 1))
                        dve.tensor_scalar(hq[:], hb[:], ih, None, ALU.mult).then_inc(s_hq, 1)
                    gate_max(t, range(2, MF))
                pipeline(dve, body, -2, NCH - 1, 2, 5)
                dve.wait_ge(s_am, NCH * MF)
                dve.tensor_reduce(loc[:, 1:2], amt[:], AX.X, ALU.max).then_inc(s_loc, 1)
                integer_scale(dve, 1, sh, 1.0, sga, kga)

            @block.gpsimd
            def _(pool):
                reduce_all(pool, 0)
                reduce_all(pool, 1)

            @block.tensor
            def _(pe):
                def body(t):
                    a = t + 1
                    if 0 <= a.t0 < NCH:
                        pe.wait_ge(s_hf, a.of(lambda n: n + 1))
                        if a.t0 >= 1:
                            pe.wait_ge(s_hl, a.of(lambda n: 2 * n))
                            pe.wait_ge(s_hi, a.of(lambda n: 2 * n))
                        for k in range(KT):
                            for j in range(TC):
                                last = pe.transpose(T[k][:, j * P:(j + 1) * P], hb[:, j, k * P:(k + 1) * P],
                                                    c["ident"][:])
                        last.then_inc(s_hT, 1)
                    if 0 <= t.t0 < NCH:
                        pe.wait_ge(s_hh, t.of(lambda n: 2 * n + 2))
                        pe.wait_ge(s_hl, t.of(lambda n: 2 * n + 2))
                        for m in range(MF):
                            b = (m + 2 * t.t0) % 4
                            if m >= 4 or t.t0 >= 1:
                                pe.wait_ge(s_ev, t.of(lambda n: MF * n + m - 3))
                            products(pe, R[b][:], 1, m, hh[t.p], hl[t.p]).then_inc(s_mm, 1)
                pipeline(pe, body, -1, NCH - 1, 2, 5)

            @block.scalar
            def _(act):
                def gate_out(t, ms):
                    for m in ms if 0 <= t.t0 < NCH else ():
                        act.wait_ge(s_mm, t.of(lambda n: MF * n + m + 1))
                        act.copy(gate_tile(t, m), R[(m + 2 * t.t0) % 4][:]).then_inc(s_ev, 1)

                def body(t):
                    a = t + 1
                    if 0 <= a.t0 < NCH:
                        act.wait_ge(s_hT, a.of(lambda n: n + 1))
                        if a.t0 >= 2:
                            act.wait_ge(s_mm, a.of(lambda n: MF * (n - 1)))
                        for k in range(KT):
                            act.copy(hh[a.p][:, k, :], T[k][:]).then_inc(s_hh, 1)
                            act.copy(hiT[:, k, bass.ds(a.n * CW, CW)], T[k][:]).then_inc(s_hi, 1)
                    gate_out(t, range(0, 4))
                    a = t + 2
                    if 0 <= a.t0 < NCH:
                        act.wait_ge(s_hq, a.of(lambda n: n + 1))
                        act.copy(hb[:], hq[:]).then_inc(s_hf, 1)
                    gate_out(t, range(4, MF))
                pipeline(act, body, -2, NCH - 1, 2, 5)
        retired.stack.close()

        with nc.Block() as block:
            @block.tensor
            def _(pe):
                def body(t):
                    pe.wait_ge(s_bh, t.of(lambda n: n + 1))
                    pe.wait_ge(s_bl, t.of(lambda n: n + 1))
                    for m in range(MF):
                        b = (m + 2 * t.t0) % 4
                        if m >= 4 or t.t0 >= 1:
                            pe.wait_ge(s_ue, t.of(lambda n: MF * n + m - 3))
                        products(pe, R[b][:], 0, m, bh, bl).then_inc(s_um, 1)
                pipeline(pe, body, 0, NCH - 1, 2, 5)

            @block.scalar
            def _(act):
                def high(t):
                    if t.t0 >= 1:
                        act.wait_ge(s_um, t.of(lambda n: MF * n))
                    act.copy(bh[:], hiT[:, :, bass.ds(t.n * CW, CW)]).then_inc(s_bh, 1)

                def body(t):
                    if t.t0 == 0:
                        high(t)
                    for q in range(UC):
                        first, par = t.t0 * UC + q, (t.t0 + q) % 2
                        if first >= 2:
                            act.wait_ge(s_g2, t.of(lambda n: UC * n + q - 1))
                        act.activation(iq[par][:], unit(t.n * UC + q), ACT.Copy, scale=kga).then_inc(s_gq, 1)
                        act.wait_ge(s_gq, t.of(lambda n: UC * n + q + 1))
                        if first >= 1:
                            act.wait_ge(s_su, t.of(lambda n: UC * n + q))
                        act.activation(sg[:], iq[par][:], ACT.Sigmoid, scale=sga).then_inc(s_sg, 1)
                        if first >= 2:
                            act.wait_ge(s_uw[par], t.of(lambda n: 16 * ((UC * n + q) // 2)))
                            act.wait_ge(s_ua, t.of(lambda n: UC * n + q - 1))
                        for m in (2 * q, 2 * q + 1):
                            act.wait_ge(s_um, t.of(lambda n: MF * n + m + 1))
                            act.copy(ub[par][:, (m % 2) * CW:(m % 2 + 1) * CW],
                                     R[(m + 2 * t.t0) % 4][:]).then_inc(s_ue, 1)
                        if q == 1 and t.t0 + 1 < NCH:
                            high(t + 1)
                pipeline(act, body, 0, NCH - 1, 2, 5)

            @block.sync
            def _(sp):
                def store(t):
                    sp.wait_ge(s_ue, t.of(lambda n: 2 * n + 2))
                    sp.dma_start(uscr[bass.ds(t.n, 1)].rearrange("u p n -> p (u n)"),
                                 ub[t.p][:]).then_inc(s_uw[t.p], 16)
                pipeline(sp, store, 0, NU - 1, 2, NU - 1)
                for i in range(2):
                    sp.wait_ge(s_uw[i], 16 * NU // 2)

            @block.gpsimd
            def _(pool):
                reduce_all(pool, 2)
                reduce_all(pool, 3)

            @block.vector
            def _(dve):
                def silu_max(t, q):
                    dve.wait_ge(s_g2, t.of(lambda n: UC * n + q + 1))
                    dve.tensor_reduce(am2[:, bass.ds(t.n * UC + q, 1)], unit(t.n * UC + q), AX.X, ALU.max,
                                      apply_absolute_value=True).then_inc(s_am2, 1)

                def remainder(t):
                    dve.wait_ge(s_bh, t.of(lambda n: n + 1))
                    if t.t0 >= 1:
                        dve.wait_ge(s_um, t.of(lambda n: MF * n))
                    dve.tensor_tensor(bl[:], hiT[:, :, bass.ds(t.n * CW, CW)], bh[:].bitcast(F32),
                                      ALU.subtract).then_inc(s_bl, 1)

                def body(t):
                    if t.t0 == 0:
                        remainder(t)
                    for q in range(UC):
                        par = (t.t0 + q) % 2
                        dve.wait_ge(s_sg, t.of(lambda n: UC * n + q + 1))
                        if t.t0 * UC + q >= 1:
                            dve.wait_ge(s_g2, t.of(lambda n: UC * n + q))
                        dve.tensor_scalar(su[:], sg[:], U16S, U16S - 1, ALU.mult, ALU.min).then_inc(s_su, 1)
                        if t.t0 * UC + q >= 1:
                            silu_max(t, q - 1)
                        dve.wait_ge(s_su, t.of(lambda n: UC * n + q + 1))
                        dve.scalar_tensor_tensor(unit(t.n * UC + q), iq[par][:], sga, su[:], ALU.mult,
                                                 ALU.mult).then_inc(s_g2, 1)
                        dve.wait_ge(s_ue, t.of(lambda n: MF * n + 2 * q + 2))
                        dve.tensor_reduce(amu[:, bass.ds(t.n * UC + q, 1)], ub[par][:], AX.X, ALU.max,
                                          apply_absolute_value=True).then_inc(s_ua, 1)
                        if q == 1 and t.t0 + 1 < NCH:
                            remainder(t + 1)
                pipeline(dve, body, 0, NCH - 1, 2, 5)
                silu_max(At(NCH - 1), UC - 1)
                dve.wait_ge(s_ua, NU)
                dve.tensor_reduce(loc[:, 2:3], amu[:], AX.X, ALU.max).then_inc(s_loc, 1)
                dve.wait_ge(s_am2, NU)
                dve.tensor_reduce(loc[:, 3:4], am2[:], AX.X, ALU.max).then_inc(s_loc, 1)
                integer_scale(dve, 2, sh, 1.0, sup, kup)
                integer_scale(dve, 3, 1.0, 1.0 / U16S, ssl, ksl)

        with nc.Block() as block:
            @block.scalar
            def _(act):
                def ints(t):
                    if t.t0 >= 2:
                        act.wait_ge(s_pr, t.of(lambda n: n - 1))
                    act.activation(gq[t.p][:], unit(t.n), ACT.Copy, scale=ksl).then_inc(s_g3, 1)
                    act.wait_ge(s_ul[t.p], t.of(lambda n: 16 * (n // 2 + 1)))
                    act.activation(uq[t.p][:], ul[t.p][:], ACT.Copy, scale=kup).then_inc(s_uq, 1)
                pipeline(act, ints, 0, NU - 1, 2, NU - 1)

            @block.sync
            def _(sp):
                def load(t):
                    if t.t0 >= 2:
                        sp.wait_ge(s_uq, t.of(lambda n: n - 1))
                    sp.dma_start(ul[t.p][:], uscr[bass.ds(t.n, 1)].rearrange("u p n -> p (u n)")
                                 ).then_inc(s_ul[t.p], 16)
                pipeline(sp, load, 0, NU - 1, 2, NU - 1)

            @block.gpsimd
            def _(pool):
                reduce_all(pool, 4)

            @block.vector
            def _(dve):
                def body(t):
                    if t.t0 < NU:
                        dve.wait_ge(s_g3, t.of(lambda n: n + 1))
                        dve.wait_ge(s_uq, t.of(lambda n: n + 1))
                        dve.tensor_tensor(unit(t.n), gq[t.p][:], uq[t.p][:], ALU.mult).then_inc(s_pr, 1)
                    a = t + -1
                    if a.t0 >= 0:
                        dve.wait_ge(s_pr, a.of(lambda n: n + 1))
                        dve.tensor_reduce(am3[:, bass.ds(a.n, 1)], unit(a.n), AX.X, ALU.max,
                                          apply_absolute_value=True).then_inc(s_am3, 1)
                pipeline(dve, body, 0, NU, 2, NU - 1)
                dve.wait_ge(s_am3, NU)
                dve.tensor_reduce(loc[:, 4:5], am3[:], AX.X, ALU.max).then_inc(s_loc, 1)
                link(dve, dve.tensor_tensor(sps, ssl, sup, ALU.mult))
                integer_scale(dve, 4, sps, 1.0, spr, kpr)

        with nc.Block() as block:
            @block.vector
            def _(dve):
                def body(t):
                    a = t + 1
                    for k in range(TC):
                        if k < UC and 0 <= a.t0 < NCH:
                            dve.wait_ge(s_oq, a.of(lambda n: UC * n + k + 1))
                            dve.wait_ge(s_oh, a.of(lambda n: UC * n + k + 1))
                            if a.t0 >= 2 and k == 0:
                                dve.wait_ge(s_dn, a.of(lambda n: TC * (n - 1)))
                            dve.tensor_tensor(ol[a.p][:, k, :], oq[(k + a.t0) % 2][:], oh[a.p][:, k, :].bitcast(F32),
                                              ALU.subtract).then_inc(s_ol, 1)
                        if 0 <= t.t0 < NCH:
                            dve.wait_ge(s_dn, t.of(lambda n: TC * n + k + 1))
                            xv = xs[:, bass.ds((t.n * TC + k) * D, D)]
                            dve.scalar_tensor_tensor(xv, Y[k][:, 0:D], spr, xv, ALU.mult,
                                                     ALU.add).then_inc(s_x2, 1)
                pipeline(dve, body, -1, NCH - 1, 2, 5)

            @block.scalar
            def _(act):
                def body(t):
                    for k in range(UC):
                        if t.t0 * UC + k >= 2:
                            act.wait_ge(s_ol, t.of(lambda n: UC * n + k - 1))
                        q = oq[(k + t.t0) % 2]
                        act.activation(q[:], unit(t.n * UC + k), ACT.Copy, scale=kpr).then_inc(s_oq, 1)
                        act.wait_ge(s_oq, t.of(lambda n: UC * n + k + 1))
                        if t.t0 >= 2 and k == 0:
                            act.wait_ge(s_dn, t.of(lambda n: TC * (n - 1)))
                        act.copy(oh[t.p][:, k, :], q[:]).then_inc(s_oh, 1)
                pipeline(act, body, 0, NCH - 1, 2, 5)

            @block.tensor
            def _(pe):
                def body(t):
                    for j in range(TC):
                        if t.t0 >= 1:
                            pe.wait_ge(s_x2, t.of(lambda n: TC * (n - 1) + j + 1))
                        if j == 0:
                            pe.wait_ge(s_oh, t.of(lambda n: UC * (n + 1)))
                            pe.wait_ge(s_ol, t.of(lambda n: UC * (n + 1)))
                        n = 0
                        for o_, w_ in ((oh, dTh), (ol, dTh), (oh, dTl)):
                            for k in range(MF):
                                lhs = o_[t.p][:, k // 2, (k % 2) * CW + j * P:(k % 2) * CW + (j + 1) * P]
                                last = pe.matmul(Y[j][:, 0:D], lhs, w_[:, k, :], start=(n == 0),
                                                 stop=(n == 3 * MF - 1))
                                n += 1
                        last.then_inc(s_dn, 1)
                pipeline(pe, body, 0, NCH - 1, 2, 5)


def moe(nc, stack, sem, sbuf, xs, xt, col, c, out):
    def s(name):
        return sem("m_" + name)
    NB = NE // 2
    EW = NE * D
    NA = 5
    s_w, s_wT, s_wh, s_wl, s_c = [s(f"w{i}") for i in range(3)], s("wT"), s("wh"), s("wl"), s("c")
    s_stat, s_aggr, s_veps, s_rstd, s_xn = s("stat"), s("aggr"), s("veps"), s("rstd"), s("xn")
    s_xT, s_xh, s_xl, s_lg, s_E = s("xT"), s("xh"), s("xl"), s("lg"), s("E")
    s_l, s_top, s_idx, s_fi, s_sel, s_sh, s_ex = s("l"), s("top"), s("idx"), s("fi"), s("sel"), s("sh"), s("ex")
    s_r, s_g, s_gT, s_gTe, s_bias, s_acc = s("r"), s("g"), s("gT"), s("gTe"), s("bias"), s("acc")
    s_out, s_m1, s_sc, s_h1, s_half, s_done = s("out"), s("m1"), s("sc"), s("h1"), s("half"), s("done")

    with ExitStack() as st:
        wh = sbuf(st, "m_wh", [P, KT, EW + NE], F32R)
        wl = sbuf(st, "m_wl", [P, KT, EW + NE], F32R)
        be = sbuf(st, "m_be", [NE, D])
        bg = sbuf(st, "m_bg", [P, NE])
        iota = sbuf(st, "m_iota", [P, NE])
        ps = [st.enter_context(nc.psum_tensor(f"m_ps{i}", [P, 512], F32)) for i in range(8)]
        X, T, GL, GT, BO = ps[0:4], ps[4], ps[5], ps[6], ps[7]
        raw = sbuf(st, "m_raw", [P, NE, 2, D])
        rg = sbuf(st, "m_rg", [NE, D])
        stats = sbuf(st, "m_stats", [P, 2, 6])
        ag = sbuf(st, "m_ag", [P, 2, 2])
        ve = sbuf(st, "m_ve", [P, 2])
        rstd = sbuf(st, "m_rstd", [P, 2])
        xn = [sbuf(st, f"m_xn{i}", [P, D]) for i in range(2)]
        xh = [sbuf(st, f"m_xh{i}", [P, KT, P], F32R) for i in range(2)]
        xl = [sbuf(st, f"m_xl{i}", [P, KT, P], F32R) for i in range(2)]
        lg = [sbuf(st, f"m_lg{i}", [P, NE]) for i in range(2)]
        ls = [sbuf(st, f"m_ls{i}", [P, NE]) for i in range(2)]
        ex = [sbuf(st, f"m_ex{i}", [P, NE]) for i in range(2)]
        m1 = [sbuf(st, f"m_max{i}", [P, 1]) for i in range(2)]
        top = [sbuf(st, f"m_top{i}", [P, NE]) for i in range(2)]
        idx = [sbuf(st, f"m_idx{i}", [P, NE], U16) for i in range(2)]
        fi = [sbuf(st, f"m_fi{i}", [P, 2]) for i in range(2)]
        sel = [sbuf(st, f"m_sel{i}", [P, 2, NE]) for i in range(2)]
        es = [sbuf(st, f"m_es{i}", [P, 1]) for i in range(2)]
        rs = [sbuf(st, f"m_rs{i}", [P, 1]) for i in range(2)]
        g = [sbuf(st, f"m_g{i}", [P, NE]) for i in range(2)]
        gT = [sbuf(st, f"m_gT{i}", [NE, P]) for i in range(2)]
        half = [sbuf(st, f"m_half{i}", [P, 4, D]) for i in range(2)]
        FIRST, LAST, LO, HI = -4, NT, 4, 27

        def bank(n):
            return ps[n % 4][:].rearrange("p (k o) -> p k o", k=KT)[:, :, 0:D if n < NE else NE]

        def part(w_, n):
            return w_[:, :, n * D:(n + 1) * D] if n < NE else w_[:, :, EW:EW + NE]

        def product(pe, a, o_, cols):
            n = 0
            for x_, w_ in ((xh, wh), (xl, wh), (xh, wl)):
                for k in range(KT):
                    last = pe.matmul(o_, x_[a.p][:, k, :], w_[:, k, cols], start=(n == 0), stop=(n == 3 * KT - 1))
                    n += 1
            return last

        with nc.Block() as block:
            @block.tensor
            def _(pe):
                for n in range(NE + 1):
                    if n % 4 == 0:
                        pe.wait_ge(s_w[n // 4], 16)
                    if n >= 4:
                        pe.wait_ge(s_wl, n - 3)
                    for k in range(KT):
                        if n < NE:
                            for m in range(2):
                                last = pe.transpose(ps[n % 4][:, k * D + m * P:k * D + (m + 1) * P],
                                                    raw[:, n, m, k * P:(k + 1) * P], c["ident"][:])
                        else:
                            last = pe.transpose(ps[n % 4][:, k * D:k * D + NE], rg[:, k * P:(k + 1) * P],
                                                c["ident"][0:NE, 0:NE])
                    last.then_inc(s_wT, 1)

                def experts(t, q):
                    if t.t0 >= 1 and q < 2:
                        pe.wait_ge(s_acc, t.of(lambda n: NA * (n - 1) + 2 * q + 2))
                    elif t.t0 >= 1:
                        pe.wait_ge(s_sc, t.of(lambda n: 4 * (n - 1) + 2 * q - 2))
                    product(pe, t, X[q][:], slice(q * 2 * D, (q + 1) * 2 * D)).then_inc(s_E, 1)

                def body(t):
                    if t.t0 == 0:
                        pe.wait_ge(s_c, 32 + NE)
                    if t.ok():
                        experts(t, 0)
                    a = t + 1
                    if a.ok():
                        if a.t0 == 0:
                            pe.wait_ge(s_wl, NE + 1)
                        pe.wait_ge(s_xl, a.of(lambda n: n + 1))
                        if a.t0 >= 1:
                            pe.wait_ge(s_l, a.of(lambda n: n))
                        product(pe, a, GL[:, 0:NE], slice(EW, EW + NE)).then_inc(s_lg, 1)
                    if t.ok():
                        experts(t, 1)
                        pe.wait_ge(s_g, t.of(lambda n: n + 1))
                        if t.t0 >= 1:
                            pe.wait_ge(s_gTe, t.of(lambda n: n))
                        pe.transpose(GT[0:NE, 0:P], g[t.p][:], c["ident"][:]).then_inc(s_gT, 1)
                    a = t + 2
                    if a.ok():
                        pe.wait_ge(s_xn, a.of(lambda n: n + 1))
                        if a.t0 >= 1:
                            pe.wait_ge(s_xl, a.of(lambda n: n))
                        for k in range(KT):
                            last = pe.transpose(T[:, k * P:(k + 1) * P], xn[a.p][:, k * P:(k + 1) * P], c["ident"][:])
                        last.then_inc(s_xT, 1)
                    if t.ok():
                        experts(t, 2)
                        experts(t, 3)
                        pe.wait_ge(s_gTe, t.of(lambda n: n + 1))
                        if t.t0 >= 1:
                            pe.wait_ge(s_acc, t.of(lambda n: NA * n))
                        pe.matmul(BO[:, 0:D], gT[t.p][:], be[:], start=True, stop=True).then_inc(s_bias, 1)
                pipeline(pe, body, FIRST, LAST, LO, HI)

            @block.scalar
            def _(act):
                for n in range(NE + 1):
                    act.wait_ge(s_wT, n + 1)
                    act.copy(part(wh, n), bank(n)).then_inc(s_wh, 1)

                def weigh(t, e):
                    act.wait_ge(s_E, t.of(lambda n: NB * n + 3 + e // 2))
                    act.activation(half[t.p][:, e, :], X[2 + e // 2][:, (e % 2) * D:(e % 2 + 1) * D], ACT.Copy,
                                   scale=g[t.p][:, 4 + e:5 + e]).then_inc(s_sc, 1)

                def body(t):
                    a = t + 1
                    if a.ok():
                        act.wait_ge(s_sh, a.of(lambda n: n + 1))
                        act.activation(ex[a.p][:], ls[a.p][:], ACT.Exp, accum_out=es[a.p][:]).then_inc(s_ex, 1)
                    if t.ok():
                        act.wait_ge(s_gT, t.of(lambda n: n + 1))
                        if t.t0 >= 2:
                            act.wait_ge(s_bias, t.of(lambda n: n - 1))
                        act.copy(gT[t.p][:], GT[0:NE, 0:P]).then_inc(s_gTe, 1)
                        if t.t0 >= 2:
                            act.wait_ge(s_done, t.of(lambda n: n - 1))
                        weigh(t, 0)
                        weigh(t, 1)
                    a = t + 2
                    if a.ok():
                        act.wait_ge(s_xT, a.of(lambda n: n + 1))
                        if a.t0 >= 2:
                            act.wait_ge(s_E, a.of(lambda n: NB * (n - 1)))
                        act.copy(xh[a.p][:].rearrange("p k n -> p (k n)"), T[:, 0:D]).then_inc(s_xh, 1)
                    if t.ok():
                        weigh(t, 2)
                        weigh(t, 3)
                pipeline(act, body, FIRST, LAST, LO, HI)

            @block.gpsimd
            def _(pool):
                for e in range(NE):
                    pool.memset(iota[:, e:e + 1], float(e)).then_inc(s_c, 1)

                def body(t):
                    if t.ok():
                        pool.wait_ge(s_sc, t.of(lambda n: 4 * n + 4))
                        pool.tensor_tensor(half[t.p][:, 0:2, :], half[t.p][:, 0:2, :], half[t.p][:, 2:4, :],
                                           ALU.add).then_inc(s_h1, 1)
                        pool.wait_ge(s_h1, t.of(lambda n: n + 1))
                        pool.tensor_tensor(half[t.p][:, 0, :], half[t.p][:, 0, :], half[t.p][:, 1, :],
                                           ALU.add).then_inc(s_half, 1)
                    a = t + 4
                    if a.ok():
                        pool.wait_ge(s_veps, a.of(lambda n: n + 1))
                        pool.tensor_tensor(rstd[:, a.p:a.p + 1], ve[:, a.p:a.p + 1], c["mhalf"][:],
                                           ALU.pow).then_inc(s_rstd, 1)
                pipeline(pool, body, FIRST, LAST, LO, HI)

            @block.sync
            def _(sp):
                for h in range(2):
                    sp.dma_start(raw[:, 4 * h:4 * h + 4].rearrange("p e m d -> p (e m) d"),
                                 c["L1_ffn_W"][4 * h:4 * h + 4].rearrange("e (m p) d -> p (e m) d", p=P)
                                 ).then_inc(s_w[h], 16)
                sp.dma_start(rg[:], c["L1_ffn_Wg"]).then_inc(s_w[2], 16)
                sp.dma_start(be[:], c["L1_ffn_b"]).then_inc(s_c, 16)
                sp.dma_start(bg[:], c["L1_ffn_bg"].partition_broadcast(P)).then_inc(s_c, 16)
                TO = TPB // 4
                with sp.Fori(0, NT // TO) as b:
                    sp.wait_ge(s_done, b * TO + TO)
                    sp.dma_start(out.rearrange("b (h t p) d -> (b h) p t d", p=P, t=TO)[bass.ds(b, 1)]
                                 .rearrange("b p t d -> p (b t) d"),
                                 xs[:, bass.ds(b * (TO * D), TO * D)].rearrange("p (t d) -> p t d", d=D)
                                 ).then_inc(s_out, 16)
                sp.wait_ge(s_out, 16 * (NT // TO))

            @block.vector
            def _(dve):
                for n in range(NE + 1):
                    dve.wait_ge(s_wh, n + 1)
                    dve.tensor_tensor(part(wl, n), bank(n), part(wh, n).bitcast(F32), ALU.subtract).then_inc(s_wl, 1)
                dve.wait_ge(s_c, 32 + NE)

                def body(t):
                    def add(e):
                        if not t.ok():
                            return
                        dve.wait_ge(s_E, t.of(lambda n: NB * n + e // 2 + 1))
                        dve.wait_ge(s_acc, t.of(lambda n: NA * n + e))
                        dve.scalar_tensor_tensor(xt(t), X[e // 2][:, (e % 2) * D:(e % 2 + 1) * D],
                                                 g[t.p][:, e:e + 1], xt(t), ALU.mult, ALU.add).then_inc(s_acc, 1)
                    a = t + 1
                    p = a.p
                    add(0)
                    if a.ok():
                        one = a.of(lambda n: n + 1)
                        dve.wait_ge(s_lg, one)
                        dve.tensor_tensor(lg[p][:], GL[:, 0:NE], bg[:], ALU.add).then_inc(s_l, 1)
                    add(1)
                    if a.ok():
                        dve.wait_ge(s_l, one)
                        dve.tensor_reduce(m1[p][:], lg[p][:], AX.X, ALU.max).then_inc(s_m1, 1)
                        dve.max(top[p][:], lg[p][:]).then_inc(s_top, 1)
                    add(2)
                    if a.ok():
                        dve.wait_ge(s_m1, one)
                        dve.wait_ge(s_top, one)
                        dve.tensor_scalar(ls[p][:], lg[p][:], m1[p][:, 0:1], None, ALU.subtract).then_inc(s_sh, 1)
                        dve.max_index(idx[p][:], top[p][:], lg[p][:]).then_inc(s_idx, 1)
                    add(3)
                    if a.ok():
                        dve.wait_ge(s_idx, one)
                        dve.tensor_copy(fi[p][:], idx[p][:, 0:2]).then_inc(s_fi, 1)
                    b = t + -1
                    if b.ok():
                        dve.wait_ge(s_acc, b.of(lambda n: NA * (n + 1)))
                        dve.wait_ge(s_half, b.of(lambda n: n + 1))
                        dve.tensor_tensor(xt(b), half[b.p][:, 0, :], xt(b), ALU.add).then_inc(s_done, 1)
                    if a.ok():
                        dve.wait_ge(s_fi, one)
                        dve.tensor_scalar(sel[p][:, 0, :], iota[:], fi[p][:, 0:1], None, ALU.is_equal).then_inc(s_sel, 1)
                        dve.wait_ge(s_ex, one)
                        dve.reciprocal(rs[p][:], es[p][:]).then_inc(s_r, 1)
                        dve.wait_ge(s_sel, a.of(lambda n: 2 * n + 1))
                        dve.scalar_tensor_tensor(sel[p][:, 1, :], iota[:], fi[p][:, 1:2], sel[p][:, 0, :],
                                                 ALU.is_equal, ALU.add).then_inc(s_sel, 1)
                        dve.wait_ge(s_r, one)
                        dve.wait_ge(s_sel, a.of(lambda n: 2 * n + 2))
                        if a.t0 >= 2:
                            dve.wait_ge(s_gT, a.of(lambda n: n - 1))
                            dve.wait_ge(s_sc, a.of(lambda n: 4 * (n - 1)))
                        dve.scalar_tensor_tensor(g[p][:], ex[p][:], rs[p][:, 0:1], sel[p][:, 1, :], ALU.mult,
                                                 ALU.mult).then_inc(s_g, 1)
                    b = t + 2
                    if b.ok():
                        dve.wait_ge(s_xh, b.of(lambda n: n + 1))
                        if b.t0 >= 2:
                            dve.wait_ge(s_E, b.of(lambda n: NB * (n - 1)))
                        dve.tensor_tensor(xl[b.p][:].rearrange("p k n -> p (k n)"), T[:, 0:D],
                                          xh[b.p][:].rearrange("p k n -> p (k n)").bitcast(F32),
                                          ALU.subtract).then_inc(s_xl, 1)
                    if t.ok():
                        dve.wait_ge(s_bias, t.of(lambda n: n + 1))
                        dve.wait_ge(s_acc, t.of(lambda n: NA * n + 4))
                        dve.tensor_tensor(xt(t), BO[:, 0:D], xt(t), ALU.add).then_inc(s_acc, 1)
                    a, b = t + 4, t + 3
                    if a.ok():
                        dve.bn_stats(stats[:, a.p, :], xt(a)).then_inc(s_stat, 1)
                        dve.wait_ge(s_stat, a.of(lambda n: n + 1))
                    if b.ok():
                        dve.wait_ge(s_rstd, b.of(lambda n: n + 1))
                        if b.t0 >= 2:
                            dve.wait_ge(s_xT, b.of(lambda n: n - 1))
                        dve.tensor_scalar(xn[b.p][:], xt(b), ag[:, b.p, 0:1], rstd[:, b.p:b.p + 1],
                                          ALU.subtract, ALU.mult).then_inc(s_xn, 1)
                    if a.ok():
                        dve.bn_aggr(ag[:, a.p, :], stats[:, a.p, :]).then_inc(s_aggr, 1)
                        dve.wait_ge(s_aggr, a.of(lambda n: n + 1))
                        dve.tensor_scalar(ve[:, a.p:a.p + 1], ag[:, a.p, 1:2], EPS, None, ALU.add).then_inc(s_veps, 1)
                pipeline(dve, body, FIRST, LAST, LO, HI)



_INS = ["x", "ctx_768", "mask_BxS2_bf1", "L0_xattn_Wq", "L0_xattn_bq", "L0_xattn_Wk", "L0_xattn_bk",
        "L0_xattn_Wv", "L0_xattn_bv", "L0_xattn_Wo", "L0_xattn_bo", "L0_ffn_w_gate", "L0_ffn_w_up",
        "L0_ffn_w_down", "L1_xattn_g_norm", "L1_xattn_null_kv", "L1_xattn_Wq", "L1_xattn_Wkv",
        "L1_xattn_Wout", "L1_xattn_g_out", "L1_ffn_W", "L1_ffn_b", "L1_ffn_Wg", "L1_ffn_bg"]


def kernel(**inputs):
    import numpy as np
    import concourse.bacc as bacc
    from concourse.bass_utils import run_bass_kernel_spmd

    nc = bacc.Bacc("TRN2", target_bir_lowering=False, num_devices=1)
    arrays, aps = {}, {}
    for name in _INS:
        a = np.ascontiguousarray(inputs[name])
        if a.dtype == np.bool_:
            a = a.view(np.uint8)
        arrays[f"in_{name}"] = a
        aps[name] = nc.dram_tensor(f"in_{name}", a.shape, mybir.dt.from_np(a.dtype), kind="ExternalInput").ap()
    out = nc.dram_tensor("out", (B, SEQ, D), F32, kind="ExternalOutput").ap()
    w = {n.replace("L0_xattn_", ""): aps[n] for n in _INS if n.startswith("L0_xattn_")}
    w.update({n: aps[n] for n in _INS})
    program(nc, aps["x"], aps["ctx_768"], aps["mask_BxS2_bf1"], w, out)
    r = run_bass_kernel_spmd(nc, [arrays], core_ids=[0])
    return r.results[0]["out"]
```
